# Optimizing a Trainium2 kernel written in Bass

```python
import numpy as np
import jax
import jax.numpy as jnp

def _softmax(x, axis=-1):
    return jax.nn.softmax(x, axis=axis)

def _gelu(x):
    return jax.nn.gelu(x, approximate=True)

def _silu(x):
    return jax.nn.silu(x)

def _sigmoid(x):
    return jax.nn.sigmoid(x)

def _layernorm(x, axis=-1, eps=1e-05):
    m = jnp.mean(x, axis=axis, keepdims=True)
    v = jnp.var(x, axis=axis, keepdims=True)
    return (x - m) / jnp.sqrt(v + eps)

def _scatter_add(tgt, idx, src, axis=0):
    return tgt.at[idx].add(src)

def _segment_sum(src, seg, n):
    return jax.ops.segment_sum(src, seg, n)
kernel_name = 'mk_adj_ffn_d1_adj_r2_c8792b'

def setup_inputs(seed: int=0):
    np.random.seed(seed)
    _w = jnp.asarray

    def _rec_inputs():
        import jax
        import jax.numpy as jnp
        _gk = jax.random.key(seed)
        x = -0.000929 + 1 * jax.random.normal(jax.random.fold_in(_gk, 1), (3327, 256), jnp.float32)
        _a = jax.random.bernoulli(jax.random.fold_in(_gk, 2), 0.00480914, (3327, 3327))
        _a = jnp.logical_or(_a, jnp.swapaxes(_a, -1, -2))
        _a = jnp.logical_or(_a, jnp.eye(3327, dtype=bool))
        adj = _a.astype(jnp.int32)
        return (x, adj)
    x, adj = _rec_inputs()

    def _L0_gnn_setup():
        import jax, jax.numpy as jnp
        import numpy as np
        B, IN_F, OUT_F, H = (1024, 256, 256, 8)
        D = OUT_F // H
        key = jax.random.key(seed)
        ks = jax.random.split(key, 4)
        x = jax.random.normal(ks[0], (B, IN_F), dtype=jnp.float32)
        W_w = jax.random.normal(ks[1], (OUT_F, IN_F), dtype=jnp.float32) * (1.0 / np.sqrt(IN_F))
        W_b = jnp.zeros((OUT_F,), dtype=jnp.float32)
        a = jax.random.normal(ks[2], (2 * D, 1), dtype=jnp.float32) * 0.1
        adj = jax.random.randint(ks[3], (B, B), 0, 2, dtype=jnp.int32)
        return {'x': x, 'adj': adj, 'W_w': W_w, 'W_b': W_b, 'a': a}
    _L0_gnn_all = _L0_gnn_setup()
    _L0_gnn_in = {k: v for k, v in _L0_gnn_all.items() if k in ('W_w', 'W_b', 'a')}
    del _L0_gnn_all

    def _L0_ffn_setup():
        import jax, jax.numpy as jnp
        import numpy as np
        B, S, D, O = (1, 1024, 256, 256)
        H, QD, K, PK = (8, 128, 16, 128)
        N = PK * PK
        HALF = QD // 2

        def _l2norm(x):
            n = jnp.sqrt(jnp.sum(x * x, axis=-1, keepdims=True))
            return x / jnp.maximum(n, 1e-12)
        key = jax.random.key(seed)
        ks = jax.random.split(key, 9)
        return {'hidden_states': jax.random.normal(ks[0], (B, S, D), jnp.float32), 'Wq': jax.random.normal(ks[1], (H * QD, D), jnp.float32) * 0.02, 'bq': jnp.zeros((H * QD,), jnp.float32), 'ln_g': jnp.ones((QD,), jnp.float32), 'ln_b': jnp.zeros((QD,), jnp.float32), 'keys0': jax.random.normal(ks[2], (PK, HALF), jnp.float32) * 0.02, 'keys1': jax.random.normal(ks[3], (PK, HALF), jnp.float32) * 0.02, 'expert_down': jax.random.normal(ks[4], (N, D), jnp.float32) * 0.02, 'expert_up': jax.random.normal(ks[5], (N, O), jnp.float32) * 0.02}
    _L0_ffn_all = _L0_ffn_setup()
    _L0_ffn_in = {k: v for k, v in _L0_ffn_all.items() if k in ('Wq', 'bq', 'ln_g', 'ln_b', 'keys0', 'keys1', 'expert_down', 'expert_up')}
    del _L0_ffn_all
    return {'x': x, 'adj': adj, 'L0_gnn_W_w': _L0_gnn_in['W_w'], 'L0_gnn_W_b': _L0_gnn_in['W_b'], 'L0_gnn_a': _L0_gnn_in['a'], 'L0_ffn_Wq': _L0_ffn_in['Wq'], 'L0_ffn_bq': _L0_ffn_in['bq'], 'L0_ffn_ln_g': _L0_ffn_in['ln_g'], 'L0_ffn_ln_b': _L0_ffn_in['ln_b'], 'L0_ffn_keys0': _L0_ffn_in['keys0'], 'L0_ffn_keys1': _L0_ffn_in['keys1'], 'L0_ffn_expert_down': _L0_ffn_in['expert_down'], 'L0_ffn_expert_up': _L0_ffn_in['expert_up']}

def reference(x, adj, L0_gnn_W_w, L0_gnn_W_b, L0_gnn_a, L0_ffn_Wq, L0_ffn_bq, L0_ffn_ln_g, L0_ffn_ln_b, L0_ffn_keys0, L0_ffn_keys1, L0_ffn_expert_down, L0_ffn_expert_up):
    import jax
    import jax.numpy as jnp

    def _L0_gnn_ref(x, adj, W_w, W_b, a):
        import jax, jax.numpy as jnp
        import numpy as np
        B, IN_F, OUT_F, H = (1024, 256, 256, 8)
        D = OUT_F // H
        Bn = x.shape[0]
        h = (x @ W_w.T + W_b).reshape(Bn, H, D)
        a_src, a_dst = (a[:D, 0], a[D:, 0])
        s_src = jnp.einsum('bhd,d->bh', h, a_src)
        s_dst = jnp.einsum('bhd,d->bh', h, a_dst)
        e = jax.nn.leaky_relu(s_src[:, None, :] + s_dst[None, :, :], negative_slope=0.2)
        e = jnp.where(adj[:, :, None] == 0, jnp.float32(-1000000000.0), e)
        attn = jax.nn.softmax(e, axis=1)
        h_prime = jnp.einsum('ijh,jhd->ihd', attn, h).reshape(Bn, H * D)
        return jax.nn.elu(h_prime)

    def _L0_ffn_ref(hidden_states, Wq, bq, ln_g, ln_b, keys0, keys1, expert_down, expert_up):
        import jax, jax.numpy as jnp
        import numpy as np
        B, S, D, O = (1, 1024, 256, 256)
        H, QD, K, PK = (8, 128, 16, 128)
        N = PK * PK
        HALF = QD // 2

        def _l2norm(x):
            n = jnp.sqrt(jnp.sum(x * x, axis=-1, keepdims=True))
            return x / jnp.maximum(n, 1e-12)
        b, s, d = hidden_states.shape
        q = (hidden_states @ Wq.T + bq).reshape(b, s, H, QD)
        mu = jnp.mean(q, axis=-1, keepdims=True)
        var = jnp.mean((q - mu) ** 2, axis=-1, keepdims=True)
        q = (q - mu) / jnp.sqrt(var + 1e-05) * ln_g + ln_b
        q0, q1 = (q[..., :HALF], q[..., HALF:])
        s0 = jnp.einsum('bshq,eq->bshe', _l2norm(q0), _l2norm(keys0))
        s1 = jnp.einsum('bshq,eq->bshe', _l2norm(q1), _l2norm(keys1))
        sc0, ix0 = jax.lax.top_k(s0, K)
        sc1, ix1 = jax.lax.top_k(s1, K)
        cs = (sc0[..., :, None] + sc1[..., None, :]).reshape(b, s, H, K * K)
        ci = (ix0[..., :, None] + ix1[..., None, :]).reshape(b, s, H, K * K)
        fs, pos = jax.lax.top_k(cs, K)
        fi = jnp.take_along_axis(ci, pos, axis=-1)
        w = jax.nn.softmax(fs, axis=-1)
        down = expert_down[fi]
        up = expert_up[fi]
        inner = jnp.einsum('bsd,bshkd->bshk', hidden_states, down)
        act = jax.nn.gelu(inner, approximate=False)
        out = jnp.einsum('bshk,bshko->bso', act * w, up)
        return out
    x = x + _L0_gnn_ref(_layernorm(x, axis=-1), adj, L0_gnn_W_w, L0_gnn_W_b, L0_gnn_a)
    x = x + _L0_ffn_ref(_layernorm(x, axis=-1)[None], L0_ffn_Wq, L0_ffn_bq, L0_ffn_ln_g, L0_ffn_ln_b, L0_ffn_keys0, L0_ffn_keys1, L0_ffn_expert_down, L0_ffn_expert_up)[0]
    return x

_drawn_inputs = setup_inputs


def setup_inputs(seed=0):
    import zlib

    import numpy as np

    out = dict(_drawn_inputs(seed))
    spreads = {'L0_gnn_W_b': (0.0, 0.1),
     'L0_ffn_bq': (0.0, 0.8),
     'L0_ffn_ln_g': (1.0, 0.6),
     'L0_ffn_ln_b': (0.0, 0.8)}
    factors = {'L0_ffn_Wq': 8.0,
     'L0_ffn_keys0': 8.0,
     'L0_ffn_keys1': 8.0,
     'L0_ffn_expert_down': 8.0,
     'L0_ffn_expert_up': 8.0}
    for name, (base, spread) in spreads.items():
        noise = np.random.default_rng([zlib.crc32(name.encode()), seed]).standard_normal(out[name].shape)
        drawn = base * np.exp(spread * noise) if base else spread * noise
        out[name] = jnp.asarray(drawn.astype(out[name].dtype))
    for name, factor in factors.items():
        out[name] = (out[name] * factor).astype(out[name].dtype)
    return out
```

```python
import concourse.bass as bass
from concourse import mybir
from contextlib import ExitStack

FP32 = mybir.dt.float32
FP16 = mybir.dt.float16
BF16 = mybir.dt.bfloat16
FP8 = mybir.dt.float8e4
U8 = mybir.dt.uint8
U16 = mybir.dt.uint16
U32 = mybir.dt.uint32
ALU = mybir.AluOpType
ACT = mybir.ActivationFunctionType
AX = mybir.AxisListType

P = 128
N = 3327
T = (N + P - 1) // P
NP = T * P
LAST = N - (T - 1) * P
D = 256
KC = D // P
H = 8
HD = D // H
HA = HD + 1
XC = 4 * HA
HT = T // 2
HN = HT * P
PASSES = 2 * H
SCALE = 1024.0
EPS = 1e-5
BY_DVE = 11
AMASKS, DMASKS = 5, 2
AHEAD = 2
CREDIT = 16


def chain(eng, sem, per=0, turn=0):
    n = [0]

    def link(ins, wait=True):
        n[0] += 1
        ins.then_inc(sem, 1)
        if wait:
            if per:
                hold(eng, sem, turn * per + n[0])
            else:
                eng.wait_ge(sem, n[0])
        return ins
    link.n = n
    return link


def hold(eng, sem, value):
    eng.wait_ge(sem, value)
    eng.nop(nofuse=True)


def bc(ap, n):
    return ap.unsqueeze(len(ap.shape)).to_broadcast(list(ap.shape) + [n])


def project(nc, ctx0, x, w, wb, a, identity, scratch_u, scratch_x, scratch_xd, keep):
    with ExitStack() as ctx:
        sb = lambda n, s, d=FP32: ctx.enter_context(nc.sbuf_tensor(n, s, d))
        pb = lambda n, s, d=FP32: ctx.enter_context(nc.psum_tensor(n, s, d))
        sem = lambda n: ctx.enter_context(nc.semaphore(n))
        xs = sb("p_xs", [P, T, D])
        ident = sb("p_ident", [P, P])
        wn = sb("p_wn", [P, KC, D])
        ablk = sb("p_ablk", [P, KC, 2 * H])
        brow = sb("p_brow", [1, D + 2 * H])
        bcol = sb("p_bcol", [P, KC])
        ones = sb("p_ones", [P, P])
        valid = sb("p_valid", [P, P])
        waug = sb("p_waug", [P, KC, D + 2 * H])
        mv = sb("p_mv", [P, T, 2])
        st = sb("p_st", [P, 2, 6])
        mv2 = sb("p_mv2", [P, 2, 2])
        rstd = sb("p_rstd", [P, T])
        xh = sb("p_xh", [P, 2, D])
        xhT = sb("p_xhT", [P, 2, KC, P])
        haug = sb("p_haug", [P, T, H, HA])
        uv = sb("p_uv", [P, T, 2 * H])
        uvs = sb("p_uvs", [P, 2, 2 * H])
        uvT = sb("p_uvT", [2 * H, NP])
        mx = sb("p_mx", [2 * H, 1])
        dmx = sb("p_dmx", [2 * H, 2 * H])
        mall = sb("p_mall", [P, 2 * H])
        tv = sb("p_tv", [P, T, H])
        t1 = sb("p_t1", [P, T, H])
        bexp = sb("p_bexp", [P, T, H])
        dexp = sb("p_dexp", [P, T, H])
        prod = sb("p_prod", [P, 2, T, HA])
        xd = sb("p_xd", [P, T, H, 2 * HA], FP16)
        xb = sb("p_xb", [P, 2, T, XC], FP16)
        ps_w = [pb(f"p_psw{k}", [P, 512]) for k in range(KC)]
        ps_t = [pb(f"p_pst{k}", [P, 512]) for k in range(2)]
        ps_h = [pb(f"p_psh{k}", [P, 512]) for k in range(2)]
        ps_v = pb("p_psv", [P, 512])
        ps_s = pb("p_pss", [P, 512])
        z_done, in_x, in_w = sem("p_zeroed"), sem("p_in_x"), sem("p_in_w")
        wt_done, waug_done = sem("p_wt"), sem("p_waug")
        dv, var_done, std_done = sem("p_dv"), sem("p_var"), sem("p_std")
        dvl, xh_done, xt_done, xhT_done = sem("p_dvl"), sem("p_xh"), sem("p_xt"), sem("p_xhT")
        mm_done, h_out, uv_out, vt_done, vt_out = sem("p_mm"), sem("p_hout"), sem("p_uvout"), sem("p_vt"), sem("p_vtout")
        dm_done, m_bc, m_out = sem("p_dm"), sem("p_mbc"), sem("p_mout")
        arg_done, exp_done, po, xb_done, u_st, x_st = (sem("p_arg"), sem("p_exp"), sem("p_po"), sem("p_xb"),
                                                       sem("p_ust"), [sem("p_xst0"), sem("p_xst1")])
        hs_done, nv_done, act_done, po_done = sem("p_hs"), sem("p_nv"), sem("p_actd"), sem("p_pod")
        NW = 5 + 2 * H

        with nc.Block() as block:
            @block.sync
            def _(sp):
                sp.dma_start(wn[:], w.rearrange("(c p) d -> p c d", p=P)).then_inc(in_w, 16)
                sp.dma_start(ident[:], identity).then_inc(in_w, 16)
                sp.dma_start(brow[0:1, 0:D], wb.unsqueeze(0)).then_inc(in_w, 16)
                sp.dma_start(bcol[:], wb.rearrange("(c p) -> p c", p=P), allow_slow_non_contiguous=True).then_inc(in_w, 16)
                sp.wait_ge(z_done, 4)
                sp.dma_start(xs[:, 0:T - 1, :], x[0:(T - 1) * P, :].rearrange("(t p) d -> p t d", p=P)).then_inc(in_x, 16)
                sp.dma_start(xs[0:LAST, T - 1, :], x[(T - 1) * P:N, :]).then_inc(in_x, 16)
                for h in range(H):
                    for s in range(2):
                        q = HD * (h % 4)
                        sp.dma_start(ablk[q:q + HD, h // 4, s * H + h:s * H + h + 1],
                                     a[s * HD:(s + 1) * HD, :]).then_inc(in_w, 16)
                sp.wait_ge(vt_out, T)
                for half in range(2):
                    sp.dma_start(scratch_u[half], uvT[0:H, half * HN:(half + 1) * HN]).then_inc(u_st, 16)
                for h in range(H):
                    sp.wait_ge(xb_done, h + 1)
                    for half in range(2):
                        sp.dma_start(scratch_x[half * H + h], xb[:, h % 2].rearrange("p t c -> p (t c)")).then_inc(x_st[h % 2], 16)
                sp.dma_start(scratch_xd, xd[:].rearrange("p t h c -> p (t h c)")).then_inc(u_st, 16)
                sp.wait_ge(u_st, 48)
                for s in range(2):
                    sp.wait_ge(x_st[s], 32 * (H // 2))

            @block.vector
            def _(dve):
                v = nc.vector
                v.memset(xs[:, T - 1, :], 0.0).then_inc(z_done, 1)
                v.memset(ablk[:], 0.0).then_inc(z_done, 1)
                v.memset(ones[:], 1.0).then_inc(z_done, 1)
                v.memset(haug[:], 1.0).then_inc(z_done, 1)
                for k in range(KC):
                    dve.wait_ge(wt_done, k + 1)
                    v.tensor_copy(waug[:, k, :], ps_w[k][:, 0:D + 2 * H]).then_inc(waug_done, 1)
                dve.wait_ge(wt_done, 3)
                v.tensor_copy(brow[0:1, D:], ps_v[0:1, 0:2 * H]).then_inc(waug_done, 1)
                dve.wait_ge(in_x, 32)
                link = chain(dve, dv)
                with dve.Fori(0, HT) as i:
                    lk = chain(dve, dvl, 5, i)
                    for s in range(2):
                        lk(v.bn_stats(st[:, s, :], xs[:, bass.ds(2 * i + s, 1), :].rearrange("p a d -> p (a d)")), wait=s == 1)
                    for s in range(2):
                        lk(v.bn_aggr(mv2[:, s, :], st[:, s, :]), wait=s == 1)
                    lk(v.tensor_copy(mv[:, bass.ds(2 * i, 2), :], mv2[:]))
                link(v.tensor_scalar(rstd[:], mv[:, :, 1], EPS, None, ALU.add), wait=False)
                dve.wait_ge(std_done, 1)
                link(v.reciprocal(rstd[:], rstd[:]))
                with dve.Fori(0, HT) as i:
                    for s in range(2):
                        t = 2 * i + s
                        dve.wait_ge(xt_done, t + 1)
                        v.tensor_scalar(xh[:, s, :], xs[:, bass.ds(t, 1), :].rearrange("p a d -> p (a d)"),
                                        mv[:, bass.ds(t, 1), 0], rstd[:, bass.ds(t, 1)],
                                        ALU.subtract, ALU.mult).then_inc(xh_done, 1)
                dve.wait_ge(vt_out, T)
                link(v.reduce_max(mx[:], uvT[:, 0:N], AX.X))
                v.tensor_scalar(dmx[:], ident[0:2 * H, 0:2 * H], mx[:, 0:1], None, ALU.mult).then_inc(dm_done, 1)
                dve.wait_ge(m_bc, 1)
                link(v.tensor_copy(mall[:], ps_s[:, 0:2 * H]))
                mb = mall[:, H:2 * H].unsqueeze(1).to_broadcast([P, T, H])
                link(v.tensor_tensor(tv[:], uv[:, :, 0:H], mb, ALU.add), wait=False)
                link(v.tensor_tensor(bexp[:], uv[:, :, H:2 * H], mb, ALU.subtract))
                v.tensor_scalar(t1[:], tv[:], 0.8, 0.0, ALU.mult, ALU.min).then_inc(arg_done, 1)
                v.tensor_scalar(tv[:], tv[:], -0.8, 0.0, ALU.mult, ALU.min).then_inc(arg_done, 1)
                v.tensor_scalar(bexp[:], bexp[:], 0.0, None, ALU.min).then_inc(arg_done, 1)
                for half in range(2):
                    v.tensor_scalar(keep.negv[:, half * H:(half + 1) * H, :],
                                    uv[:, :, H:2 * H].rearrange("p t h -> p h t"), -1.0, None, ALU.mult).then_inc(nv_done, 1)
                dve.wait_ge(exp_done, 4)
                link(v.tensor_scalar(bexp[:], bexp[:], SCALE, None, ALU.mult), wait=False)
                link(v.tensor_scalar(dexp[:], dexp[:], SCALE, None, ALU.mult))
                for h in range(H):
                    if h >= 2:
                        dve.wait_ge(x_st[h % 2], 32 * (h // 2))
                    for n, e in enumerate((bexp, dexp)):
                        link(v.tensor_tensor(prod[:, n], haug[:, :, h, :], bc(e[:, :, h], HA), ALU.mult), wait=n == 1)
                    for n in range(2):
                        link(v.tensor_copy(xb[:, h % 2, :, 2 * n * HA:(2 * n + 1) * HA], prod[:, n]), wait=n == 1)
                    for n in range(2):
                        c = 2 * n * HA
                        link(v.tensor_tensor(xb[:, h % 2, :, c + HA:c + 2 * HA], prod[:, n], xb[:, h % 2, :, c:c + HA],
                                             ALU.subtract), wait=n == 1)
                    v.tensor_copy(xd[:, :, h, :], xb[:, h % 2, :, 2 * HA:4 * HA]).then_inc(xb_done, 1)
                dve.wait_ge(hs_done, 1)
                v.tensor_copy(keep.hsum[:], ps_s[:, 0:H * HA]).then_inc(nv_done, 1)

            @block.scalar
            def _(act):
                s_ = nc.scalar
                act.wait_ge(z_done, 4)
                act.wait_ge(dv, 1)
                s_.activation(rstd[:], rstd[:], ACT.Sqrt).then_inc(std_done, 1)
                with act.Fori(0, HT) as i:
                    for s in range(2):
                        t = 2 * i + s
                        act.wait_ge(xt_done, t + 3)
                        act.wait_ge(mm_done, t + 1)
                        s_.activation(xhT[:, s], ps_t[s][:, 0:D].rearrange("p (c n) -> p c n", c=KC), ACT.Copy).then_inc(xhT_done, 1)
                        act.wait_ge(mm_done, t + 3)
                        s_.activation(haug[:, bass.ds(t, 1), :, 0:HD].rearrange("p a h d -> p (a h) d"),
                                      ps_h[s][:, 0:D].rearrange("p (h d) -> p h d", h=H), ACT.Copy).then_inc(h_out, 1)
                        s_.activation(uv[:, bass.ds(t, 1), :].rearrange("p a c -> p (a c)"), ps_h[s][:, D:D + 2 * H], ACT.Copy)
                        s_.activation(uvs[:, s, :], ps_h[s][:, D:D + 2 * H], ACT.Copy).then_inc(uv_out, 1)
                        act.wait_ge(vt_done, t + 1)
                        s_.activation(uvT[:, bass.ds(t * P, P)], ps_v[0:2 * H, 0:P], ACT.Copy).then_inc(vt_out, 1)
                act.wait_ge(arg_done, 3)
                s_.activation(keep.a[:].rearrange("p h t -> p t h"), t1[:], ACT.Exp).then_inc(exp_done, 1)
                s_.activation(keep.c[:].rearrange("p h t -> p t h"), tv[:], ACT.Exp).then_inc(exp_done, 1)
                s_.activation(dexp[:], bexp[:], ACT.Exp, scale=0.2).then_inc(exp_done, 1)
                act.wait_ge(exp_done, 3)
                s_.activation(bexp[:], bexp[:], ACT.Exp).then_inc(exp_done, 1)

            @block.tensor
            def _(pe):
                t_ = nc.tensor
                pe.wait_ge(in_w, 16 * (4 + 2 * H))
                pe.wait_ge(z_done, 4)
                for k in range(KC):
                    for c in range(KC):
                        t_.transpose(ps_w[k][:, c * P:(c + 1) * P], wn[:, c, k * P:(k + 1) * P], ident[:])
                    for c in range(KC):
                        last = t_.matmul(ps_w[k][:, D:D + 2 * H], wn[:, c, k * P:(k + 1) * P], ablk[:, c, :],
                                         start=c == 0, stop=c == KC - 1)
                    last.then_inc(wt_done, 1)
                for c in range(KC):
                    last = t_.matmul(ps_v[0:1, 0:2 * H], bcol[:, c:c + 1], ablk[:, c, :], start=c == 0, stop=c == KC - 1)
                last.then_inc(wt_done, 1)
                pe.wait_ge(waug_done, KC + 1)
                pe.nop().then_inc(xt_done, 2)
                pe.nop().then_inc(mm_done, 2)
                with pe.Fori(0, HT) as i:
                    for s in range(2):
                        t = 2 * i + s
                        pe.wait_ge(xh_done, t + 1)
                        for k in range(KC):
                            last = t_.transpose(ps_t[s][:, k * P:(k + 1) * P], xh[:, s, k * P:(k + 1) * P], ident[:])
                        last.then_inc(xt_done, 1)
                        pe.wait_ge(xhT_done, t + 1)
                        for k in range(KC):
                            t_.matmul(ps_h[s][:, 0:D + 2 * H], xhT[:, s, k, :], waug[:, k, :], start=k == 0, stop=False)
                        t_.matmul(ps_h[s][:, 0:D + 2 * H], ones[0:1, :], brow[0:1, :], start=False, stop=True).then_inc(mm_done, 1)
                        pe.wait_ge(uv_out, t + 1)
                        t_.transpose(ps_v[0:2 * H, 0:P], uvs[:, s, :], ident[:]).then_inc(vt_done, 1)
                pe.wait_ge(dm_done, 1)
                t_.matmul(ps_s[:, 0:2 * H], ones[0:2 * H, :], dmx[:], start=True, stop=True).then_inc(m_bc, 1)
                pe.wait_ge(h_out, T)
                pe.wait_ge(dv, 4)
                for t in range(T):
                    rows = LAST if t == T - 1 else P
                    last = t_.matmul(ps_s[:, 0:H * HA], ones[0:rows, :], haug[0:rows, t].rearrange("p h d -> p (h d)"),
                                     start=t == 0, stop=t == T - 1)
                last.then_inc(hs_done, 1)


def adjacency(nc, adj, identity, scratch_xd, keep):
    with ExitStack() as ctx:
        sb = lambda n, s, d=FP32: ctx.enter_context(nc.sbuf_tensor(n, s, d))
        pb = lambda n, s, d=FP32: ctx.enter_context(nc.psum_tensor(n, s, d))
        sem = lambda n: ctx.enter_context(nc.semaphore(n))
        ident32 = sb("a_id32", [P, P])
        ident = sb("a_ident", [P, P], BF16)
        xd = sb("a_xd", [P, T, H, 2 * HA], FP16)
        in_xd = sem("a_inxd")
        stage = [sb(f"a_stage{s}", [P, NP], BF16) for s in range(2)]
        col = [sb(f"a_col{s}", [P, T, P], U8) for s in range(2)]
        raw = [sb(f"a_raw{s}", [P, H, 2, HA]) for s in range(2)]
        GRP = 8
        groups = [(g, min(GRP, T - g)) for g in range(0, T, GRP)]
        NG = len(groups)
        ps_t = [pb(f"a_pst{k}", [P, GRP * P], BF16) for k in range(NG)]
        ps_d = [[pb(f"a_psd{s}{k}", [P, 512]) for k in range(2)] for s in range(2)]
        zeroed, in_id, id_done = sem("a_zero"), sem("a_inid"), sem("a_id")
        in_adj = [sem("a_in0"), sem("a_in1")]
        tr, tr_out, copied, mm, raw_done, add_done, stage_free = (sem("a_tr"), sem("a_trout"), sem("a_copied"), sem("a_mm"),
                                                                sem("a_raw"), sem("a_add"), sem("a_sfree"))

        with nc.Block() as block:
            @block.sync
            def _(sp):
                sp.dma_start(ident32[:], identity).then_inc(in_id, 16)
                sp.dma_start(xd[:].rearrange("p t h c -> p (t h c)"), scratch_xd).then_inc(in_xd, 16)

            @block.gpsimd
            def _(pool):
                g = nc.gpsimd
                for s in range(2):
                    g.memset(stage[s][:, N:NP], 0.0).then_inc(zeroed, 1)

                def load(t, s, rows=P):
                    g.dma_start(stage[s][0:rows, 0:N], adj[bass.ds(t * P, rows), :]).then_inc(in_adj[s], 16)

                def turn(t, s, rows=P):
                    pool.wait_ge(tr, NG * (t + 1))
                    load(t + 2, s, rows)
                    collect(t, s)

                def collect(t, s):
                    pool.wait_ge(tr_out, NG * (t + 1))
                    g.tensor_copy(keep.col32(t), col[s][:].bitcast(U32)).then_inc(copied, 1)
                    pool.wait_ge(raw_done, t + 1)
                    g.tensor_tensor(keep.adjd[:, bass.ds(t, 1)].rearrange("p a h d -> p (a h) d"), raw[s][:, :, 0, :],
                                    raw[s][:, :, 1, :], ALU.add).then_inc(add_done, 1)
                pool.wait_ge(zeroed, 2)
                load(0, 0)
                load(1, 1)
                with pool.Fori(0, HT - 2) as i:
                    for s in range(2):
                        turn(2 * i + s, s)
                turn(T - 4, 0)
                turn(T - 3, 1, LAST)
                collect(T - 2, 0)
                collect(T - 1, 1)

            @block.vector
            def _(dve):
                v = nc.vector
                dve.wait_ge(in_id, 16)
                v.tensor_copy(ident[:], ident32[:]).then_inc(id_done, 1)
                v.nop().then_inc(copied, 2)
                with dve.Fori(0, HT) as i:
                    for s in range(2):
                        t = 2 * i + s
                        dve.wait_ge(copied, t + 1)
                        dve.wait_ge(mm, t + 1)
                        for n, (g0, w) in enumerate(groups):
                            dve.wait_ge(tr, NG * t + n + 1)
                            v.tensor_scalar(col[s][:, g0:g0 + w, :].rearrange("p a b -> p (a b)"), ps_t[n][:, 0:w * P],
                                            0.0, 64.0, ALU.not_equal, ALU.mult).then_inc(tr_out, 1)

            @block.scalar
            def _(act):
                s_ = nc.scalar
                act.nop().then_inc(add_done, 2)
                with act.Fori(0, HT) as i:
                    for s in range(2):
                        t = 2 * i + s
                        act.wait_ge(mm, t + 3)
                        act.wait_ge(add_done, t + 1)
                        for k in range(2):
                            ins = s_.activation(raw[s][:, 4 * k:4 * k + 4].rearrange("p h a d -> p (h a d)"),
                                                ps_d[s][k][:, 0:8 * HA], ACT.Copy)
                        ins.then_inc(raw_done, 1)

            @block.tensor
            def _(pe):
                t_ = nc.tensor
                pe.nop().then_inc(mm, 2)
                pe.wait_ge(id_done, 1)

                def transposes(t, s, loads):
                    pe.wait_ge(in_adj[s], 16 * loads)
                    pe.wait_ge(zeroed, 2)
                    for n, (g0, w) in enumerate(groups):
                        if not (isinstance(t, int) and t == 0):
                            pe.wait_ge(tr_out, NG * (t - 1) + n + 1)
                        for k in range(w):
                            last = t_.transpose(ps_t[n][:, k * P:(k + 1) * P], stage[s][:, (g0 + k) * P:(g0 + k + 1) * P], ident[:])
                        last.then_inc(tr, 1)

                def products(t, s):
                    hold(pe, tr_out, NG * (t + 1))
                    for j in range(T):
                        for k in range(2):
                            last = t_.matmul(ps_d[s][k][:, 0:8 * HA], col[s][:, j, :].bitcast(FP8),
                                             xd[:, j, 4 * k:4 * k + 4, :].rearrange("p h c -> p (h c)"),
                                             start=j == 0, stop=j == T - 1)
                    last.then_inc(mm, 1)
                transposes(0, 0, 1)
                pe.wait_ge(in_xd, 16)
                with pe.Fori(0, HT - 1) as i:
                    transposes(2 * i + 1, 1, i + 1)
                    pe.wait_ge(add_done, 2 * i + 1)
                    products(2 * i, 0)
                    transposes(2 * i + 2, 0, i + 2)
                    pe.wait_ge(add_done, 2 * i + 2)
                    products(2 * i + 1, 1)
                transposes(T - 1, 1, HT)
                pe.wait_ge(add_done, T - 1)
                products(T - 2, 0)
                pe.wait_ge(add_done, T)
                products(T - 1, 1)


def attention(nc, scratch_u, scratch_x, keep):
    with ExitStack() as ctx:
        sb = lambda n, s, d=FP32: ctx.enter_context(nc.sbuf_tensor(n, s, d))
        pb = lambda n, s, d=FP32: ctx.enter_context(nc.psum_tensor(n, s, d))
        sem = lambda n: ctx.enter_context(nc.semaphore(n))
        PER = 3
        NB = (HT + PER - 1) // PER
        ub = [sb(f"g_u{s}", [P, HN]) for s in range(2)]
        nv = [sb(f"g_nv{s}", [P, T]) for s in range(2)]
        xo = [sb(f"g_x{s}", [P, T, XC], FP16) for s in range(2)]
        mask = {True: [sb(f"g_amask{k}", [P, HN], FP8) for k in range(AMASKS)],
                False: [sb(f"g_dmask{k}", [P, HN], FP8) for k in range(DMASKS)]}
        raw = sb("g_raw", [P, HT, XC])
        comb = sb("g_comb", [P, HT, 2, HA])
        acc = pb("g_acc", [P, NB, 512])
        loaded = [sem("g_in0"), sem("g_in1")]
        signs, made, ready, free, evac, summed, pl = (sem("g_signs"), sem("g_made"), sem("g_ready"), sem("g_free"), sem("g_evac"),
                                                      sem("g_summed"), sem("g_pl"))

        by_act = [not (j + 1) * BY_DVE // T > j * BY_DVE // T for j in range(T)] * 2
        assert 2 * (T - BY_DVE) % AMASKS == 0 and 2 * BY_DVE % DMASKS == 0
        order = [sum(1 for m in range(n) if by_act[m] == by_act[n]) for n in range(2 * T)]
        buf = [mask[by_act[n]][order[n] % (AMASKS if by_act[n] else DMASKS)] for n in range(2 * T)]
        before = [max(m for m in range(-2 * T, n) if buf[m % (2 * T)] is buf[n]) for n in range(2 * T)]
        assert min(before) >= -CREDIT

        with nc.Block() as block:
            @block.sync
            def _(sp):
                def load(p, s):
                    sp.dma_start(ub[s][:], scratch_u[bass.ds(p, 1), :].partition_broadcast(P) if not isinstance(p, int)
                                 else scratch_u[p:p + 1, :].partition_broadcast(P)).then_inc(loaded[s], 16)
                    sp.dma_start(xo[s][:].rearrange("p t c -> p (t c)"), scratch_x[bass.ds(p, 1)].rearrange("a p n -> p (a n)")).then_inc(loaded[s], 16)
                    sp.dma_start(nv[s][:], keep.negv[:, bass.ds(p, 1), :].rearrange("p a t -> p (a t)")).then_inc(loaded[s], 16)
                load(0, 0)
                load(1, 1)
                with sp.Fori(0, PASSES // 2 - 1) as r:
                    for s in range(2):
                        sp.wait_ge(free, CREDIT + T * (2 * r + s + 1))
                        load(2 * r + s + 2, s)

            @block.scalar
            def _(act):
                s_ = nc.scalar
                full = (NB - 1) * PER

                def masks(r, s, columns):
                    for j in columns:
                        n = s * T + j
                        if j == 0:
                            act.wait_ge(loaded[s], 48 * (r + 1))
                        if by_act[n]:
                            hold(act, free, 2 * T * r + before[n] + 1 + CREDIT)
                            s_.activation(buf[n][:], ub[s][:], ACT.Sign, bias=nv[s][:, j:j + 1], scale=-1.0, saturate=False).then_inc(signs, 1)

                def copy_out(p):
                    act.wait_ge(free, CREDIT + T * (p + 1))
                    act.wait_ge(summed, p + 1)
                    s_.activation(raw[:, 0:full, :].rearrange("p (b t) c -> p b (t c)", t=PER),
                                  acc[:, 0:NB - 1, 0:PER * XC], ACT.Copy).then_inc(evac, 1)
                    s_.activation(raw[:, full:HT, :].rearrange("p t c -> p (t c)"),
                                  acc[:, NB - 1, 0:(HT - full) * XC], ACT.Copy).then_inc(evac, 1)

                masks(0, 0, range(AHEAD))

                def turn(r, more=True):
                    masks(r, 0, range(AHEAD, T))
                    masks(r, 1, range(AHEAD))
                    copy_out(2 * r)
                    masks(r, 1, range(AHEAD, T))
                    if more:
                        masks(r + 1, 0, range(AHEAD))
                    copy_out(2 * r + 1)
                with act.Fori(0, PASSES // 2 - 1) as r:
                    turn(r)
                turn(PASSES // 2 - 1, False)

            @block.vector
            def _(dve):
                v = nc.vector
                A2, D2 = 2 * (T - BY_DVE), 2 * BY_DVE
                with dve.Fori(0, 2) as half:
                    with dve.Fori(0, H // 2) as q:
                        def make(n):
                            s, j = n // T, n % T
                            hold(dve, free, (H * T) * half + (2 * T) * q + before[n] + 1 + CREDIT)
                            v.tensor_scalar(buf[n][:], ub[s][:], nv[s][:, j:j + 1], 2.0, ALU.is_gt, ALU.mult, saturate=False).then_inc(made, 1)

                        for n in range(2 * T):
                            s, j = n // T, n % T
                            if j == 0:
                                dve.wait_ge(loaded[s], 16 * 3 * (H // 2) * half + 48 * q + 48)
                            if j + 1 < T and not by_act[n + 1]:
                                make(n + 1)
                            bits, edges = buf[n][:].bitcast(U32), keep.adj32(half, j)
                            if by_act[n]:
                                dve.wait_ge(signs, (A2 * (H // 2)) * half + A2 * q + order[n] + 1)
                                v.scalar_tensor_tensor(bits, bits, 1, edges, ALU.logical_shift_right, ALU.bitwise_and).then_inc(ready, 1)
                            else:
                                dve.wait_ge(made, (D2 * (H // 2)) * half + D2 * q + order[n] + 1)
                                v.tensor_tensor(bits, bits, edges, ALU.bitwise_and).then_inc(ready, 1)

            @block.tensor
            def _(pe):
                t_ = nc.tensor
                pe.nop().then_inc(free, CREDIT)
                pe.nop().then_inc(evac, 2)
                with pe.Fori(0, PASSES // 2) as r:
                    for n in range(2 * T):
                        s, j = n // T, n % T
                        if j == 0:
                            pe.wait_ge(loaded[s], 48 * (r + 1))
                            pe.wait_ge(evac, 2 * (2 * r + s) + 2)
                        hold(pe, ready, 2 * T * r + n + 1)
                        for it in range(HT):
                            b, c = it // PER, it % PER
                            last = t_.matmul(acc[:, b, c * XC:(c + 1) * XC], buf[n][:, it * P:(it + 1) * P],
                                             xo[s][:, j, :], start=(j == 0 and c == 0), stop=j == T - 1, skip_group_check=True)
                        last.then_inc(free, 1)

            @block.gpsimd
            def _(pool):
                g = nc.gpsimd
                g.nop().then_inc(summed, 1)
                with pool.Fori(0, 2) as half:
                    with pool.Fori(0, H) as h:
                        p = H * half + h
                        rr = raw[:].rearrange("p t (k a d) -> p t k a d", k=2, a=2)
                        at = keep.adjd[:, bass.ds(half * HT, HT), bass.ds(h, 1), :].rearrange("p t a d -> p t (a d)")
                        link = chain(pool, pl, 6, p)
                        pool.wait_ge(evac, 2 * p + 4)
                        link(g.tensor_tensor(comb[:, :, 0], rr[:, :, 0, 0], rr[:, :, 0, 1], ALU.add), wait=False)
                        link(g.tensor_tensor(comb[:, :, 1], rr[:, :, 1, 0], rr[:, :, 1, 1], ALU.add))
                        g.nop().then_inc(summed, 1)
                        link(g.tensor_tensor(comb[:, :, 1], at, comb[:, :, 1], ALU.subtract))
                        ah = keep.a[:, bass.ds(h, 1), bass.ds(half * HT, HT)].rearrange("p a t -> p (a t)")
                        ch = keep.c[:, bass.ds(h, 1), bass.ds(half * HT, HT)].rearrange("p a t -> p (a t)")
                        link(g.tensor_tensor(comb[:, :, 0], comb[:, :, 0], bc(ah, HA), ALU.mult), wait=False)
                        link(g.tensor_tensor(comb[:, :, 1], comb[:, :, 1], bc(ch, HA), ALU.mult))
                        link(g.tensor_tensor(at, comb[:, :, 0], comb[:, :, 1], ALU.add))


def residual(nc, x, identity, keep, scratch_x1, yT):
    with ExitStack() as ctx:
        sb = lambda n, s, d=FP32: ctx.enter_context(nc.sbuf_tensor(n, s, d))
        pb = lambda n, s, d=FP32: ctx.enter_context(nc.psum_tensor(n, s, d))
        sem = lambda n: ctx.enter_context(nc.semaphore(n))
        ident = sb("r_ident", [P, P])
        xs = sb("r_xs", [P, T, D])
        flag = sb("r_flag", [P, H])
        fall = sb("r_fall", [P, H, HA])
        num = sb("r_num", [P, H, HA])
        rec = sb("r_rec", [P, H])
        hv = [sb(f"r_hv{s}", [P, D]) for s in range(2)]
        ng = [sb(f"r_ng{s}", [P, D]) for s in range(2)]
        st = sb("r_st", [P, 6])
        mv1 = sb("r_mv1", [P, 2])
        mv = sb("r_mv", [P, T, 2])
        rstd = sb("r_rstd", [P, T])
        y = [sb(f"r_y{s}", [P, D]) for s in range(2)]
        ps = [pb(f"r_ps{s}", [P, 512]) for s in range(2)]
        stored = sem("r_stored")
        zeroed, in_x, dl, dl1, neg, ex, dl2, std, y_done, tr, out = (sem("r_z"), sem("r_inx"), sem("r_dl"), sem("r_dl1"), sem("r_neg"), sem("r_ex"),
                                                               sem("r_dl2"), sem("r_std"), sem("r_y"), sem("r_tr"), sem("r_out"))
        with nc.Block() as block:
            @block.sync
            def _(sp):
                sp.dma_start(ident[:], identity).then_inc(in_x, 16)
                sp.dma_start(xs[:, 0:T - 1, :], x[0:(T - 1) * P, :].rearrange("(t p) d -> p t d", p=P)).then_inc(in_x, 16)
                sp.wait_ge(zeroed, 1)
                sp.dma_start(xs[0:LAST, T - 1, :], x[(T - 1) * P:N, :]).then_inc(in_x, 16)
                sp.wait_ge(dl, 10 * T)
                sp.dma_start(scratch_x1.rearrange("(t p) d -> p t d", p=P), xs[:]).then_inc(stored, 16)
                sp.wait_ge(stored, 16)

            @block.vector
            def _(dve):
                v = nc.vector
                v.memset(xs[:, T - 1, :], 0.0).then_inc(zeroed, 1)
                dve.wait_ge(in_x, 48)
                hsum = keep.hsum[:].rearrange("p (h d) -> p h d", h=H)
                with dve.Fori(0, HT) as i:
                    lk = chain(dve, dl, 20, i)
                    for s in range(2):
                        t = 2 * i + s
                        row = keep.adjd[:, bass.ds(t, 1)].rearrange("p a h d -> p (a h) d")
                        xt = xs[:, bass.ds(t, 1), :].rearrange("p a d -> p (a d)")
                        lk(v.tensor_scalar(flag[:], row[:, :, HD], 0.0, None, ALU.is_equal))
                        lk(v.tensor_tensor(fall[:], hsum, bc(flag[:], HA), ALU.mult))
                        lk(v.tensor_tensor(num[:], row, fall[:], ALU.add))
                        lk(v.reciprocal(rec[:], num[:, :, HD]))
                        lk(v.tensor_tensor(hv[s][:].rearrange("p (h d) -> p h d", h=H), num[:, :, 0:HD], bc(rec[:], HD), ALU.mult))
                        v.tensor_scalar(ng[s][:], hv[s][:], 0.0, None, ALU.min).then_inc(neg, 1)
                        lk(v.scalar_tensor_tensor(xt, hv[s][:], 0.0, xt, ALU.max, ALU.add), wait=False)
                        dve.wait_ge(ex, t + 1)
                        dve.wait_ge(dl, 20 * i + 10 * s + 6)
                        lk(v.scalar_tensor_tensor(xt, ng[s][:], -1.0, xt, ALU.add, ALU.add))
                        lk(v.bn_stats(st[:], xt))
                        lk(v.bn_aggr(mv1[:], st[:]))
                        lk(v.tensor_copy(mv[:, bass.ds(t, 1), :].rearrange("p a d -> p (a d)"), mv1[:]))
                l1 = chain(dve, dl1)
                l1(v.tensor_scalar(rstd[:], mv[:, :, 1], EPS, None, ALU.add))
                dve.wait_ge(std, 1)
                l1(v.reciprocal(rstd[:], rstd[:]))
                with dve.Fori(0, HT) as i:
                    for s in range(2):
                        t = 2 * i + s
                        dve.wait_ge(tr, t + 1)
                        v.tensor_scalar(y[s][:], xs[:, bass.ds(t, 1), :].rearrange("p a d -> p (a d)"), mv[:, bass.ds(t, 1), 0],
                                        rstd[:, bass.ds(t, 1)], ALU.subtract, ALU.mult).then_inc(y_done, 1)

            @block.scalar
            def _(act):
                s_ = nc.scalar
                with act.Fori(0, HT) as i:
                    for s in range(2):
                        act.wait_ge(neg, 2 * i + s + 1)
                        s_.activation(ng[s][:], ng[s][:], ACT.Exp).then_inc(ex, 1)
                act.wait_ge(dl1, 1)
                s_.activation(rstd[:], rstd[:], ACT.Sqrt).then_inc(std, 1)
                with act.Fori(0, HT) as i:
                    for s in range(2):
                        t = 2 * i + s
                        act.wait_ge(tr, t + 3)
                        s_.activation(yT[:, :, bass.ds(t * P, P)], ps[s][:, 0:D].rearrange("p (c n) -> p c n", c=KC), ACT.Copy).then_inc(out, 1)

            @block.tensor
            def _(pe):
                t_ = nc.tensor
                pe.wait_ge(in_x, 48)
                pe.nop().then_inc(tr, 2)
                pe.nop().then_inc(out, 2)
                with pe.Fori(0, HT) as i:
                    for s in range(2):
                        t = 2 * i + s
                        pe.wait_ge(y_done, t + 1)
                        pe.wait_ge(out, t + 1)
                        for k in range(KC):
                            last = t_.transpose(ps[s][:, k * P:(k + 1) * P], y[s][:, k * P:(k + 1) * P], ident[:])
                        last.then_inc(tr, 1)


class Keep:
    pass


PAIRS = 50
TOP = 16
KEYS = 128
QD = 128
HALF = QD // 2
G = 2
GT = G * P
NGRP = T // G
U = G * H
ROWS = [TOP // (i + 1) for i in range(TOP)]
AT = [sum(ROWS[:i]) for i in range(TOP)]
SLOTS = 23
BLK = 4
KT = 2
KR = 4 * SLOTS
EA, EB = 32, 8
QUAD = 4
WSCALE = 4096.0
LOW = -3.0e38


def slots():
    cells = [(i + 1, j + 1) for i in range(TOP) for j in range(ROWS[i])]

    def together(a, b):
        return a[0] * a[1] + b[0] * b[1] - min(a[0], b[0]) * min(a[1], b[1]) <= TOP
    near = [[k for k in range(PAIRS) if k != m and together(cells[m], cells[k])] for m in range(PAIRS)]
    slot = [-1] * PAIRS
    for _ in range(PAIRS):
        open_ = [m for m in range(PAIRS) if slot[m] < 0]
        used = {m: {slot[k] for k in near[m] if slot[k] >= 0} for m in open_}
        m = max(open_, key=lambda m: (len(used[m]), len(near[m]), -m))
        slot[m] = min(c for c in range(PAIRS) if c not in used[m])
    assert max(slot) < SLOTS
    return slot


def router_weights(nc, wq, bq, ln_g, ln_b, keys, down, up, identity, centre, own, k):
    with ExitStack() as ctx:
        sb = lambda n, s, d=FP32: ctx.enter_context(nc.sbuf_tensor(n, s, d))
        pb = lambda n, s, d=FP32: ctx.enter_context(nc.psum_tensor(n, s, d))
        sem = lambda n: ctx.enter_context(nc.semaphore(n))
        wn = sb("w_wn", [P, H, D])
        bt = sb("w_bt", [P, H])
        cm = sb("w_cm", [P, P])
        gb = sb("w_gb", [P, 2])
        kn = sb("w_kn", [P, 2, HALF])
        ksq = sb("w_ksq", [P, 2, HALF])
        kz = sb("w_kz", [P, 2, QD])
        nrm = sb("w_nrm", [P, 2])
        ones = sb("w_ones", [P, P])
        half = sb("w_half", [P, 2])
        tmp = sb("w_tmp", [P, 2])
        kt = sb("w_kt", [P, 2 * KEYS])
        bsel = sb("w_bsel", [P, 2 * H])
        dn = sb("w_dn", [P, KC, D])
        ps = [pb(f"w_ps{n}", [P, 512]) for n in range(8)]
        got, zero, st, mm, sq, ev = (sem("w_got"), sem("w_zero"), sem("w_st"), sem("w_mm"), sem("w_sq"), sem("w_ev"))
        with nc.Block() as block:
            @block.sync
            def _(sp):
                sp.dma_start(wn[:], wq.rearrange("(h q) d -> q h d", q=QD)).then_inc(got, 16)
                sp.dma_start(bt[:], bq.rearrange("(h q) -> q h", q=QD), allow_slow_non_contiguous=True).then_inc(got, 16)
                sp.dma_start(cm[:], centre).then_inc(got, 16)
                sp.dma_start(k.ident[:], identity).then_inc(got, 16)
                sp.dma_start(gb[:, 0:1], ln_g.unsqueeze(1), allow_slow_non_contiguous=True).then_inc(got, 16)
                sp.dma_start(gb[:, 1:2], ln_b.unsqueeze(1), allow_slow_non_contiguous=True).then_inc(got, 16)
                for n in range(2):
                    sp.dma_start(kn[:, n, :], keys[n]).then_inc(got, 16)
                sp.dma_start(dn[:], down[0:EA * EB, :].rearrange("(c p) d -> p c d", p=P)).then_inc(got, 16)
                for q in range(QUAD):
                    sp.dma_start(k.up[q:P:QUAD], up[0:EA * EB, :].rearrange("(a b) o -> a b o", b=EB)).then_inc(got, 16)
                sp.dma_start(k.own[:], own).then_inc(got, 16)
                sp.wait_ge(got, 16 * (10 + QUAD))

            @block.vector
            def _(dve):
                v = nc.vector
                link = chain(dve, st)
                v.memset(ones[:], 1.0).then_inc(zero, 1)
                v.memset(kz[:], 0.0).then_inc(zero, 1)
                v.memset(half[:], 0.0).then_inc(zero, 1)
                v.memset(bsel[:], 0.0).then_inc(zero, 1)
                v.memset(k.mean8[:], 0.0).then_inc(zero, 1)
                v.memset(k.eps[:], EPS).then_inc(zero, 1)
                dve.wait_ge(zero, 6)
                v.memset(half[0:HALF, 0:1], 1.0).then_inc(zero, 1)
                v.memset(half[HALF:QD, 1:2], 1.0).then_inc(zero, 1)
                v.memset(k.mean8[:, H - 1:H], 1.0 / QD).then_inc(zero, 1)
                v.memset(k.rsq[:, 0:1], 1.0 / QD).then_inc(zero, 1)
                dve.wait_ge(zero, 10)
                dve.wait_ge(got, 16 * (10 + QUAD))
                link(v.tensor_copy(k.ident16[:], k.ident[:]), wait=False)
                link(v.tensor_tensor(ksq[:], kn[:], kn[:], ALU.mult))
                link(v.tensor_reduce(nrm[:], ksq[:], AX.X, ALU.add))
                dve.wait_ge(sq, 1)
                link(v.tensor_scalar(nrm[:], nrm[:], 1e-12, None, ALU.max))
                link(v.reciprocal(nrm[:], nrm[:]))
                for n in range(2):
                    link(v.tensor_scalar(kz[:, n, n * HALF:(n + 1) * HALF], kn[:, n, :], nrm[:, n:n + 1], None, ALU.mult), wait=n == 1)
                link(v.tensor_copy(bsel[:, H - 1:H], gb[:, 1:2]), wait=False)
                link(v.tensor_scalar(tmp[:], half[:], gb[:, 1:2], None, ALU.mult))
                link(v.tensor_scalar(k.rq[:], tmp[:], gb[:, 0:1], None, ALU.mult), wait=False)
                link(v.tensor_scalar(k.rsq[:, 1:3], half[:], gb[:, 0:1], gb[:, 0:1], ALU.mult, ALU.mult), wait=False)
                link(v.tensor_scalar(tmp[:], tmp[:], gb[:, 1:2], None, ALU.mult))
                dve.wait_ge(mm, 2)
                link(v.tensor_copy(kt[:], ps[4][:, 0:2 * KEYS]))
                link(v.tensor_scalar(k.kg[:], kt[:], gb[:, 0:1], None, ALU.mult), wait=False)
                dve.wait_ge(mm, 3)
                v.tensor_copy(k.bsq[:], ps[5][:, 0:2]).then_inc(ev, 1)
                dve.wait_ge(mm, 4)
                for n in range(4):
                    v.tensor_copy(k.kb[:, 2 * n:2 * n + 2, :].rearrange("p h k -> p (h k)"), ps[n][0:H, :]).then_inc(ev, 1)
                dve.wait_ge(mm, 5)
                for n in range(4):
                    v.tensor_copy(k.wq[:, n // 2, (n % 2) * 512:(n % 2 + 1) * 512], ps[n][:]).then_inc(ev, 1)
                dve.wait_ge(mm, 6)
                v.tensor_copy(k.bq[:], ps[5][:, 0:H]).then_inc(ev, 1)
                for q in range(QUAD):
                    for c in range(KC):
                        v.tensor_copy(k.down[:, c, :, :, q],
                                      ps[6 + c][:, 0:D].rearrange("p (a b) -> p b a", b=EB)).then_inc(ev, 1)

            @block.scalar
            def _(act):
                act.wait_ge(st, 3)
                nc.scalar.activation(nrm[:], nrm[:], ACT.Sqrt).then_inc(sq, 1)

            @block.tensor
            def _(pe):
                t_ = nc.tensor
                pe.wait_ge(zero, 10)
                pe.wait_ge(st, 12)
                for n in range(2):
                    t_.transpose(ps[4][:, n * KEYS:(n + 1) * KEYS], kz[:, n, :], k.ident[:]).then_inc(mm, 1)
                t_.matmul(ps[5][:, 0:2], ones[:], tmp[:], start=True, stop=True).then_inc(mm, 1)
                pe.wait_ge(st, 13)
                for h in range(H):
                    last = t_.matmul(ps[h // 2][0:H, (h % 2) * 256:(h % 2 + 1) * 256], bsel[:, H - 1 - h:2 * H - 1 - h], kt[:],
                                     start=True, stop=True)
                last.then_inc(mm, 1)
                pe.wait_ge(ev, 5)
                for h in range(H):
                    for c in range(KC):
                        last = t_.matmul(ps[2 * c + h // 4][:, (h % 4) * P:(h % 4 + 1) * P], wn[:, h, c * P:(c + 1) * P], cm[:],
                                         start=True, stop=True)
                last.then_inc(mm, 1)
                t_.matmul(ps[5][:, 0:H], cm[:], bt[:], start=True, stop=True)
                for c in range(KC):
                    for e in range(KC):
                        last = t_.transpose(ps[6 + c][:, e * P:(e + 1) * P], dn[:, e, c * P:(c + 1) * P], k.ident[:])
                last.then_inc(mm, 1)


def experts(nc, yT, scratch_x1, merge, k, out):
    with ExitStack() as ctx:
        sb = lambda n, s, d=FP32: ctx.enter_context(nc.sbuf_tensor(n, s, d))
        pb = lambda n, s, d=FP32: ctx.enter_context(nc.psum_tensor(n, s, d))
        sem = lambda n: ctx.enter_context(nc.semaphore(n))
        qT = sb("f_qT", [P, H, GT])
        qq = sb("f_qq", [P, H, GT])
        stdT = sb("f_stdT", [H, GT])
        std = sb("f_std", [P, U])
        fac = sb("f_fac", [P, U, 2])
        fa2 = sb("f_fa2", [P, U, 2])
        z = sb("f_z", [P, U, 2 * KEYS])
        zr = sb("f_zr", [P, 2, 2 * KEYS])
        top = sb("f_top", [P, U, 2, TOP])
        idx = sb("f_idx", [P, U, 2, TOP], U16)
        sc = sb("f_sc", [P, U, 2, TOP])
        ixf = sb("f_ixf", [P, U, 2, TOP])
        cand = sb("f_cand", [P, U, PAIRS])
        ecand = sb("f_ecand", [P, U, PAIRS])
        cr1 = sb("f_cr1", [P, U, PAIRS])
        cr2 = sb("f_cr2", [P, U, PAIRS])
        best = sb("f_best", [P, U, TOP])
        be = sb("f_be", [P, U, TOP])
        zsum = sb("f_zsum", [P, U])
        wgt = cr1
        wm = sb("f_wm", [P, U, PAIRS])
        em = sb("f_em", [P, U, PAIRS], FP16)
        wT = sb("f_wT", [2 * PAIRS, BLK, GT])
        eT = sb("f_eT", [2 * PAIRS, BLK, GT], FP16)
        mg = sb("f_mg", [2 * PAIRS, 2, KR])
        mg16 = sb("f_mg16", [2 * PAIRS, 2, KR], FP16)
        wh = sb("f_wh", [KR, KT * GT], FP16)
        wl = sb("f_wl", [KR, KT * GT], FP16)
        eu = sb("f_eu", [KR, KT * GT], U16)
        ea = sb("f_ea", [KR, KT * GT], U16)
        eb = sb("f_eb", [KR, KT * GT], U16)
        oa = sb("f_oa", [KR, KT * GT // QUAD, EA, QUAD], FP16)
        ob = sb("f_ob", [KR, EB, KT * GT], FP16)
        wob = [sb(f"f_wob{n}", [KR, EB, KT * GT], FP16) for n in range(2)]
        hh = sb("f_hh", [P, G, EB, P])
        x1 = sb("f_x1", [P, G, D])
        ps_q = [pb(f"f_psq{n}", [P, 512]) for n in range(2)]
        ps_z = [pb(f"f_psz{n}", [P, 512]) for n in range(2)]
        ps_s = pb("f_pss", [P, 512])
        ps_b = [pb(f"f_psb{n}", [P, 512]) for n in range(3)]
        S_ = {n: sem("f_" + n) for n in (
            "q_mm", "q_out", "std_mm", "stdT", "stats", "std", "facs", "fac", "z_mm", "z_out", "z_free", "fstep", "tstep",
            "top", "pool", "sums", "sel", "argp", "arg", "expd", "zs", "wgtd", "masked", "mstep", "tr", "trout", "mrg", "whd",
            "oh", "ostep", "sct", "prod", "fin", "inner", "gelu", "resd", "mgd", "rfree")}
        in_x1, in_mg = [sem("f_inx0"), sem("f_inx1")], sem("f_inmg")
        put = [sem("f_put0"), sem("f_put1")]

        def grp(name, per, g, n):
            return g * per + n

        with nc.Block() as block:
            @block.sync
            def _(sp):
                sp.dma_start(mg[:], merge).then_inc(in_mg, 16)
                for t in range(G):
                    sp.nop().then_inc(put[t], 16)

                def turn(g, rows):
                    for t in range(G):
                        sp.wait_ge(put[t], 16 * g + 16)
                        sp.dma_start(x1[:, t, :], scratch_x1[bass.ds((g * G + t) * P, P), :]).then_inc(in_x1[t], 16)
                    for t in range(G):
                        sp.wait_ge(S_["resd"], G * g + G + t + 1)
                        n = rows if t == G - 1 else P
                        sp.dma_start(out[bass.ds((g * G + t) * P, n), :], x1[0:n, t, :]).then_inc(put[t], 16)
                with sp.Fori(0, NGRP - 1) as g:
                    turn(g, P)
                turn(NGRP - 1, LAST)
                for t in range(G):
                    sp.wait_ge(put[t], 16 * NGRP + 16)

            @block.tensor
            def _(pe):
                t_ = nc.tensor

                def queries(g):
                    for h in range(H):
                        n = h % 2
                        pe.wait_ge(S_["q_out"], 2 * (H * g + h) + 2)
                        for c in range(KC):
                            last = t_.matmul(ps_q[n][:, 0:GT], k.wq[:, c, h * QD:(h + 1) * QD], yT[:, c, bass.ds(g * GT, GT)],
                                             start=c == 0, stop=c == KC - 1)
                        last.then_inc(S_["q_mm"], 1)
                    pe.wait_ge(S_["q_out"], 2 * H * (g + 1) + 4)
                    pe.wait_ge(S_["z_out"], H * g + 2)
                    for h in range(H):
                        last = t_.matmul(ps_z[0][0:H, 0:GT], k.mean8[:, H - 1 - h:2 * H - 1 - h], qq[:, h, :],
                                         start=h == 0, stop=h == H - 1)
                    last.then_inc(S_["std_mm"], 1)
                    pe.wait_ge(S_["facs"], g + 1)
                    for t in range(G):
                        for h in range(H):
                            at = 5 * (t * H + h)
                            t_.matmul(ps_s[:, at:at + 2], qT[:, h, t * P:(t + 1) * P], k.rq[:], start=True, stop=True)
                            last = t_.matmul(ps_s[:, at + 2:at + 5], qq[:, h, t * P:(t + 1) * P], k.rsq[:], start=True, stop=True)
                    last.then_inc(S_["stats"], 1)
                    pe.wait_ge(S_["stdT"], g + 1)
                    for t in range(G):
                        for h2 in range(H // 2):
                            n = h2 % 2
                            pe.wait_ge(S_["z_out"], H * g + 4 * t + h2 + 1)
                            for h in (2 * h2, 2 * h2 + 1):
                                o = ps_z[n][:, (h % 2) * 256:(h % 2 + 1) * 256]
                                t_.matmul(o, qT[:, h, t * P:(t + 1) * P], k.kg[:], start=True, stop=False)
                                last = t_.matmul(o, stdT[:, t * P:(t + 1) * P], k.kb[:, h, :], start=False, stop=True)
                            last.then_inc(S_["z_mm"], 1)

                def merges(g):
                    pe.wait_ge(S_["masked"], 2 * (g + 1))
                    pe.wait_ge(S_["resd"], G * g + G)
                    for t in range(G):
                        for b in range(BLK):
                            n = t * BLK + b
                            src = wm[:, t * H + 2 * b:t * H + 2 * b + 2, :].rearrange("p h c -> p (h c)")
                            t_.transpose(ps_b[n // 4][0:2 * PAIRS, (n % 4) * P:(n % 4 + 1) * P], src, k.ident[:])
                    for t in range(G):
                        for b in range(BLK):
                            n = t * BLK + b
                            src = em[:, t * H + 2 * b:t * H + 2 * b + 2, :].rearrange("p h c -> p (h c)")
                            last = t_.transpose(ps_b[2][0:2 * PAIRS, :].bitcast(FP16)[:, n * P:(n + 1) * P], src, k.ident16[:])
                    last.then_inc(S_["tr"], 1)
                    pe.wait_ge(S_["trout"], 3 * (g + 1))
                    for kt in range(KT):
                        for n in range(2):
                            t_.matmul(ps_b[0][0:KR, kt * GT:(kt + 1) * GT], mg[:, n, :], wT[:, 2 * kt + n, :], start=n == 0, stop=n == 1)
                    for kt in range(KT):
                        for n in range(2):
                            last = t_.matmul(ps_b[1][0:KR, kt * GT:(kt + 1) * GT], mg16[:, n, :], eT[:, 2 * kt + n, :],
                                             start=n == 0, stop=n == 1)
                    last.then_inc(S_["mrg"], 1)

                def inner(g):
                    for r in range(EB // 2):
                        n = r % 2
                        pe.wait_ge(S_["gelu"], QUAD * (4 * g + r) + QUAD)
                        for b in (2 * r, 2 * r + 1):
                            for c in range(KC):
                                last = t_.matmul(ps_q[n][:, (b % 2) * GT:(b % 2 + 1) * GT], k.down[:, c, b].rearrange("p a g -> p (a g)"),
                                                 yT[:, c, bass.ds(g * GT, GT)], start=c == 0, stop=c == KC - 1)
                        last.then_inc(S_["inner"], 1)
                    pe.wait_ge(S_["gelu"], QUAD * (4 * g + 4) + 2 * QUAD)

                HALF_G = P // QUAD // 2

                def scatter(g):
                    pe.wait_ge(S_["oh"], g + 1)
                    for q in range(2 * G):
                        bank = ps_b[q % 3]
                        if q == 3:
                            pe.wait_ge(S_["prod"], 2 * G * g + 2 * G + 1)
                        for m in range(HALF_G):
                            tok = (q // 2) * P + (q % 2) * (P // 2) + m * QUAD
                            for kt in range(KT):
                                for part in range(2):
                                    at = kt * GT + tok
                                    last = t_.matmul(bank[:].rearrange("p (b m g) -> p b m g", b=EB, g=QUAD)[:, :, m, :],
                                                     oa[:, at // QUAD].rearrange("p a g -> p (a g)"),
                                                     wob[part][:, :, at:at + QUAD],
                                                     start=kt == 0 and part == 0, stop=kt == KT - 1 and part == 1)
                        last.then_inc(S_["sct"], 1)

                def final(g):
                    for t in range(G):
                        pe.wait_ge(S_["prod"], 2 * G * g + 2 * G + (2, 4)[t])
                        for b in range(EB):
                            last = t_.matmul(ps_b[1 + t][:, 0:D],
                                             hh[:, t, b, :], k.up[:, b, :], start=b == 0, stop=b == EB - 1)
                        last.then_inc(S_["fin"], 1)

                def turn(g, more=True):
                    merges(g)
                    inner(g)
                    if more:
                        queries(g + 2)
                    scatter(g)
                    final(g)
                pe.nop().then_inc(S_["q_out"], 4)
                pe.nop().then_inc(S_["z_out"], 2)
                pe.nop().then_inc(S_["gelu"], 2 * QUAD)
                pe.wait_ge(S_["mgd"], 1)
                queries(0)
                queries(1)
                with pe.Fori(0, NGRP - 2) as g:
                    turn(g)
                turn(NGRP - 2, False)
                turn(NGRP - 1, False)

            @block.scalar
            def _(act):
                s_ = nc.scalar

                def queries(g):
                    for h in range(H):
                        n = h % 2
                        act.wait_ge(S_["q_mm"], H * g + h + 1)
                        if h == 0:
                            act.wait_ge(S_["z_mm"], H * g + H)
                        s_.activation(qT[:, h, :], ps_q[n][:, 0:GT], ACT.Identity, bias=k.bq[:, h:h + 1]).then_inc(S_["q_out"], 1)
                        s_.activation(qq[:, h, :], ps_q[n][:, 0:GT], ACT.Square, bias=k.bq[:, h:h + 1]).then_inc(S_["q_out"], 1)
                    act.wait_ge(S_["std_mm"], g + 1)
                    s_.activation(stdT[:], ps_z[0][0:H, 0:GT], ACT.Sqrt, bias=k.eps[0:H, :]).then_inc(S_["stdT"], 1)
                    for t in range(G):
                        for h2 in range(H // 2):
                            n = h2 % 2
                            at = 4 * t + h2
                            act.wait_ge(S_["z_mm"], H * g + H + at + 1)
                            act.wait_ge(S_["z_free"], H * g + at + 1)
                            s_.activation(z[:, 2 * at:2 * at + 2, :].rearrange("p u c -> p (u c)"), ps_z[n][:], ACT.Copy).then_inc(S_["z_out"], 1)

                def factors(g):
                    act.wait_ge(S_["stats"], g + 1)
                    s_.activation(std[:], ps_s[:, 0:5 * U].rearrange("p (u c) -> p u c", c=5)[:, :, 2], ACT.Sqrt,
                                  bias=k.eps[:, :]).then_inc(S_["std"], 1)
                    act.wait_ge(S_["fac"], g + 1)
                    s_.activation(fac[:], fac[:], ACT.Sqrt).then_inc(S_["std"], 1)

                def weights(g):
                    act.wait_ge(S_["arg"], 2 * g + 1)
                    s_.activation(be[:], be[:], ACT.Exp).then_inc(S_["expd"], 1)
                    act.wait_ge(S_["arg"], 2 * g + 2)
                    s_.activation(wgt[:], wgt[:], ACT.Exp).then_inc(S_["expd"], 1)

                def finish(g):
                    act.wait_ge(S_["tr"], g + 1)
                    for t in range(G):
                        s_.activation(wT[:, :, t * P:(t + 1) * P], ps_b[t][0:2 * PAIRS, :].rearrange("p (b n) -> p b n", b=BLK),
                                      ACT.Copy).then_inc(S_["trout"], 1)
                    s_.activation(eT[:].rearrange("p b (t n) -> p t b n", t=G),
                                  ps_b[2][0:2 * PAIRS, :].bitcast(FP16).rearrange("p (t b n) -> p t b n", t=G, b=BLK),
                                  ACT.Copy).then_inc(S_["trout"], 1)
                    act.wait_ge(S_["mrg"], g + 1)
                    s_.activation(wh[:], ps_b[0][0:KR, :], ACT.Copy).then_inc(S_["whd"], 1)
                    act.wait_ge(S_["prod"], 2 * G * g + 4)
                    for r in range(EB // 2):
                        n = r % 2
                        act.wait_ge(S_["inner"], 4 * g + r + 1)
                        for q in range(QUAD):
                            src = ps_q[n][:].rearrange("p (b m g) -> p b m g", b=2, g=QUAD)[:, :, :, q]
                            dst = k.acts[:, 2 * r:2 * r + 2, :, q]
                            s_.activation(dst, src, ACT.Gelu, scale=k.own[:, q:q + 1]).then_inc(S_["gelu"], 1)
                act.nop().then_inc(S_["z_mm"], H)
                act.nop().then_inc(S_["prod"], 4)
                queries(0)
                factors(0)
                queries(1)
                weights(0)
                factors(1)
                with act.Fori(0, NGRP - 2) as g:
                    finish(g)
                    queries(g + 2)
                    weights(g + 1)
                    factors(g + 2)
                finish(NGRP - 2)
                weights(NGRP - 1)
                finish(NGRP - 1)

            @block.vector
            def _(dve):
                v = nc.vector

                def step(name, per, g):
                    return chain(dve, S_[name], per, g)

                def factors(g):
                    stt = ps_s[:, 0:5 * U].rearrange("p (u c) -> p u c", c=5)
                    lk = step("fstep", 6, g)
                    sdb = bc(std[:], 2)
                    dve.wait_ge(S_["std"], 2 * g + 1)
                    lk(v.tensor_tensor(fa2[:], sdb, k.bsq[:].unsqueeze(1).to_broadcast([P, U, 2]), ALU.mult))
                    lk(v.scalar_tensor_tensor(fa2[:], stt[:, :, 0:2], 2.0, fa2[:], ALU.mult, ALU.add))
                    lk(v.tensor_tensor(fa2[:], fa2[:], sdb, ALU.mult))
                    lk(v.tensor_tensor(fac[:], fa2[:], stt[:, :, 3:5], ALU.add))
                    v.tensor_scalar(fac[:], fac[:], 0.0, None, ALU.max).then_inc(S_["fac"], 1)
                    dve.wait_ge(S_["std"], 2 * g + 2)
                    lk(v.tensor_scalar(fa2[:], sdb, 1e-12, None, ALU.mult))
                    lk(v.tensor_tensor(fac[:], fac[:], fa2[:], ALU.max))
                    v.reciprocal(fac[:], fac[:]).then_inc(S_["facs"], 1)

                def topk(g):
                    lk = step("tstep", 6 * U, g)
                    for u in range(U):
                        if u % 2 == 0:
                            hold(dve, S_["z_out"], H * g + u // 2 + 3)
                        m = u % 2
                        zz = [z[:, u, n * KEYS:(n + 1) * KEYS] for n in range(2)]
                        zq = [zr[:, m, n * KEYS:(n + 1) * KEYS] for n in range(2)]
                        hi = [top[:, u, n, 0:8] for n in range(2)]
                        lo = [top[:, u, n, 8:16] for n in range(2)]
                        lk(v.max(hi[0], zz[0]), wait=False)
                        lk(v.max(hi[1], zz[1]))
                        lk(v.match_replace(zq[0], hi[0], zz[0], LOW), wait=False)
                        lk(v.match_replace(zq[1], hi[1], zz[1], LOW))
                        lk(v.max(lo[0], zq[0]), wait=False)
                        lk(v.max(lo[1], zq[1]))
                        for n in range(2):
                            last = v.max_index(idx[:, u, n, 0:8], hi[n], zz[n])
                        if u % 2 == 1:
                            last.then_inc(S_["z_free"], 1)
                        for n in range(2):
                            last = v.max_index(idx[:, u, n, 8:16], lo[n], zq[n])
                    last.then_inc(S_["top"], 1)

                def select(g):
                    hold(dve, S_["sums"], 2 * (g + 1))
                    lk = step("sel", 4 * U, g)
                    for q in range(4):
                        for u in range(U):
                            if q == 0:
                                ins = v.max(best[:, u, 0:8], cand[:, u, :])
                            elif q == 1:
                                ins = v.match_replace(cr1[:, u, :], best[:, u, 0:8], cand[:, u, :], LOW)
                            elif q == 2:
                                ins = v.max(best[:, u, 8:16], cr1[:, u, :])
                            else:
                                ins = v.match_replace(cr2[:, u, :], best[:, u, 8:16], cr1[:, u, :], LOW)
                            lk(ins, wait=u == U - 1)

                def masks(g):
                    lk = step("mstep", 3, g)
                    dve.wait_ge(S_["expd"], 2 * g + 1)
                    lk(v.tensor_reduce(zsum[:], be[:], AX.X, ALU.add))
                    lk(v.reciprocal(zsum[:], zsum[:]))
                    lk(v.tensor_scalar(zsum[:], zsum[:], WSCALE, None, ALU.mult))
                    dve.wait_ge(S_["wgtd"], g + 1)
                    v.scalar_tensor_tensor(wm[:], cr2[:], LOW / 2, wgt[:], ALU.is_lt, ALU.mult).then_inc(S_["masked"], 1)
                    v.scalar_tensor_tensor(em[:], cr2[:], LOW / 2, ecand[:], ALU.is_lt, ALU.mult).then_inc(S_["masked"], 1)

                def onehots(g):
                    lk = step("ostep", 4 + EB, g)
                    dve.wait_ge(S_["whd"], g + 1)
                    lk(v.tensor_tensor(wl[:], ps_b[0][0:KR, :], wh[:], ALU.subtract), wait=False)
                    lk(v.tensor_copy(eu[:], ps_b[1][0:KR, :]))
                    lk(v.tensor_scalar(ea[:], eu[:], 3, None, ALU.logical_shift_right), wait=False)
                    lk(v.tensor_scalar(eb[:], eu[:], EB - 1, None, ALU.bitwise_and))
                    for b in range(EB):
                        lk(v.tensor_scalar(ob[:, b, :], eb[:], float(b), None, ALU.is_equal), wait=b == EB - 1)
                    for a in range(EA):
                        v.tensor_scalar(oa[:, :, a, :], ea[:].rearrange("p (m g) -> p m g", g=QUAD), float(a), None, ALU.is_equal)
                    v.tensor_tensor(wob[0][:], ob[:], wh[:].unsqueeze(1).to_broadcast([KR, EB, KT * GT]), ALU.mult)
                    v.tensor_tensor(wob[1][:], ob[:], wl[:].unsqueeze(1).to_broadcast([KR, EB, KT * GT]), ALU.mult).then_inc(S_["oh"], 1)

                HALF_G = P // QUAD // 2

                def products(g):
                    dve.wait_ge(S_["gelu"], QUAD * (4 * g + 4) + 2 * QUAD)
                    for q in range(2 * G):
                        t, n = q // 2, q % 2
                        dve.wait_ge(S_["sct"], 2 * G * g + q + 1)
                        at = t * (P // QUAD) + n * HALF_G
                        v.scalar_tensor_tensor(hh[:, t, :, n * (P // 2):(n + 1) * (P // 2)],
                                               ps_b[q % 3][:].rearrange("p (b n) -> p b n", b=EB), 1.0 / WSCALE,
                                               k.acts[:, :, at:at + HALF_G].rearrange("p b m g -> p b (m g)"),
                                               ALU.mult, ALU.mult).then_inc(S_["prod"], 1)

                def results(g):
                    for t in range(G):
                        dve.wait_ge(S_["fin"], G * g + t + 1)
                        dve.wait_ge(in_x1[t], 16 * (g + 1))
                        v.tensor_tensor(x1[:, t, :], ps_b[1 + t][:, 0:D], x1[:, t, :], ALU.add).then_inc(S_["resd"], 1)

                def start(g):
                    factors(g)
                    topk(g)

                v.nop().then_inc(S_["resd"], G)
                v.nop().then_inc(S_["facs"], 1)
                v.nop().then_inc(S_["z_free"], H)
                dve.wait_ge(in_mg, 16)
                v.tensor_copy(mg16[:], mg[:]).then_inc(S_["mgd"], 1)
                start(0)
                select(0)
                masks(0)
                with dve.Fori(0, NGRP - 1) as g:
                    start(g + 1)
                    onehots(g)
                    select(g + 1)
                    products(g)
                    masks(g + 1)
                    results(g)
                onehots(NGRP - 1)
                products(NGRP - 1)
                results(NGRP - 1)

            @block.gpsimd
            def _(pool):
                g_ = nc.gpsimd

                def turn(g):
                    lk = chain(pool, S_["pool"], 2, g)
                    hold(pool, S_["top"], g + 1)
                    lk(g_.tensor_copy(ixf[:], idx[:]), wait=False)
                    lk(g_.tensor_tensor(sc[:], top[:], bc(fac[:], TOP), ALU.mult))
                    for dst, src in ((ecand, ixf), (cand, sc)):
                        last = None
                        i = 0
                        while i < TOP:
                            m = ROWS[i]
                            n = sum(1 for r in ROWS if r == m)
                            o = dst[:, :, AT[i]:AT[i] + n * m].rearrange("p u (n m) -> p u n m", m=m)
                            last = g_.tensor_tensor(o, src[:, :, 0, i:i + n].unsqueeze(3).to_broadcast([P, U, n, m]),
                                                    src[:, :, 1, 0:m].unsqueeze(2).to_broadcast([P, U, n, m]), ALU.add)
                            i += n
                        last.then_inc(S_["sums"], 1)
                    pool.wait_ge(S_["sel"], 4 * U * (g + 1))
                    mx = best[:, :, 0]
                    g_.tensor_tensor(be[:], best[:], bc(mx, TOP), ALU.subtract).then_inc(S_["arg"], 1)
                    g_.tensor_tensor(wgt[:], cand[:], bc(mx, PAIRS), ALU.subtract).then_inc(S_["arg"], 1)
                    pool.wait_ge(S_["expd"], 2 * (g + 1))
                    pool.wait_ge(S_["mstep"], 3 * (g + 1))
                    g_.tensor_tensor(wgt[:], wgt[:], bc(zsum[:], PAIRS), ALU.mult).then_inc(S_["wgtd"], 1)
                with pool.Fori(0, NGRP) as g:
                    turn(g)


def program(nc, x, adj, w, wb, a, wq, bq, ln_g, ln_b, keys0, keys1, down, up, identity, centre, own, merge, out):
    with ExitStack() as ctx:
        scratch_u = nc.dram_tensor("scratch_u", [2, H, HN], FP32, kind="Internal").ap()
        scratch_x = nc.dram_tensor("scratch_x", [PASSES, P, T * XC], FP16, kind="Internal").ap()
        scratch_xd = nc.dram_tensor("scratch_xd", [P, T * H * 2 * HA], FP16, kind="Internal").ap()
        scratch_x1 = nc.dram_tensor("scratch_x1", [NP, D], FP32, kind="Internal").ap()
        yT = ctx.enter_context(nc.sbuf_tensor("yT", [P, KC, NP], FP32))
        with ExitStack() as gnn:
            sb = lambda n, s, d=FP32: gnn.enter_context(nc.sbuf_tensor(n, s, d))
            keep = Keep()
            keep.adjd = sb("adjd", [P, T, H, HA])
            keep.a = sb("a_all", [P, H, T])
            keep.c = sb("c_all", [P, H, T])
            keep.negv = sb("negv", [P, PASSES, T])
            keep.hsum = sb("hsum", [P, H * HA])
            project(nc, ctx, x, w, wb, a, identity, scratch_u, scratch_x, scratch_xd, keep)
            with ExitStack() as big:
                adjT = big.enter_context(nc.sbuf_tensor("adjT", [P, T, NP // 4], U32))
                keep.col32 = lambda t: adjT[:, :, bass.ds(t * (P // 4), P // 4)]
                keep.adj32 = lambda half, j: adjT[:, j, bass.ds(half * (HN // 4), HN // 4)]
                adjacency(nc, adj, identity, scratch_xd, keep)
                attention(nc, scratch_u.rearrange("a h n -> (a h) n"), scratch_x, keep)
            residual(nc, x, identity, keep, scratch_x1, yT)
        sb = lambda n, s, d=FP32: ctx.enter_context(nc.sbuf_tensor(n, s, d))
        k = Keep()
        k.ident = sb("ident", [P, P])
        k.ident16 = sb("ident16", [P, P], FP16)
        k.wq = sb("wqT", [P, KC, H * QD])
        k.bq = sb("bqc", [P, H])
        k.kg = sb("kg", [P, 2 * KEYS])
        k.kb = sb("kb", [H, H, 2 * KEYS])
        k.rq = sb("rq", [P, 2])
        k.rsq = sb("rsq", [P, 3])
        k.bsq = sb("bsq", [P, 2])
        k.mean8 = sb("mean8", [P, 2 * H])
        k.eps = sb("eps", [P, 1])
        k.own = sb("own", [P, QUAD])
        k.down = sb("downT", [P, KC, EB, EA, QUAD])
        k.up = sb("upb", [P, EB, D])
        k.acts = sb("acts", [P, EB, G * P // QUAD, QUAD])
        router_weights(nc, wq, bq, ln_g, ln_b, (keys0, keys1), down, up, identity, centre, own, k)
        experts(nc, yT, scratch_x1, merge, k, out)


def kernel(**inputs):
    import numpy as _np
    import concourse.bacc as _bacc
    from concourse import mybir as _mybir
    from concourse.bass_utils import run_bass_kernel_spmd as _run

    nc = _bacc.Bacc("TRN2", target_bir_lowering=False, num_devices=1)
    arrays, args = {}, []

    def give(name, array):
        array = _np.ascontiguousarray(array)
        arrays[name] = array
        args.append(nc.dram_tensor(name, array.shape, _mybir.dt.from_np(array.dtype), kind="ExternalInput").ap())
    for name in ("x", "adj", "L0_gnn_W_w", "L0_gnn_W_b", "L0_gnn_a", "L0_ffn_Wq", "L0_ffn_bq", "L0_ffn_ln_g", "L0_ffn_ln_b",
                 "L0_ffn_keys0", "L0_ffn_keys1", "L0_ffn_expert_down", "L0_ffn_expert_up"):
        give(f"in_{name}", inputs[name])
    give("in_identity", _np.eye(P, dtype=_np.float32))
    give("in_centre", _np.eye(P, dtype=_np.float32) - _np.float32(1.0 / P))
    give("in_own", _np.tile(_np.eye(QUAD, dtype=_np.float32), (EA, 1)))
    merge = _np.zeros((2 * PAIRS, 2, KR), _np.float32)
    for c, s in enumerate(slots()):
        for head in range(2):
            for n in range(2):
                merge[head * PAIRS + c, n, (2 * n + head) * SLOTS + s] = 1.0
    give("in_merge", merge)
    args.append(nc.dram_tensor("out_0", (N, D), _mybir.dt.float32, kind="ExternalOutput").ap())
    program(nc, *args)
    r = _run(nc, [arrays], core_ids=[0])
    return r.results[0]["out_0"]
```

```python
import concourse.bass as bass
from concourse import mybir
from contextlib import ExitStack

FP32 = mybir.dt.float32
FP16 = mybir.dt.float16
BF16 = mybir.dt.bfloat16
FP8 = mybir.dt.float8e4
U8 = mybir.dt.uint8
U16 = mybir.dt.uint16
U32 = mybir.dt.uint32
ALU = mybir.AluOpType
ACT = mybir.ActivationFunctionType
AX = mybir.AxisListType

P = 128
N = 3327
T = (N + P - 1) // P
NP = T * P
LAST = N - (T - 1) * P
D = 256
KC = D // P
H = 8
HD = D // H
HA = HD + 1
XC = 4 * HA
HT = T // 2
HN = HT * P
PASSES = 2 * H
SCALE = 1024.0
EPS = 1e-5
BY_DVE = 11
AMASKS, DMASKS = 5, 2
AHEAD = 2
CREDIT = 16


def chain(eng, sem, per=0, turn=0):
    n = [0]

    def link(ins, wait=True):
        n[0] += 1
        ins.then_inc(sem, 1)
        if wait:
            if per:
                hold(eng, sem, turn * per + n[0])
            else:
                eng.wait_ge(sem, n[0])
        return ins
    link.n = n
    return link


def hold(eng, sem, value):
    eng.wait_ge(sem, value)
    eng.nop(nofuse=True)


def bc(ap, n):
    return ap.unsqueeze(len(ap.shape)).to_broadcast(list(ap.shape) + [n])


def project(nc, ctx0, x, w, wb, a, identity, scratch_u, scratch_x, scratch_xd, keep):
    with ExitStack() as ctx:
        sb = lambda n, s, d=FP32: ctx.enter_context(nc.sbuf_tensor(n, s, d))
        pb = lambda n, s, d=FP32: ctx.enter_context(nc.psum_tensor(n, s, d))
        sem = lambda n: ctx.enter_context(nc.semaphore(n))
        xs = sb("p_xs", [P, T, D])
        ident = sb("p_ident", [P, P])
        wn = sb("p_wn", [P, KC, D])
        ablk = sb("p_ablk", [P, KC, 2 * H])
        brow = sb("p_brow", [1, D + 2 * H])
        bcol = sb("p_bcol", [P, KC])
        ones = sb("p_ones", [P, P])
        valid = sb("p_valid", [P, P])
        waug = sb("p_waug", [P, KC, D + 2 * H])
        mv = sb("p_mv", [P, T, 2])
        st = sb("p_st", [P, 2, 6])
        mv2 = sb("p_mv2", [P, 2, 2])
        rstd = sb("p_rstd", [P, T])
        xh = sb("p_xh", [P, 2, D])
        xhT = sb("p_xhT", [P, 2, KC, P])
        haug = sb("p_haug", [P, T, H, HA])
        uv = sb("p_uv", [P, T, 2 * H])
        uvs = sb("p_uvs", [P, 2, 2 * H])
        uvT = sb("p_uvT", [2 * H, NP])
        mx = sb("p_mx", [2 * H, 1])
        dmx = sb("p_dmx", [2 * H, 2 * H])
        mall = sb("p_mall", [P, 2 * H])
        tv = sb("p_tv", [P, T, H])
        t1 = sb("p_t1", [P, T, H])
        bexp = sb("p_bexp", [P, T, H])
        dexp = sb("p_dexp", [P, T, H])
        prod = sb("p_prod", [P, 2, T, HA])
        xd = sb("p_xd", [P, T, H, 2 * HA], FP16)
        xb = sb("p_xb", [P, 2, T, XC], FP16)
        ps_w = [pb(f"p_psw{k}", [P, 512]) for k in range(KC)]
        ps_t = [pb(f"p_pst{k}", [P, 512]) for k in range(2)]
        ps_h = [pb(f"p_psh{k}", [P, 512]) for k in range(2)]
        ps_v = pb("p_psv", [P, 512])
        ps_s = pb("p_pss", [P, 512])
        z_done, in_x, in_w = sem("p_zeroed"), sem("p_in_x"), sem("p_in_w")
        wt_done, waug_done = sem("p_wt"), sem("p_waug")
        dv, var_done, std_done = sem("p_dv"), sem("p_var"), sem("p_std")
        dvl, xh_done, xt_done, xhT_done = sem("p_dvl"), sem("p_xh"), sem("p_xt"), sem("p_xhT")
        mm_done, h_out, uv_out, vt_done, vt_out = sem("p_mm"), sem("p_hout"), sem("p_uvout"), sem("p_vt"), sem("p_vtout")
        dm_done, m_bc, m_out = sem("p_dm"), sem("p_mbc"), sem("p_mout")
        arg_done, exp_done, po, xb_done, u_st, x_st = (sem("p_arg"), sem("p_exp"), sem("p_po"), sem("p_xb"),
                                                       sem("p_ust"), [sem("p_xst0"), sem("p_xst1")])
        hs_done, nv_done, act_done, po_done = sem("p_hs"), sem("p_nv"), sem("p_actd"), sem("p_pod")
        NW = 5 + 2 * H

        with nc.Block() as block:
            @block.sync
            def _(sp):
                sp.dma_start(wn[:], w.rearrange("(c p) d -> p c d", p=P)).then_inc(in_w, 16)
                sp.dma_start(ident[:], identity).then_inc(in_w, 16)
                sp.dma_start(brow[0:1, 0:D], wb.unsqueeze(0)).then_inc(in_w, 16)
                sp.dma_start(bcol[:], wb.rearrange("(c p) -> p c", p=P), allow_slow_non_contiguous=True).then_inc(in_w, 16)
                sp.wait_ge(z_done, 4)
                sp.dma_start(xs[:, 0:T - 1, :], x[0:(T - 1) * P, :].rearrange("(t p) d -> p t d", p=P)).then_inc(in_x, 16)
                sp.dma_start(xs[0:LAST, T - 1, :], x[(T - 1) * P:N, :]).then_inc(in_x, 16)
                for h in range(H):
                    for s in range(2):
                        q = HD * (h % 4)
                        sp.dma_start(ablk[q:q + HD, h // 4, s * H + h:s * H + h + 1],
                                     a[s * HD:(s + 1) * HD, :]).then_inc(in_w, 16)
                sp.wait_ge(vt_out, T)
                for half in range(2):
                    sp.dma_start(scratch_u[half], uvT[0:H, half * HN:(half + 1) * HN]).then_inc(u_st, 16)
                for h in range(H):
                    sp.wait_ge(xb_done, h + 1)
                    for half in range(2):
                        sp.dma_start(scratch_x[half * H + h], xb[:, h % 2].rearrange("p t c -> p (t c)")).then_inc(x_st[h % 2], 16)
                sp.dma_start(scratch_xd, xd[:].rearrange("p t h c -> p (t h c)")).then_inc(u_st, 16)
                sp.wait_ge(u_st, 48)
                for s in range(2):
                    sp.wait_ge(x_st[s], 32 * (H // 2))

            @block.vector
            def _(dve):
                v = nc.vector
                v.memset(xs[:, T - 1, :], 0.0).then_inc(z_done, 1)
                v.memset(ablk[:], 0.0).then_inc(z_done, 1)
                v.memset(ones[:], 1.0).then_inc(z_done, 1)
                v.memset(haug[:], 1.0).then_inc(z_done, 1)
                for k in range(KC):
                    dve.wait_ge(wt_done, k + 1)
                    v.tensor_copy(waug[:, k, :], ps_w[k][:, 0:D + 2 * H]).then_inc(waug_done, 1)
                dve.wait_ge(wt_done, 3)
                v.tensor_copy(brow[0:1, D:], ps_v[0:1, 0:2 * H]).then_inc(waug_done, 1)
                dve.wait_ge(in_x, 32)
                link = chain(dve, dv)
                with dve.Fori(0, HT) as i:
                    lk = chain(dve, dvl, 5, i)
                    for s in range(2):
                        lk(v.bn_stats(st[:, s, :], xs[:, bass.ds(2 * i + s, 1), :].rearrange("p a d -> p (a d)")), wait=s == 1)
                    for s in range(2):
                        lk(v.bn_aggr(mv2[:, s, :], st[:, s, :]), wait=s == 1)
                    lk(v.tensor_copy(mv[:, bass.ds(2 * i, 2), :], mv2[:]))
                link(v.tensor_scalar(rstd[:], mv[:, :, 1], EPS, None, ALU.add), wait=False)
                dve.wait_ge(std_done, 1)
                link(v.reciprocal(rstd[:], rstd[:]))
                with dve.Fori(0, HT) as i:
                    for s in range(2):
                        t = 2 * i + s
                        dve.wait_ge(xt_done, t + 1)
                        v.tensor_scalar(xh[:, s, :], xs[:, bass.ds(t, 1), :].rearrange("p a d -> p (a d)"),
                                        mv[:, bass.ds(t, 1), 0], rstd[:, bass.ds(t, 1)],
                                        ALU.subtract, ALU.mult).then_inc(xh_done, 1)
                dve.wait_ge(vt_out, T)
                link(v.reduce_max(mx[:], uvT[:, 0:N], AX.X))
                v.tensor_scalar(dmx[:], ident[0:2 * H, 0:2 * H], mx[:, 0:1], None, ALU.mult).then_inc(dm_done, 1)
                dve.wait_ge(m_bc, 1)
                link(v.tensor_copy(mall[:], ps_s[:, 0:2 * H]))
                mb = mall[:, H:2 * H].unsqueeze(1).to_broadcast([P, T, H])
                link(v.tensor_tensor(tv[:], uv[:, :, 0:H], mb, ALU.add), wait=False)
                link(v.tensor_tensor(bexp[:], uv[:, :, H:2 * H], mb, ALU.subtract))
                v.tensor_scalar(t1[:], tv[:], 0.8, 0.0, ALU.mult, ALU.min).then_inc(arg_done, 1)
                v.tensor_scalar(tv[:], tv[:], -0.8, 0.0, ALU.mult, ALU.min).then_inc(arg_done, 1)
                v.tensor_scalar(bexp[:], bexp[:], 0.0, None, ALU.min).then_inc(arg_done, 1)
                for half in range(2):
                    v.tensor_scalar(keep.negv[:, half * H:(half + 1) * H, :],
                                    uv[:, :, H:2 * H].rearrange("p t h -> p h t"), -1.0, None, ALU.mult).then_inc(nv_done, 1)
                dve.wait_ge(exp_done, 4)
                link(v.tensor_scalar(bexp[:], bexp[:], SCALE, None, ALU.mult), wait=False)
                link(v.tensor_scalar(dexp[:], dexp[:], SCALE, None, ALU.mult))
                for h in range(H):
                    if h >= 2:
                        dve.wait_ge(x_st[h % 2], 32 * (h // 2))
                    for n, e in enumerate((bexp, dexp)):
                        link(v.tensor_tensor(prod[:, n], haug[:, :, h, :], bc(e[:, :, h], HA), ALU.mult), wait=n == 1)
                    for n in range(2):
                        link(v.tensor_copy(xb[:, h % 2, :, 2 * n * HA:(2 * n + 1) * HA], prod[:, n]), wait=n == 1)
                    for n in range(2):
                        c = 2 * n * HA
                        link(v.tensor_tensor(xb[:, h % 2, :, c + HA:c + 2 * HA], prod[:, n], xb[:, h % 2, :, c:c + HA],
                                             ALU.subtract), wait=n == 1)
                    v.tensor_copy(xd[:, :, h, :], xb[:, h % 2, :, 2 * HA:4 * HA]).then_inc(xb_done, 1)
                dve.wait_ge(hs_done, 1)
                v.tensor_copy(keep.hsum[:], ps_s[:, 0:H * HA]).then_inc(nv_done, 1)

            @block.scalar
            def _(act):
                s_ = nc.scalar
                act.wait_ge(z_done, 4)
                act.wait_ge(dv, 1)
                s_.activation(rstd[:], rstd[:], ACT.Sqrt).then_inc(std_done, 1)
                with act.Fori(0, HT) as i:
                    for s in range(2):
                        t = 2 * i + s
                        act.wait_ge(xt_done, t + 3)
                        act.wait_ge(mm_done, t + 1)
                        s_.activation(xhT[:, s], ps_t[s][:, 0:D].rearrange("p (c n) -> p c n", c=KC), ACT.Copy).then_inc(xhT_done, 1)
                        act.wait_ge(mm_done, t + 3)
                        s_.activation(haug[:, bass.ds(t, 1), :, 0:HD].rearrange("p a h d -> p (a h) d"),
                                      ps_h[s][:, 0:D].rearrange("p (h d) -> p h d", h=H), ACT.Copy).then_inc(h_out, 1)
                        s_.activation(uv[:, bass.ds(t, 1), :].rearrange("p a c -> p (a c)"), ps_h[s][:, D:D + 2 * H], ACT.Copy)
                        s_.activation(uvs[:, s, :], ps_h[s][:, D:D + 2 * H], ACT.Copy).then_inc(uv_out, 1)
                        act.wait_ge(vt_done, t + 1)
                        s_.activation(uvT[:, bass.ds(t * P, P)], ps_v[0:2 * H, 0:P], ACT.Copy).then_inc(vt_out, 1)
                act.wait_ge(arg_done, 3)
                s_.activation(keep.a[:].rearrange("p h t -> p t h"), t1[:], ACT.Exp).then_inc(exp_done, 1)
                s_.activation(keep.c[:].rearrange("p h t -> p t h"), tv[:], ACT.Exp).then_inc(exp_done, 1)
                s_.activation(dexp[:], bexp[:], ACT.Exp, scale=0.2).then_inc(exp_done, 1)
                act.wait_ge(exp_done, 3)
                s_.activation(bexp[:], bexp[:], ACT.Exp).then_inc(exp_done, 1)

            @block.tensor
            def _(pe):
                t_ = nc.tensor
                pe.wait_ge(in_w, 16 * (4 + 2 * H))
                pe.wait_ge(z_done, 4)
                for k in range(KC):
                    for c in range(KC):
                        t_.transpose(ps_w[k][:, c * P:(c + 1) * P], wn[:, c, k * P:(k + 1) * P], ident[:])
                    for c in range(KC):
                        last = t_.matmul(ps_w[k][:, D:D + 2 * H], wn[:, c, k * P:(k + 1) * P], ablk[:, c, :],
                                         start=c == 0, stop=c == KC - 1)
                    last.then_inc(wt_done, 1)
                for c in range(KC):
                    last = t_.matmul(ps_v[0:1, 0:2 * H], bcol[:, c:c + 1], ablk[:, c, :], start=c == 0, stop=c == KC - 1)
                last.then_inc(wt_done, 1)
                pe.wait_ge(waug_done, KC + 1)
                pe.nop().then_inc(xt_done, 2)
                pe.nop().then_inc(mm_done, 2)
                with pe.Fori(0, HT) as i:
                    for s in range(2):
                        t = 2 * i + s
                        pe.wait_ge(xh_done, t + 1)
                        for k in range(KC):
                            last = t_.transpose(ps_t[s][:, k * P:(k + 1) * P], xh[:, s, k * P:(k + 1) * P], ident[:])
                        last.then_inc(xt_done, 1)
                        pe.wait_ge(xhT_done, t + 1)
                        for k in range(KC):
                            t_.matmul(ps_h[s][:, 0:D + 2 * H], xhT[:, s, k, :], waug[:, k, :], start=k == 0, stop=False)
                        t_.matmul(ps_h[s][:, 0:D + 2 * H], ones[0:1, :], brow[0:1, :], start=False, stop=True).then_inc(mm_done, 1)
                        pe.wait_ge(uv_out, t + 1)
                        t_.transpose(ps_v[0:2 * H, 0:P], uvs[:, s, :], ident[:]).then_inc(vt_done, 1)
                pe.wait_ge(dm_done, 1)
                t_.matmul(ps_s[:, 0:2 * H], ones[0:2 * H, :], dmx[:], start=True, stop=True).then_inc(m_bc, 1)
                pe.wait_ge(h_out, T)
                pe.wait_ge(dv, 4)
                for t in range(T):
                    rows = LAST if t == T - 1 else P
                    last = t_.matmul(ps_s[:, 0:H * HA], ones[0:rows, :], haug[0:rows, t].rearrange("p h d -> p (h d)"),
                                     start=t == 0, stop=t == T - 1)
                last.then_inc(hs_done, 1)


def adjacency(nc, adj, identity, scratch_xd, keep):
    with ExitStack() as ctx:
        sb = lambda n, s, d=FP32: ctx.enter_context(nc.sbuf_tensor(n, s, d))
        pb = lambda n, s, d=FP32: ctx.enter_context(nc.psum_tensor(n, s, d))
        sem = lambda n: ctx.enter_context(nc.semaphore(n))
        ident32 = sb("a_id32", [P, P])
        ident = sb("a_ident", [P, P], BF16)
        xd = sb("a_xd", [P, T, H, 2 * HA], FP16)
        in_xd = sem("a_inxd")
        stage = [sb(f"a_stage{s}", [P, NP], BF16) for s in range(2)]
        col = [sb(f"a_col{s}", [P, T, P], U8) for s in range(2)]
        raw = [sb(f"a_raw{s}", [P, H, 2, HA]) for s in range(2)]
        GRP = 8
        groups = [(g, min(GRP, T - g)) for g in range(0, T, GRP)]
        NG = len(groups)
        ps_t = [pb(f"a_pst{k}", [P, GRP * P], BF16) for k in range(NG)]
        ps_d = [[pb(f"a_psd{s}{k}", [P, 512]) for k in range(2)] for s in range(2)]
        zeroed, in_id, id_done = sem("a_zero"), sem("a_inid"), sem("a_id")
        in_adj = [sem("a_in0"), sem("a_in1")]
        tr, tr_out, copied, mm, raw_done, add_done, stage_free = (sem("a_tr"), sem("a_trout"), sem("a_copied"), sem("a_mm"),
                                                                sem("a_raw"), sem("a_add"), sem("a_sfree"))

        with nc.Block() as block:
            @block.sync
            def _(sp):
                sp.dma_start(ident32[:], identity).then_inc(in_id, 16)
                sp.dma_start(xd[:].rearrange("p t h c -> p (t h c)"), scratch_xd).then_inc(in_xd, 16)

            @block.gpsimd
            def _(pool):
                g = nc.gpsimd
                for s in range(2):
                    g.memset(stage[s][:, N:NP], 0.0).then_inc(zeroed, 1)

                def load(t, s, rows=P):
                    g.dma_start(stage[s][0:rows, 0:N], adj[bass.ds(t * P, rows), :]).then_inc(in_adj[s], 16)

                def turn(t, s, rows=P):
                    pool.wait_ge(tr, NG * (t + 1))
                    load(t + 2, s, rows)
                    collect(t, s)

                def collect(t, s):
                    pool.wait_ge(tr_out, NG * (t + 1))
                    g.tensor_copy(keep.col32(t), col[s][:].bitcast(U32)).then_inc(copied, 1)
                    pool.wait_ge(raw_done, t + 1)
                    g.tensor_tensor(keep.adjd[:, bass.ds(t, 1)].rearrange("p a h d -> p (a h) d"), raw[s][:, :, 0, :],
                                    raw[s][:, :, 1, :], ALU.add).then_inc(add_done, 1)
                pool.wait_ge(zeroed, 2)
                load(0, 0)
                load(1, 1)
                with pool.Fori(0, HT - 2) as i:
                    for s in range(2):
                        turn(2 * i + s, s)
                turn(T - 4, 0)
                turn(T - 3, 1, LAST)
                collect(T - 2, 0)
                collect(T - 1, 1)

            @block.vector
            def _(dve):
                v = nc.vector
                dve.wait_ge(in_id, 16)
                v.tensor_copy(ident[:], ident32[:]).then_inc(id_done, 1)
                v.nop().then_inc(copied, 2)
                with dve.Fori(0, HT) as i:
                    for s in range(2):
                        t = 2 * i + s
                        dve.wait_ge(copied, t + 1)
                        dve.wait_ge(mm, t + 1)
                        for n, (g0, w) in enumerate(groups):
                            dve.wait_ge(tr, NG * t + n + 1)
                            v.tensor_scalar(col[s][:, g0:g0 + w, :].rearrange("p a b -> p (a b)"), ps_t[n][:, 0:w * P],
                                            0.0, 64.0, ALU.not_equal, ALU.mult).then_inc(tr_out, 1)

            @block.scalar
            def _(act):
                s_ = nc.scalar
                act.nop().then_inc(add_done, 2)
                with act.Fori(0, HT) as i:
                    for s in range(2):
                        t = 2 * i + s
                        act.wait_ge(mm, t + 3)
                        act.wait_ge(add_done, t + 1)
                        for k in range(2):
                            ins = s_.activation(raw[s][:, 4 * k:4 * k + 4].rearrange("p h a d -> p (h a d)"),
                                                ps_d[s][k][:, 0:8 * HA], ACT.Copy)
                        ins.then_inc(raw_done, 1)

            @block.tensor
            def _(pe):
                t_ = nc.tensor
                pe.nop().then_inc(mm, 2)
                pe.wait_ge(id_done, 1)

                def transposes(t, s, loads):
                    pe.wait_ge(in_adj[s], 16 * loads)
                    pe.wait_ge(zeroed, 2)
                    for n, (g0, w) in enumerate(groups):
                        if not (isinstance(t, int) and t == 0):
                            pe.wait_ge(tr_out, NG * (t - 1) + n + 1)
                        for k in range(w):
                            last = t_.transpose(ps_t[n][:, k * P:(k + 1) * P], stage[s][:, (g0 + k) * P:(g0 + k + 1) * P], ident[:])
                        last.then_inc(tr, 1)

                def products(t, s):
                    hold(pe, tr_out, NG * (t + 1))
                    for j in range(T):
                        for k in range(2):
                            last = t_.matmul(ps_d[s][k][:, 0:8 * HA], col[s][:, j, :].bitcast(FP8),
                                             xd[:, j, 4 * k:4 * k + 4, :].rearrange("p h c -> p (h c)"),
                                             start=j == 0, stop=j == T - 1)
                    last.then_inc(mm, 1)
                transposes(0, 0, 1)
                pe.wait_ge(in_xd, 16)
                with pe.Fori(0, HT - 1) as i:
                    transposes(2 * i + 1, 1, i + 1)
                    pe.wait_ge(add_done, 2 * i + 1)
                    products(2 * i, 0)
                    transposes(2 * i + 2, 0, i + 2)
                    pe.wait_ge(add_done, 2 * i + 2)
                    products(2 * i + 1, 1)
                transposes(T - 1, 1, HT)
                pe.wait_ge(add_done, T - 1)
                products(T - 2, 0)
                pe.wait_ge(add_done, T)
                products(T - 1, 1)


def attention(nc, scratch_u, scratch_x, keep):
    with ExitStack() as ctx:
        sb = lambda n, s, d=FP32: ctx.enter_context(nc.sbuf_tensor(n, s, d))
        pb = lambda n, s, d=FP32: ctx.enter_context(nc.psum_tensor(n, s, d))
        sem = lambda n: ctx.enter_context(nc.semaphore(n))
        PER = 3
        NB = (HT + PER - 1) // PER
        ub = [sb(f"g_u{s}", [P, HN]) for s in range(2)]
        nv = [sb(f"g_nv{s}", [P, T]) for s in range(2)]
        xo = [sb(f"g_x{s}", [P, T, XC], FP16) for s in range(2)]
        mask = {True: [sb(f"g_amask{k}", [P, HN], FP8) for k in range(AMASKS)],
                False: [sb(f"g_dmask{k}", [P, HN], FP8) for k in range(DMASKS)]}
        raw = sb("g_raw", [P, HT, XC])
        comb = sb("g_comb", [P, HT, 2, HA])
        acc = pb("g_acc", [P, NB, 512])
        loaded = [sem("g_in0"), sem("g_in1")]
        signs, made, ready, free, evac, summed, pl = (sem("g_signs"), sem("g_made"), sem("g_ready"), sem("g_free"), sem("g_evac"),
                                                      sem("g_summed"), sem("g_pl"))

        by_act = [not (j + 1) * BY_DVE // T > j * BY_DVE // T for j in range(T)] * 2
        assert 2 * (T - BY_DVE) % AMASKS == 0 and 2 * BY_DVE % DMASKS == 0
        order = [sum(1 for m in range(n) if by_act[m] == by_act[n]) for n in range(2 * T)]
        buf = [mask[by_act[n]][order[n] % (AMASKS if by_act[n] else DMASKS)] for n in range(2 * T)]
        before = [max(m for m in range(-2 * T, n) if buf[m % (2 * T)] is buf[n]) for n in range(2 * T)]
        assert min(before) >= -CREDIT

        with nc.Block() as block:
            @block.sync
            def _(sp):
                def load(p, s):
                    sp.dma_start(ub[s][:], scratch_u[bass.ds(p, 1), :].partition_broadcast(P) if not isinstance(p, int)
                                 else scratch_u[p:p + 1, :].partition_broadcast(P)).then_inc(loaded[s], 16)
                    sp.dma_start(xo[s][:].rearrange("p t c -> p (t c)"), scratch_x[bass.ds(p, 1)].rearrange("a p n -> p (a n)")).then_inc(loaded[s], 16)
                    sp.dma_start(nv[s][:], keep.negv[:, bass.ds(p, 1), :].rearrange("p a t -> p (a t)")).then_inc(loaded[s], 16)
                load(0, 0)
                load(1, 1)
                with sp.Fori(0, PASSES // 2 - 1) as r:
                    for s in range(2):
                        sp.wait_ge(free, CREDIT + T * (2 * r + s + 1))
                        load(2 * r + s + 2, s)

            @block.scalar
            def _(act):
                s_ = nc.scalar
                full = (NB - 1) * PER

                def masks(r, s, columns):
                    for j in columns:
                        n = s * T + j
                        if j == 0:
                            act.wait_ge(loaded[s], 48 * (r + 1))
                        if by_act[n]:
                            hold(act, free, 2 * T * r + before[n] + 1 + CREDIT)
                            s_.activation(buf[n][:], ub[s][:], ACT.Sign, bias=nv[s][:, j:j + 1], scale=-1.0, saturate=False).then_inc(signs, 1)

                def copy_out(p):
                    act.wait_ge(free, CREDIT + T * (p + 1))
                    act.wait_ge(summed, p + 1)
                    s_.activation(raw[:, 0:full, :].rearrange("p (b t) c -> p b (t c)", t=PER),
                                  acc[:, 0:NB - 1, 0:PER * XC], ACT.Copy).then_inc(evac, 1)
                    s_.activation(raw[:, full:HT, :].rearrange("p t c -> p (t c)"),
                                  acc[:, NB - 1, 0:(HT - full) * XC], ACT.Copy).then_inc(evac, 1)

                masks(0, 0, range(AHEAD))

                def turn(r, more=True):
                    masks(r, 0, range(AHEAD, T))
                    masks(r, 1, range(AHEAD))
                    copy_out(2 * r)
                    masks(r, 1, range(AHEAD, T))
                    if more:
                        masks(r + 1, 0, range(AHEAD))
                    copy_out(2 * r + 1)
                with act.Fori(0, PASSES // 2 - 1) as r:
                    turn(r)
                turn(PASSES // 2 - 1, False)

            @block.vector
            def _(dve):
                v = nc.vector
                A2, D2 = 2 * (T - BY_DVE), 2 * BY_DVE
                with dve.Fori(0, 2) as half:
                    with dve.Fori(0, H // 2) as q:
                        def make(n):
                            s, j = n // T, n % T
                            hold(dve, free, (H * T) * half + (2 * T) * q + before[n] + 1 + CREDIT)
                            v.tensor_scalar(buf[n][:], ub[s][:], nv[s][:, j:j + 1], 2.0, ALU.is_gt, ALU.mult, saturate=False).then_inc(made, 1)

                        for n in range(2 * T):
                            s, j = n // T, n % T
                            if j == 0:
                                dve.wait_ge(loaded[s], 16 * 3 * (H // 2) * half + 48 * q + 48)
                            if j + 1 < T and not by_act[n + 1]:
                                make(n + 1)
                            bits, edges = buf[n][:].bitcast(U32), keep.adj32(half, j)
                            if by_act[n]:
                                dve.wait_ge(signs, (A2 * (H // 2)) * half + A2 * q + order[n] + 1)
                                v.scalar_tensor_tensor(bits, bits, 1, edges, ALU.logical_shift_right, ALU.bitwise_and).then_inc(ready, 1)
                            else:
                                dve.wait_ge(made, (D2 * (H // 2)) * half + D2 * q + order[n] + 1)
                                v.tensor_tensor(bits, bits, edges, ALU.bitwise_and).then_inc(ready, 1)

            @block.tensor
            def _(pe):
                t_ = nc.tensor
                pe.nop().then_inc(free, CREDIT)
                pe.nop().then_inc(evac, 2)
                with pe.Fori(0, PASSES // 2) as r:
                    for n in range(2 * T):
                        s, j = n // T, n % T
                        if j == 0:
                            pe.wait_ge(loaded[s], 48 * (r + 1))
                            pe.wait_ge(evac, 2 * (2 * r + s) + 2)
                        hold(pe, ready, 2 * T * r + n + 1)
                        for it in range(HT):
                            b, c = it // PER, it % PER
                            last = t_.matmul(acc[:, b, c * XC:(c + 1) * XC], buf[n][:, it * P:(it + 1) * P],
                                             xo[s][:, j, :], start=(j == 0 and c == 0), stop=j == T - 1, skip_group_check=True)
                        last.then_inc(free, 1)

            @block.gpsimd
            def _(pool):
                g = nc.gpsimd
                g.nop().then_inc(summed, 1)
                with pool.Fori(0, 2) as half:
                    with pool.Fori(0, H) as h:
                        p = H * half + h
                        rr = raw[:].rearrange("p t (k a d) -> p t k a d", k=2, a=2)
                        at = keep.adjd[:, bass.ds(half * HT, HT), bass.ds(h, 1), :].rearrange("p t a d -> p t (a d)")
                        link = chain(pool, pl, 6, p)
                        pool.wait_ge(evac, 2 * p + 4)
                        link(g.tensor_tensor(comb[:, :, 0], rr[:, :, 0, 0], rr[:, :, 0, 1], ALU.add), wait=False)
                        link(g.tensor_tensor(comb[:, :, 1], rr[:, :, 1, 0], rr[:, :, 1, 1], ALU.add))
                        g.nop().then_inc(summed, 1)
                        link(g.tensor_tensor(comb[:, :, 1], at, comb[:, :, 1], ALU.subtract))
                        ah = keep.a[:, bass.ds(h, 1), bass.ds(half * HT, HT)].rearrange("p a t -> p (a t)")
                        ch = keep.c[:, bass.ds(h, 1), bass.ds(half * HT, HT)].rearrange("p a t -> p (a t)")
                        link(g.tensor_tensor(comb[:, :, 0], comb[:, :, 0], bc(ah, HA), ALU.mult), wait=False)
                        link(g.tensor_tensor(comb[:, :, 1], comb[:, :, 1], bc(ch, HA), ALU.mult))
                        link(g.tensor_tensor(at, comb[:, :, 0], comb[:, :, 1], ALU.add))


def residual(nc, x, identity, keep, scratch_x1, yT):
    with ExitStack() as ctx:
        sb = lambda n, s, d=FP32: ctx.enter_context(nc.sbuf_tensor(n, s, d))
        pb = lambda n, s, d=FP32: ctx.enter_context(nc.psum_tensor(n, s, d))
        sem = lambda n: ctx.enter_context(nc.semaphore(n))
        B = 2
        NB = T // B
        PARTS = 4
        cut = [NB * n // PARTS * B for n in range(PARTS)] + [T]
        ident = sb("r_ident", [P, P])
        xs = sb("r_xs", [P, T, D])
        flag = sb("r_flag", [P, T, H])
        fall = sb("r_fall", [P, B, H, HA])
        rec = sb("r_rec", [P, T, H])
        hv = sb("r_hv", [P, T, D])
        ng = sb("r_ng", [P, T, D])
        st = sb("r_st", [P, B, 6])
        mv1 = sb("r_mv1", [P, B, 2])
        mv = sb("r_mv", [P, T, 2])
        rstd = sb("r_rstd", [P, T])
        SL = 4
        y = [sb(f"r_y{s}", [P, D]) for s in range(SL)]
        ps = [pb(f"r_ps{s}", [P, 512]) for s in range(SL)]
        in_id, zeroed, stored = sem("r_inid"), sem("r_z"), sem("r_stored")
        in_x = [sem(f"r_inx{n}") for n in range(PARTS)]
        fl, num, div, added, neg, ex, x1_done, stats, scales, std, y_done, tr, high, low = (
            sem("r_fl"), sem("r_num"), sem("r_div"), sem("r_added"), sem("r_neg"), sem("r_ex"), sem("r_x1"), sem("r_stats"), sem("r_scales"),
            sem("r_std"), sem("r_y"), sem("r_tr"), sem("r_high"), sem("r_low"))
        with nc.Block() as block:
            @block.sync
            def _(sp):
                for n in range(PARTS):
                    if n == PARTS - 1:
                        sp.wait_ge(zeroed, 1)
                        sp.dma_start(xs[:, cut[n]:T - 1, :], x[cut[n] * P:(T - 1) * P, :].rearrange("(t p) d -> p t d", p=P)).then_inc(in_x[n], 16)
                        sp.dma_start(xs[0:LAST, T - 1, :], x[(T - 1) * P:N, :]).then_inc(in_x[n], 16)
                    else:
                        sp.dma_start(xs[:, cut[n]:cut[n + 1], :], x[cut[n] * P:cut[n + 1] * P, :].rearrange("(t p) d -> p t d", p=P)).then_inc(in_x[n], 16)
                sp.dma_start(ident[:], identity).then_inc(in_id, 16)
                for n in range(PARTS):
                    sp.wait_ge(x1_done, cut[n + 1] // B)
                    sp.dma_start(scratch_x1[cut[n] * P:cut[n + 1] * P, :].rearrange("(t p) d -> p t d", p=P), xs[:, cut[n]:cut[n + 1], :]).then_inc(stored, 16)
                sp.wait_ge(stored, 16 * PARTS)

            @block.gpsimd
            def _(pool):
                g = nc.gpsimd
                g.tensor_scalar(flag[:], keep.adjd[:, :, :, HD], 0.0, None, ALU.is_equal).then_inc(fl, 1)
                pool.wait_ge(fl, 1)
                hsum = keep.hsum[:].rearrange("p (h d) -> p h d", h=H).unsqueeze(1).to_broadcast([P, B, H, HA])
                with pool.Fori(0, NB) as b:
                    row = keep.adjd[:, bass.ds(B * b, B)]
                    g.tensor_tensor(fall[:], hsum, bc(flag[:, bass.ds(B * b, B), :], HA), ALU.mult).then_inc(fl, 1)
                    hold(pool, fl, b + 2)
                    g.tensor_tensor(row, row, fall[:], ALU.add).then_inc(num, 1)
                    hold(pool, num, b + 1)

            @block.vector
            def _(dve):
                v = nc.vector
                v.memset(xs[:, T - 1, :], 0.0).then_inc(zeroed, 1)

                def quotient(b):
                    row = keep.adjd[:, bass.ds(B * b, B)].rearrange("p b h d -> p (b h) d")
                    at = bass.ds(B * b, B)
                    dve.wait_ge(num, b + 1)
                    r = rec[:, at, :].rearrange("p b h -> p (b h)")
                    v.reciprocal(r, row[:, :, HD]).then_inc(div, 1)
                    dve.wait_ge(div, 2 * b + 1)
                    h = hv[:, at, :].rearrange("p b d -> p (b d)")
                    v.tensor_tensor(h.rearrange("p (u d) -> p u d", d=HD), row[:, :, 0:HD], bc(r, HD), ALU.mult).then_inc(div, 1)
                    dve.wait_ge(div, 2 * b + 2)
                    v.tensor_scalar(ng[:, at, :].rearrange("p b d -> p (b d)"), h, 0.0, None, ALU.min).then_inc(neg, 1)

                def add(b):
                    at = bass.ds(B * b, B)
                    xt, h, e = (t[:, at, :].rearrange("p b d -> p (b d)") for t in (xs, hv, ng))
                    v.scalar_tensor_tensor(xt, h, 0.0, xt, ALU.max, ALU.add).then_inc(added, 1)
                    dve.wait_ge(ex, b + 1)
                    dve.wait_ge(added, b + 1)
                    v.scalar_tensor_tensor(xt, e, -1.0, xt, ALU.add, ALU.add).then_inc(x1_done, 1)

                def moments(b):
                    hold(dve, x1_done, b + 1)
                    for n in range(B):
                        v.bn_stats(st[:, n, :], xs[:, bass.ds(B * b + n, 1), :].rearrange("p a d -> p (a d)")).then_inc(stats, 1)
                    for n in range(B):
                        hold(dve, stats, (2 * B + 1) * b + B)
                        v.bn_aggr(mv1[:, n, :], st[:, n, :]).then_inc(stats, 1)
                    hold(dve, stats, (2 * B + 1) * b + 2 * B)
                    v.tensor_copy(mv[:, bass.ds(B * b, B), :], mv1[:]).then_inc(stats, 1)
                    hold(dve, stats, (2 * B + 1) * b + 2 * B + 1)

                quotient(0)
                for n in range(PARTS):
                    dve.wait_ge(in_x[n], 32 if n == PARTS - 1 else 16)
                    lo, hi = cut[n] // B, min(cut[n + 1] // B, NB - 1)
                    with dve.Fori(lo, hi) as b:
                        quotient(b + 1)
                        add(b)
                        moments(b)
                add(NB - 1)
                moments(NB - 1)
                v.tensor_scalar(rstd[:], mv[:, :, 1], EPS, None, ALU.add).then_inc(scales, 1)
                dve.wait_ge(std, 1)
                v.reciprocal(rstd[:], rstd[:]).then_inc(scales, 1)
                dve.wait_ge(scales, 2)

                def normal(t, s):
                    dve.wait_ge(tr, t + 1)
                    v.tensor_scalar(y[s][:], xs[:, bass.ds(t, 1), :].rearrange("p a d -> p (a d)"), mv[:, bass.ds(t, 1), 0],
                                    rstd[:, bass.ds(t, 1)], ALU.subtract, ALU.mult).then_inc(y_done, 1)

                def lows(t, s):
                    hold(dve, high, t + 1)
                    v.tensor_tensor(yT[1][:, :, bass.ds(t * P, P)], ps[s][:, 0:D].rearrange("p (c n) -> p c n", c=KC),
                                    yT[0][:, :, bass.ds(t * P, P)], ALU.subtract).then_inc(low, 1)
                for t in range(2):
                    normal(t, t)
                with dve.Fori(0, (T - 2) // SL) as i:
                    for s in range(SL):
                        normal(SL * i + s + 2, (s + 2) % SL)
                        lows(SL * i + s, s)
                for t in range(T - 2, T):
                    lows(t, t % SL)

            @block.scalar
            def _(act):
                s_ = nc.scalar
                with act.Fori(0, NB) as b:
                    act.wait_ge(neg, b + 1)
                    e = ng[:, bass.ds(B * b, B), :].rearrange("p b d -> p (b d)")
                    s_.activation(e, e, ACT.Exp).then_inc(ex, 1)
                act.wait_ge(scales, 1)
                s_.activation(rstd[:], rstd[:], ACT.Sqrt).then_inc(std, 1)

                def highs(t, s):
                    act.wait_ge(tr, t + SL + 1)
                    s_.activation(yT[0][:, :, bass.ds(t * P, P)], ps[s][:, 0:D].rearrange("p (c n) -> p c n", c=KC), ACT.Copy).then_inc(high, 1)
                with act.Fori(0, T // SL) as i:
                    for s in range(SL):
                        highs(SL * i + s, s)
                for t in range(T // SL * SL, T):
                    highs(t, t % SL)

            @block.tensor
            def _(pe):
                t_ = nc.tensor
                pe.wait_ge(in_id, 16)
                pe.nop().then_inc(tr, SL)
                pe.nop().then_inc(low, SL)

                def transposes(t, s):
                    pe.wait_ge(y_done, t + 1)
                    pe.wait_ge(low, t + 1)
                    for k in range(KC):
                        last = t_.transpose(ps[s][:, k * P:(k + 1) * P], y[s][:, k * P:(k + 1) * P], ident[:])
                    last.then_inc(tr, 1)
                with pe.Fori(0, T // SL) as i:
                    for s in range(SL):
                        transposes(SL * i + s, s)
                for t in range(T // SL * SL, T):
                    transposes(t, t % SL)


class Keep:
    pass


PAIRS = 50
TOP = 16
KEYS = 128
QD = 128
HALF = QD // 2
G = 2
GT = G * P
NGRP = T // G
U = G * H
ROWS = [TOP // (i + 1) for i in range(TOP)]
AT = [sum(ROWS[:i]) for i in range(TOP)]
SLOTS = 23
BLK = 4
KT = 2
KR = 4 * SLOTS
EA, EB = 32, 8
QUAD = 4
RSCALE = 64.0
WSCALE = 4096.0
LOW = -3.0e38


def slots():
    cells = [(i + 1, j + 1) for i in range(TOP) for j in range(ROWS[i])]

    def together(a, b):
        return a[0] * a[1] + b[0] * b[1] - min(a[0], b[0]) * min(a[1], b[1]) <= TOP
    near = [[k for k in range(PAIRS) if k != m and together(cells[m], cells[k])] for m in range(PAIRS)]
    slot = [-1] * PAIRS
    for _ in range(PAIRS):
        open_ = [m for m in range(PAIRS) if slot[m] < 0]
        used = {m: {slot[k] for k in near[m] if slot[k] >= 0} for m in open_}
        m = max(open_, key=lambda m: (len(used[m]), len(near[m]), -m))
        slot[m] = min(c for c in range(PAIRS) if c not in used[m])
    assert max(slot) < SLOTS
    return slot


def router_weights(nc, wq, bq, ln_g, ln_b, keys, down, up, identity, centre, own, k):
    with ExitStack() as ctx:
        sb = lambda n, s, d=FP32: ctx.enter_context(nc.sbuf_tensor(n, s, d))
        pb = lambda n, s, d=FP32: ctx.enter_context(nc.psum_tensor(n, s, d))
        sem = lambda n: ctx.enter_context(nc.semaphore(n))
        wn = sb("w_wn", [P, H, D])
        bt = sb("w_bt", [P, H])
        cm = sb("w_cm", [P, P])
        gb = sb("w_gb", [P, 2])
        kn = sb("w_kn", [P, 2, HALF])
        ksq = sb("w_ksq", [P, 2, HALF])
        kz = sb("w_kz", [P, 2, QD])
        nrm = sb("w_nrm", [P, 2])
        ones = sb("w_ones", [P, P])
        half = sb("w_half", [P, 2])
        tmp = sb("w_tmp", [P, 2])
        kt = sb("w_kt", [P, 2 * KEYS])
        bsel = sb("w_bsel", [P, H * (3 * H + 1)])
        kgf = sb("w_kgf", [P, 2 * KEYS])
        rqf = sb("w_rqf", [P, 2])
        kbh = sb("w_kbh", [3 * H, H, 2 * KEYS], FP16)
        kbl = sb("w_kbl", [3 * H, H, 2 * KEYS], FP16)
        low_row = sb("w_low", [3 * H, 2])
        dn = sb("w_dn", [P, KC, D])
        ps = [pb(f"w_ps{n}", [P, 512]) for n in range(8)]
        got, zero, st, mm, sq, ev = (sem("w_got"), sem("w_zero"), sem("w_st"), sem("w_mm"), sem("w_sq"), sem("w_ev"))
        with nc.Block() as block:
            @block.sync
            def _(sp):
                sp.dma_start(wn[:], wq.rearrange("(h q) d -> q h d", q=QD)).then_inc(got, 16)
                sp.dma_start(bt[:], bq.rearrange("(h q) -> q h", q=QD), allow_slow_non_contiguous=True).then_inc(got, 16)
                sp.dma_start(cm[:], centre).then_inc(got, 16)
                sp.dma_start(k.ident[:], identity).then_inc(got, 16)
                sp.dma_start(gb[:, 0:1], ln_g.unsqueeze(1), allow_slow_non_contiguous=True).then_inc(got, 16)
                sp.dma_start(gb[:, 1:2], ln_b.unsqueeze(1), allow_slow_non_contiguous=True).then_inc(got, 16)
                for n in range(2):
                    sp.dma_start(kn[:, n, :], keys[n]).then_inc(got, 16)
                sp.dma_start(dn[:], down[0:EA * EB, :].rearrange("(c p) d -> p c d", p=P)).then_inc(got, 16)
                for q in range(QUAD):
                    sp.dma_start(k.up[q:P:QUAD], up[0:EA * EB, :].rearrange("(a b) o -> a b o", b=EB)).then_inc(got, 16)
                sp.dma_start(k.own[:], own).then_inc(got, 16)
                sp.wait_ge(got, 16 * (10 + QUAD))

            @block.vector
            def _(dve):
                v = nc.vector
                link = chain(dve, st)
                v.memset(ones[:], 1.0).then_inc(zero, 1)
                v.memset(kz[:], 0.0).then_inc(zero, 1)
                v.memset(half[:], 0.0).then_inc(zero, 1)
                v.memset(bsel[:], 0.0).then_inc(zero, 1)
                v.memset(low_row[:], 0.0).then_inc(zero, 1)
                v.memset(k.eps[:], EPS).then_inc(zero, 1)
                dve.wait_ge(zero, 6)
                v.memset(half[0:HALF, 0:1], 1.0).then_inc(zero, 1)
                v.memset(half[HALF:QD, 1:2], 1.0).then_inc(zero, 1)
                v.memset(k.rsq[:, 0:1], 1.0 / QD).then_inc(zero, 1)
                dve.wait_ge(zero, 9)
                dve.wait_ge(got, 16 * (10 + QUAD))
                link(v.tensor_copy(k.ident16[:], k.ident[:]), wait=False)
                link(v.tensor_tensor(ksq[:], kn[:], kn[:], ALU.mult))
                link(v.tensor_reduce(nrm[:], ksq[:], AX.X, ALU.add))
                dve.wait_ge(sq, 1)
                link(v.tensor_scalar(nrm[:], nrm[:], 1e-12, None, ALU.max))
                link(v.reciprocal(nrm[:], nrm[:]))
                link(v.tensor_scalar(nrm[:], nrm[:], RSCALE, None, ALU.mult))
                for n in range(2):
                    link(v.tensor_scalar(kz[:, n, n * HALF:(n + 1) * HALF], kn[:, n, :], nrm[:, n:n + 1], None, ALU.mult), wait=n == 1)
                for n in range(3):
                    link(v.tensor_copy(bsel[:].rearrange("p (h x) -> p h x", h=H)[:, :, n * H], gb[:, 1:2].to_broadcast([P, H])), wait=False)
                link(v.tensor_reduce(low_row[:, 0:1], k.ident[0:3 * H, H:2 * H], AX.X, ALU.add))
                link(v.tensor_scalar(low_row[:, 1:2], low_row[:, 0:1], -1.0, 1.0, ALU.mult, ALU.add), wait=False)
                link(v.tensor_scalar(tmp[:], half[:], gb[:, 1:2], None, ALU.mult))
                link(v.tensor_scalar(rqf[:], tmp[:], gb[:, 0:1], 2.0, ALU.mult, ALU.mult))
                link(v.tensor_copy(k.rq[:, 0, :], rqf[:]))
                link(v.tensor_tensor(k.rq[:, 1, :], rqf[:], k.rq[:, 0, :], ALU.subtract), wait=False)
                link(v.tensor_scalar(k.rsq[:, 1:3], half[:], gb[:, 0:1], gb[:, 0:1], ALU.mult, ALU.mult), wait=False)
                link(v.tensor_scalar(tmp[:], tmp[:], gb[:, 1:2], None, ALU.mult))
                dve.wait_ge(mm, 2)
                link(v.tensor_copy(kt[:], ps[4][:, 0:2 * KEYS]))
                link(v.tensor_scalar(kgf[:], kt[:], gb[:, 0:1], None, ALU.mult))
                link(v.tensor_copy(k.kg[:, 0, :], kgf[:]))
                link(v.tensor_tensor(k.kg[:, 1, :], kgf[:], k.kg[:, 0, :], ALU.subtract))
                dve.wait_ge(mm, 3)
                v.tensor_copy(k.bsq[:], ps[5][:, 0:2]).then_inc(ev, 1)
                dve.wait_ge(mm, 4)
                for n in range(4):
                    two = lambda t: t[:, 2 * n:2 * n + 2, :].rearrange("p h k -> p (h k)")
                    link(v.tensor_copy(two(kbh), ps[n][0:3 * H, :]))
                    v.tensor_tensor(two(kbl), ps[n][0:3 * H, :], two(kbh), ALU.subtract).then_inc(ev, 1)
                dve.wait_ge(ev, 5)
                link(v.tensor_scalar(kbl[:], kbl[:], low_row[:, 0:1], None, ALU.mult))
                link(v.scalar_tensor_tensor(k.kb[:], kbh[:], low_row[:, 1:2], kbl[:], ALU.mult, ALU.add), wait=False)
                dve.wait_ge(mm, 5)
                for n in range(4):
                    wide = lambda part: k.wq[part][:, n // 2, (n % 2) * 512:(n % 2 + 1) * 512]
                    link(v.tensor_scalar(wide(0), ps[n][:], RSCALE, None, ALU.mult))
                    v.scalar_tensor_tensor(wide(1), ps[n][:], RSCALE, wide(0), ALU.mult, ALU.subtract).then_inc(ev, 1)
                dve.wait_ge(mm, 6)
                v.tensor_copy(k.bq[:], ps[5][:, 0:H]).then_inc(ev, 1)
                for q in range(QUAD):
                    for c in range(KC):
                        src = ps[6 + c][:, 0:D].rearrange("p (a b) -> p b a", b=EB)
                        link(v.tensor_scalar(k.down[0][:, c, :, :, q], src, RSCALE, None, ALU.mult))
                        v.scalar_tensor_tensor(k.down[1][:, c, :, :, q], src, RSCALE, k.down[0][:, c, :, :, q],
                                               ALU.mult, ALU.subtract).then_inc(ev, 1)

            @block.scalar
            def _(act):
                act.wait_ge(st, 3)
                nc.scalar.activation(nrm[:], nrm[:], ACT.Sqrt).then_inc(sq, 1)

            @block.tensor
            def _(pe):
                t_ = nc.tensor
                pe.wait_ge(zero, 9)
                pe.wait_ge(st, 19)
                for n in range(2):
                    t_.transpose(ps[4][:, n * KEYS:(n + 1) * KEYS], kz[:, n, :], k.ident[:]).then_inc(mm, 1)
                t_.matmul(ps[5][:, 0:2], ones[:], tmp[:], start=True, stop=True).then_inc(mm, 1)
                pe.wait_ge(st, 20)
                for h in range(H):
                    last = t_.matmul(ps[h // 2][0:3 * H, (h % 2) * 256:(h % 2 + 1) * 256], bsel[:, 3 * H * h:3 * H * (h + 1)], kt[:],
                                     start=True, stop=True)
                last.then_inc(mm, 1)
                pe.wait_ge(ev, 5)
                for h in range(H):
                    for c in range(KC):
                        last = t_.matmul(ps[2 * c + h // 4][:, (h % 4) * P:(h % 4 + 1) * P], wn[:, h, c * P:(c + 1) * P], cm[:],
                                         start=True, stop=True)
                last.then_inc(mm, 1)
                t_.matmul(ps[5][:, 0:H], cm[:], bt[:], start=True, stop=True)
                for c in range(KC):
                    for e in range(KC):
                        last = t_.transpose(ps[6 + c][:, e * P:(e + 1) * P], dn[:, e, c * P:(c + 1) * P], k.ident[:])
                last.then_inc(mm, 1)


def experts(nc, yT, scratch_x1, merge, k, out):
    with ExitStack() as ctx:
        sb = lambda n, s, d=FP32: ctx.enter_context(nc.sbuf_tensor(n, s, d))
        pb = lambda n, s, d=FP32: ctx.enter_context(nc.psum_tensor(n, s, d))
        sem = lambda n: ctx.enter_context(nc.semaphore(n))
        qT = sb("f_qT", [P, H, GT])
        qq = sb("f_qq", [P, H, GT])
        qh = sb("f_qh", [P, H, GT], FP16)
        ql = sb("f_ql", [P, H, GT], FP16)
        stdx = sb("f_stdx", [P, G, 3 * H], FP16)
        stdT = sb("f_stdT", [3 * H, GT], FP16)
        stt = sb("f_stt", [P, U, 5])
        facn = sb("f_facn", [P, U, 2])
        std = sb("f_std", [P, U])
        fac = sb("f_fac", [P, U, 2])
        fa2 = sb("f_fa2", [P, U, 2])
        z = sb("f_z", [P, U, 2 * KEYS])
        zr = sb("f_zr", [P, 2, 2 * KEYS])
        top = sb("f_top", [P, U, 2, TOP])
        idx = sb("f_idx", [P, U, 2, TOP], U16)
        sc = sb("f_sc", [P, U, 2, TOP])
        ixf = sb("f_ixf", [P, U, 2, TOP])
        cand = sb("f_cand", [P, U, PAIRS])
        ecand = sb("f_ecand", [P, U, PAIRS])
        cr1 = sb("f_cr1", [P, U, PAIRS])
        cr2 = sb("f_cr2", [P, U, PAIRS])
        best = sb("f_best", [P, U, TOP])
        be = sb("f_be", [P, U, TOP])
        zsum = sb("f_zsum", [P, U])
        wgt = cr1
        wm = sb("f_wm", [P, U, PAIRS])
        em = sb("f_em", [P, U, PAIRS], FP16)
        wT = sb("f_wT", [2 * PAIRS, BLK, GT])
        eT = sb("f_eT", [2 * PAIRS, BLK, GT], FP16)
        mg = sb("f_mg", [2 * PAIRS, 2, KR])
        mg16 = sb("f_mg16", [2 * PAIRS, 2, KR], FP16)
        wh = sb("f_wh", [KR, KT * GT], FP16)
        wl = sb("f_wl", [KR, KT * GT], FP16)
        eu = sb("f_eu", [KR, KT * GT], U16)
        ea = sb("f_ea", [KR, KT * GT], U16)
        eb = sb("f_eb", [KR, KT * GT], U16)
        oa = sb("f_oa", [KR, KT * GT // QUAD, EA, QUAD], FP16)
        ob = sb("f_ob", [KR, EB, KT * GT], FP16)
        wob = [sb("f_wob0", [KR, EB, KT * GT], FP16), ob]
        hh = sb("f_hh", [P, G, EB, P])
        x1 = sb("f_x1", [P, G, D])
        ps_q = [pb(f"f_psq{n}", [P, 512]) for n in range(2)]
        ps_z = [pb(f"f_psz{n}", [P, 512]) for n in range(2)]
        ps_s = pb("f_pss", [P, 512])
        ps_b = [pb(f"f_psb{n}", [P, 512]) for n in range(3)]
        S_ = {n: sem("f_" + n) for n in (
            "q_mm", "q_out", "stdx", "stdxT", "stdT", "stats", "std", "statsd", "fac", "facd", "qls", "ones0", "wlow", "inverted", "z_mm", "z_out", "z_free", "fstep", "tstep",
            "top", "pool", "sums", "sel", "argp", "arg", "expd", "zs", "wgtd", "masked", "mstep", "tr", "trout", "mrg", "whd",
            "oh", "ostep", "sct", "prod", "fin", "inner", "gelu", "resd", "mgd")}
        in_x1, in_mg = [sem("f_inx0"), sem("f_inx1")], sem("f_inmg")
        put = [sem("f_put0"), sem("f_put1")]

        def grp(name, per, g, n):
            return g * per + n

        with nc.Block() as block:
            @block.sync
            def _(sp):
                sp.dma_start(mg[:], merge).then_inc(in_mg, 16)
                for t in range(G):
                    sp.nop().then_inc(put[t], 16)

                def turn(g, rows):
                    for t in range(G):
                        sp.wait_ge(put[t], 16 * g + 16)
                        sp.dma_start(x1[:, t, :], scratch_x1[bass.ds((g * G + t) * P, P), :]).then_inc(in_x1[t], 16)
                    for t in range(G):
                        sp.wait_ge(S_["resd"], G * g + G + t + 1)
                        n = rows if t == G - 1 else P
                        sp.dma_start(out[bass.ds((g * G + t) * P, n), :], x1[0:n, t, :]).then_inc(put[t], 16)
                with sp.Fori(0, NGRP - 1) as g:
                    turn(g, P)
                turn(NGRP - 1, LAST)
                for t in range(G):
                    sp.wait_ge(put[t], 16 * NGRP + 16)

            @block.tensor
            def _(pe):
                t_ = nc.tensor

                def split(o, lhs, rhs, start, stop):
                    for n, (a, b) in enumerate(((0, 0), (0, 1), (1, 0))):
                        last = t_.matmul(o, lhs[a], rhs[b], start=start and n == 0, stop=stop and n == 2)
                    return last

                def queries(g):
                    for h in range(H):
                        n = h % 2
                        pe.wait_ge(S_["q_out"], 3 * (H * g + h) + 3)
                        for c in range(KC):
                            last = split(ps_q[n][:, 0:GT], [w[:, c, h * QD:(h + 1) * QD] for w in k.wq],
                                         [y[:, c, bass.ds(g * GT, GT)] for y in yT], c == 0, c == KC - 1)
                        last.then_inc(S_["q_mm"], 1)
                    pe.wait_ge(S_["q_out"], 3 * H * (g + 1) + 6)
                    pe.wait_ge(S_["statsd"], g + 1)
                    for t in range(G):
                        for h in range(H):
                            at = 5 * (t * H + h)
                            t_.matmul(ps_s[:, at + 2:at + 5], qq[:, h, t * P:(t + 1) * P], k.rsq[:], start=True, stop=True)
                    pe.wait_ge(S_["qls"], 2 * (g + 1))
                    for t in range(G):
                        for h in range(H):
                            at = 5 * (t * H + h)
                            last = split(ps_s[:, at:at + 2], [q[:, h, t * P:(t + 1) * P] for q in (qh, ql)],
                                         [k.rq[:, 0, :], k.rq[:, 1, :]], True, True)
                    last.then_inc(S_["stats"], 1)
                    pe.wait_ge(S_["stdx"], g + 1)
                    for t in range(G):
                        last = t_.transpose(ps_s[0:3 * H, KEYS:].bitcast(FP16)[:, t * P:(t + 1) * P], stdx[:, t, :], k.ident16[:])
                    last.then_inc(S_["stdxT"], 1)

                def scores(g):
                    pe.wait_ge(S_["stdT"], g + 1)
                    for t in range(G):
                        for h2 in range(H // 2):
                            n = h2 % 2
                            pe.wait_ge(S_["z_out"], H * g + 4 * t + h2 + 1)
                            for h in (2 * h2, 2 * h2 + 1):
                                o = ps_z[n][:, (h % 2) * 256:(h % 2 + 1) * 256]
                                split(o, [q[:, h, t * P:(t + 1) * P] for q in (qh, ql)], [k.kg[:, 0, :], k.kg[:, 1, :]], True, False)
                                last = t_.matmul(o, stdT[:, t * P:(t + 1) * P], k.kb[:, h, :], start=False, stop=True)
                            last.then_inc(S_["z_mm"], 1)

                def merges(g):
                    pe.wait_ge(S_["masked"], 2 * (g + 1))
                    pe.wait_ge(S_["resd"], G * g + G)
                    for t in range(G):
                        for b in range(BLK):
                            n = t * BLK + b
                            src = wm[:, t * H + 2 * b:t * H + 2 * b + 2, :].rearrange("p h c -> p (h c)")
                            t_.transpose(ps_b[n // 4][0:2 * PAIRS, (n % 4) * P:(n % 4 + 1) * P], src, k.ident[:])
                    for t in range(G):
                        for b in range(BLK):
                            n = t * BLK + b
                            src = em[:, t * H + 2 * b:t * H + 2 * b + 2, :].rearrange("p h c -> p (h c)")
                            last = t_.transpose(ps_b[2][0:2 * PAIRS, :].bitcast(FP16)[:, n * P:(n + 1) * P], src, k.ident16[:])
                    last.then_inc(S_["tr"], 1)
                    pe.wait_ge(S_["trout"], 3 * (g + 1))
                    for kt in range(KT):
                        for n in range(2):
                            t_.matmul(ps_b[0][0:KR, kt * GT:(kt + 1) * GT], mg[:, n, :], wT[:, 2 * kt + n, :], start=n == 0, stop=n == 1)
                    for kt in range(KT):
                        for n in range(2):
                            last = t_.matmul(ps_b[1][0:KR, kt * GT:(kt + 1) * GT], mg16[:, n, :], eT[:, 2 * kt + n, :],
                                             start=n == 0, stop=n == 1)
                    last.then_inc(S_["mrg"], 1)

                def inner(g):
                    for r in range(EB // 2):
                        n = r % 2
                        pe.wait_ge(S_["gelu"], QUAD * (4 * g + r) + QUAD)
                        for b in (2 * r, 2 * r + 1):
                            for c in range(KC):
                                last = split(ps_q[n][:, (b % 2) * GT:(b % 2 + 1) * GT],
                                             [w[:, c, b].rearrange("p a g -> p (a g)") for w in k.down],
                                             [y[:, c, bass.ds(g * GT, GT)] for y in yT], c == 0, c == KC - 1)
                        last.then_inc(S_["inner"], 1)

                HALF_G = P // QUAD // 2

                def scatter(g):
                    pe.wait_ge(S_["oh"], g + 1)
                    pe.wait_ge(S_["wlow"], g + 1)
                    for q in range(2 * G):
                        bank = ps_b[q % 3]
                        if q == 3:
                            pe.wait_ge(S_["prod"], 2 * G * g + 2 * G + 1)
                        for m in range(HALF_G):
                            tok = (q // 2) * P + (q % 2) * (P // 2) + m * QUAD
                            for kt in range(KT):
                                for part in range(2):
                                    at = kt * GT + tok
                                    last = t_.matmul(bank[:].rearrange("p (b m g) -> p b m g", b=EB, g=QUAD)[:, :, m, :],
                                                     oa[:, at // QUAD].rearrange("p a g -> p (a g)"),
                                                     wob[part][:, :, at:at + QUAD],
                                                     start=kt == 0 and part == 0, stop=kt == KT - 1 and part == 1)
                        last.then_inc(S_["sct"], 1)

                def final(g):
                    for t in range(G):
                        pe.wait_ge(S_["prod"], 2 * G * g + 2 * G + (2, 4)[t])
                        for b in range(EB):
                            last = t_.matmul(ps_b[1 + t][:, 0:D],
                                             hh[:, t, b, :], k.up[:, b, :], start=b == 0, stop=b == EB - 1)
                        last.then_inc(S_["fin"], 1)

                def turn(g, more=True):
                    pe.wait_ge(S_["gelu"], QUAD * 4 * g + 2 * QUAD)
                    if more:
                        queries(g + 2)
                    merges(g)
                    inner(g)
                    if more:
                        scores(g + 2)
                    scatter(g)
                    final(g)
                pe.nop().then_inc(S_["q_out"], 6)
                pe.nop().then_inc(S_["z_out"], 2)
                pe.nop().then_inc(S_["gelu"], 2 * QUAD)
                pe.wait_ge(S_["mgd"], 1)
                for g in range(2):
                    queries(g)
                    scores(g)
                with pe.Fori(0, NGRP - 2) as g:
                    turn(g)
                turn(NGRP - 2, False)
                turn(NGRP - 1, False)

            @block.scalar
            def _(act):
                s_ = nc.scalar

                def queries(g):
                    for h in range(H):
                        n = h % 2
                        act.wait_ge(S_["q_mm"], H * g + h + 1)
                        if h == 0:
                            act.wait_ge(S_["z_mm"], H * g + H)
                        for dst, f in ((qh, ACT.Identity), (qT, ACT.Identity), (qq, ACT.Square)):
                            s_.activation(dst[:, h, :], ps_q[n][:, 0:GT], f, bias=k.bq[:, h:h + 1], scale=1.0 / RSCALE).then_inc(S_["q_out"], 1)
                    act.wait_ge(S_["stats"], g + 1)
                    s_.activation(stt[:].rearrange("p u c -> p (u c)"), ps_s[:, 0:5 * U], ACT.Copy)
                    s_.activation(std[:], ps_s[:, 0:5 * U].rearrange("p (u c) -> p u c", c=5)[:, :, 2], ACT.Sqrt,
                                  bias=k.eps[:, :]).then_inc(S_["std"], 1)
                    act.nop().then_inc(S_["statsd"], 1)
                    act.wait_ge(S_["stdxT"], g + 1)
                    s_.activation(stdT[:], ps_s[0:3 * H, KEYS:].bitcast(FP16)[:, 0:GT], ACT.Copy).then_inc(S_["stdT"], 1)
                    act.wait_ge(S_["fac"], g + 1)
                    s_.activation(facn[:], facn[:], ACT.Sqrt, scale=RSCALE * RSCALE).then_inc(S_["facd"], 1)

                def scores(g):
                    for t in range(G):
                        for h2 in range(H // 2):
                            n = h2 % 2
                            at = 4 * t + h2
                            act.wait_ge(S_["z_mm"], H * g + H + at + 1)
                            act.wait_ge(S_["z_free"], H * g + at + 1)
                            s_.activation(z[:, 2 * at:2 * at + 2, :].rearrange("p u c -> p (u c)"), ps_z[n][:], ACT.Copy).then_inc(S_["z_out"], 1)

                def weights(g):
                    act.wait_ge(S_["arg"], 2 * g + 1)
                    s_.activation(be[:], be[:], ACT.Exp).then_inc(S_["expd"], 1)
                    act.wait_ge(S_["arg"], 2 * g + 2)
                    s_.activation(wgt[:], wgt[:], ACT.Exp).then_inc(S_["expd"], 1)

                def finish(g):
                    act.wait_ge(S_["tr"], g + 1)
                    for t in range(G):
                        s_.activation(wT[:, :, t * P:(t + 1) * P], ps_b[t][0:2 * PAIRS, :].rearrange("p (b n) -> p b n", b=BLK),
                                      ACT.Copy).then_inc(S_["trout"], 1)
                    s_.activation(eT[:].rearrange("p b (t n) -> p t b n", t=G),
                                  ps_b[2][0:2 * PAIRS, :].bitcast(FP16).rearrange("p (t b n) -> p t b n", t=G, b=BLK),
                                  ACT.Copy).then_inc(S_["trout"], 1)
                    act.wait_ge(S_["mrg"], g + 1)
                    s_.activation(wh[:], ps_b[0][0:KR, :], ACT.Copy).then_inc(S_["whd"], 1)
                    act.wait_ge(S_["prod"], 2 * G * g + 4)
                    for r in range(EB // 2):
                        n = r % 2
                        act.wait_ge(S_["inner"], 4 * g + r + 1)
                        for q in range(QUAD):
                            src = ps_q[n][:].rearrange("p (b m g) -> p b m g", b=2, g=QUAD)[:, :, :, q]
                            dst = k.acts[:, 2 * r:2 * r + 2, :, q]
                            s_.activation(dst, src, ACT.Gelu, scale=k.own[:, q:q + 1]).then_inc(S_["gelu"], 1)
                act.nop().then_inc(S_["z_mm"], H)
                act.nop().then_inc(S_["statsd"], 1)
                act.nop().then_inc(S_["prod"], 4)
                for g in range(2):
                    queries(g)
                    scores(g)
                weights(0)
                with act.Fori(0, NGRP - 2) as g:
                    queries(g + 2)
                    finish(g)
                    scores(g + 2)
                    weights(g + 1)
                finish(NGRP - 2)
                weights(NGRP - 1)
                finish(NGRP - 1)

            @block.vector
            def _(dve):
                v = nc.vector

                def step(name, per, g):
                    return chain(dve, S_[name], per, g)

                def topk(g, pairs):
                    for m in pairs:
                        hold(dve, S_["z_out"], H * g + m + 3)
                        halves = [(2 * m + s, s, n) for s in range(2) for n in range(2)]
                        base = 6 * U * g + 12 * m
                        zz = lambda u, s, n: z[:, u, n * KEYS:(n + 1) * KEYS]
                        zq = lambda u, s, n: zr[:, s, n * KEYS:(n + 1) * KEYS]
                        hi = lambda u, n: top[:, u, n, 0:8]
                        lo = lambda u, n: top[:, u, n, 8:16]
                        for u, s, n in halves:
                            v.max(hi(u, n), zz(u, s, n)).then_inc(S_["tstep"], 1)
                        for u, s, n in halves:
                            if n == 0:
                                hold(dve, S_["tstep"], base + 2 * s + 2)
                            v.match_replace(zq(u, s, n), hi(u, n), zz(u, s, n), LOW).then_inc(S_["tstep"], 1)
                        for u, s, n in halves:
                            if n == 0:
                                hold(dve, S_["tstep"], base + 2 * s + 6)
                            v.max(lo(u, n), zq(u, s, n)).then_inc(S_["tstep"], 1)
                        for u, s, n in halves:
                            last = v.max_index(idx[:, u, n, 0:8], hi(u, n), zz(u, s, n))
                        last.then_inc(S_["z_free"], 1)
                        hold(dve, S_["tstep"], base + 12)
                        for u, s, n in halves:
                            last = v.max_index(idx[:, u, n, 8:16], lo(u, n), zq(u, s, n))
                    if m == U // 2 - 1:
                        last.then_inc(S_["top"], 1)

                def invert(g):
                    dve.wait_ge(S_["facd"], g + 1)
                    v.reciprocal(fac[:], facn[:]).then_inc(S_["inverted"], 1)

                def select(g, more=True):
                    hold(dve, S_["sums"], 2 * (g + 1))
                    if more:
                        invert(g + 1)
                    lk = step("sel", 4 * U, g)
                    for q in range(4):
                        for u in range(U):
                            if q == 0:
                                ins = v.max(best[:, u, 0:8], cand[:, u, :])
                            elif q == 1:
                                ins = v.match_replace(cr1[:, u, :], best[:, u, 0:8], cand[:, u, :], LOW)
                            elif q == 2:
                                ins = v.max(best[:, u, 8:16], cr1[:, u, :])
                            else:
                                ins = v.match_replace(cr2[:, u, :], best[:, u, 8:16], cr1[:, u, :], LOW)
                            lk(ins, wait=u == U - 1)

                def totals(g):
                    lk = step("mstep", 3, g)
                    dve.wait_ge(S_["expd"], 2 * g + 1)
                    lk(v.tensor_reduce(zsum[:], be[:], AX.X, ALU.add))
                    lk(v.reciprocal(zsum[:], zsum[:]))
                    lk(v.tensor_scalar(zsum[:], zsum[:], WSCALE, None, ALU.mult), wait=False)

                def masks(g):
                    v.scalar_tensor_tensor(em[:], cr2[:], LOW / 2, ecand[:], ALU.is_lt, ALU.mult).then_inc(S_["masked"], 1)
                    dve.wait_ge(S_["wgtd"], g + 1)
                    v.scalar_tensor_tensor(wm[:], cr2[:], LOW / 2, wgt[:], ALU.is_lt, ALU.mult).then_inc(S_["masked"], 1)

                def onehots(g):
                    lk = step("ostep", 4 + EB, g)
                    dve.wait_ge(S_["whd"], g + 1)
                    lk(v.tensor_tensor(wl[:], ps_b[0][0:KR, :], wh[:], ALU.subtract), wait=False)
                    lk(v.tensor_copy(eu[:], ps_b[1][0:KR, :]))
                    lk(v.tensor_scalar(eb[:], eu[:], EB - 1, None, ALU.bitwise_and), wait=False)
                    lk(v.tensor_scalar(ea[:], eu[:], 3, None, ALU.logical_shift_right))
                    for b in range(EB):
                        lk(v.tensor_scalar(ob[:, b, :], eb[:], float(b), None, ALU.is_equal), wait=b == EB - 1)
                    v.tensor_tensor(wob[0][:], ob[:], wh[:].unsqueeze(1).to_broadcast([KR, EB, KT * GT]), ALU.mult).then_inc(S_["ones0"], 1)
                    for a in range(EA):
                        last = v.tensor_scalar(oa[:, :, a, :], ea[:].rearrange("p (m g) -> p m g", g=QUAD), float(a), None, ALU.is_equal)
                    last.then_inc(S_["oh"], 1)

                HALF_G = P // QUAD // 2

                def products(g):
                    dve.wait_ge(S_["gelu"], QUAD * (4 * g + 4) + 2 * QUAD)
                    for q in range(2 * G):
                        t, n = q // 2, q % 2
                        dve.wait_ge(S_["sct"], 2 * G * g + q + 1)
                        at = t * (P // QUAD) + n * HALF_G
                        v.scalar_tensor_tensor(hh[:, t, :, n * (P // 2):(n + 1) * (P // 2)],
                                               ps_b[q % 3][:].rearrange("p (b n) -> p b n", b=EB), 1.0 / WSCALE,
                                               k.acts[:, :, at:at + HALF_G].rearrange("p b m g -> p b (m g)"),
                                               ALU.mult, ALU.mult).then_inc(S_["prod"], 1)

                def results(g):
                    for t in range(G):
                        dve.wait_ge(S_["fin"], G * g + t + 1)
                        dve.wait_ge(in_x1[t], 16 * (g + 1))
                        v.tensor_tensor(x1[:, t, :], ps_b[1 + t][:, 0:D], x1[:, t, :], ALU.add).then_inc(S_["resd"], 1)

                v.nop().then_inc(S_["resd"], G)
                v.nop().then_inc(S_["z_free"], H)
                dve.wait_ge(in_mg, 16)
                v.tensor_copy(mg16[:], mg[:]).then_inc(S_["mgd"], 1)
                invert(0)
                topk(0, range(U // 2))
                select(0)

                def turn(g, first=False, more=True):
                    topk(g + 1, range(0, 1))
                    if not first:
                        products(g - 1)
                    topk(g + 1, range(1, 2))
                    totals(g)
                    topk(g + 1, range(2, 3))
                    if not first:
                        results(g - 1)
                    masks(g)
                    topk(g + 1, range(3, U // 2))
                    onehots(g)
                    select(g + 1, more)
                turn(0, first=True)
                with dve.Fori(1, NGRP - 2) as g:
                    turn(g)
                turn(NGRP - 2, more=False)
                products(NGRP - 2)
                results(NGRP - 2)
                totals(NGRP - 1)
                masks(NGRP - 1)
                onehots(NGRP - 1)
                products(NGRP - 1)
                results(NGRP - 1)

            @block.gpsimd
            def _(pool):
                g_ = nc.gpsimd

                def prepare(g):
                    for n in range(2):
                        hs = slice(n * H // 2, (n + 1) * H // 2)
                        hold(pool, S_["q_out"], 3 * (H * g + (n + 1) * H // 2) + 6)
                        g_.tensor_tensor(ql[:, hs, :], qT[:, hs, :], qh[:, hs, :], ALU.subtract).then_inc(S_["qls"], 1)
                    lk = chain(pool, S_["fstep"], 9, g)
                    hold(pool, S_["std"], g + 1)
                    byh = std[:].rearrange("p (t h) -> p t h", t=G)
                    lk(g_.tensor_copy(stdx[:, :, 0:2 * H].rearrange("p t (n h) -> p t n h", n=2),
                                      byh.unsqueeze(2).to_broadcast([P, G, 2, H])))
                    g_.tensor_tensor(stdx[:, :, 2 * H:], byh, stdx[:, :, 0:H], ALU.subtract).then_inc(S_["stdx"], 1)
                    sdb = bc(std[:], 2)
                    lk(g_.tensor_tensor(fa2[:], sdb, k.bsq[:].unsqueeze(1).to_broadcast([P, U, 2]), ALU.mult))
                    lk(g_.tensor_tensor(fa2[:], fa2[:], stt[:, :, 0:2], ALU.add))
                    lk(g_.tensor_tensor(fa2[:], fa2[:], sdb, ALU.mult))
                    lk(g_.tensor_tensor(facn[:], fa2[:], stt[:, :, 3:5], ALU.add))
                    lk(g_.tensor_scalar(fa2[:], sdb, 1e-12, None, ALU.mult))
                    lk(g_.tensor_tensor(fa2[:], fa2[:], fa2[:], ALU.mult))
                    lk(g_.tensor_tensor(facn[:], facn[:], fa2[:], ALU.subtract))
                    lk(g_.tensor_scalar(facn[:], facn[:], 0.0, None, ALU.max))
                    g_.tensor_tensor(facn[:], facn[:], fa2[:], ALU.add).then_inc(S_["fac"], 1)

                def sums(g):
                    lk = chain(pool, S_["pool"], 2, g)
                    hold(pool, S_["top"], g + 1)
                    hold(pool, S_["inverted"], g + 1)
                    lk(g_.tensor_copy(ixf[:], idx[:]), wait=False)
                    lk(g_.tensor_tensor(sc[:], top[:], bc(fac[:], TOP), ALU.mult))
                    for dst, src in ((cand, sc), (ecand, ixf)):
                        last = None
                        i = 0
                        while i < TOP:
                            m = ROWS[i]
                            n = sum(1 for r in ROWS if r == m)
                            o = dst[:, :, AT[i]:AT[i] + n * m].rearrange("p u (n m) -> p u n m", m=m)
                            last = g_.tensor_tensor(o, src[:, :, 0, i:i + n].unsqueeze(3).to_broadcast([P, U, n, m]),
                                                    src[:, :, 1, 0:m].unsqueeze(2).to_broadcast([P, U, n, m]), ALU.add)
                            i += n
                        last.then_inc(S_["sums"], 1)

                def low_weights(g):
                    hold(pool, S_["ones0"], g + 1)
                    g_.tensor_tensor(ob[:], ob[:], wl[:].unsqueeze(1).to_broadcast([KR, EB, KT * GT]), ALU.mult).then_inc(S_["wlow"], 1)

                def arguments(g):
                    pool.wait_ge(S_["sel"], 4 * U * (g + 1))
                    mx = best[:, :, 0]
                    g_.tensor_tensor(be[:], best[:], bc(mx, TOP), ALU.subtract).then_inc(S_["arg"], 1)
                    g_.tensor_tensor(wgt[:], cand[:], bc(mx, PAIRS), ALU.subtract).then_inc(S_["arg"], 1)

                def normalise(g):
                    pool.wait_ge(S_["expd"], 2 * (g + 1))
                    pool.wait_ge(S_["mstep"], 3 * (g + 1))
                    g_.tensor_tensor(wgt[:], wgt[:], bc(zsum[:], PAIRS), ALU.mult).then_inc(S_["wgtd"], 1)

                def turn(g, more=True):
                    normalise(g)
                    if more:
                        prepare(g + 2)
                    sums(g + 1)
                    low_weights(g)
                    arguments(g + 1)
                prepare(0)
                pool.wait_ge(S_["inverted"], 1)
                prepare(1)
                sums(0)
                arguments(0)
                with pool.Fori(0, NGRP - 2) as g:
                    turn(g)
                turn(NGRP - 2, False)
                normalise(NGRP - 1)
                low_weights(NGRP - 1)


def program(nc, x, adj, w, wb, a, wq, bq, ln_g, ln_b, keys0, keys1, down, up, identity, centre, own, merge, out):
    with ExitStack() as ctx:
        scratch_u = nc.dram_tensor("scratch_u", [2, H, HN], FP32, kind="Internal").ap()
        scratch_x = nc.dram_tensor("scratch_x", [PASSES, P, T * XC], FP16, kind="Internal").ap()
        scratch_xd = nc.dram_tensor("scratch_xd", [P, T * H * 2 * HA], FP16, kind="Internal").ap()
        scratch_x1 = nc.dram_tensor("scratch_x1", [NP, D], FP32, kind="Internal").ap()
        yT = [ctx.enter_context(nc.sbuf_tensor(f"yT{n}", [P, KC, NP], FP16)) for n in range(2)]
        with ExitStack() as gnn:
            sb = lambda n, s, d=FP32: gnn.enter_context(nc.sbuf_tensor(n, s, d))
            keep = Keep()
            keep.adjd = sb("adjd", [P, T, H, HA])
            keep.a = sb("a_all", [P, H, T])
            keep.c = sb("c_all", [P, H, T])
            keep.negv = sb("negv", [P, PASSES, T])
            keep.hsum = sb("hsum", [P, H * HA])
            project(nc, ctx, x, w, wb, a, identity, scratch_u, scratch_x, scratch_xd, keep)
            with ExitStack() as big:
                adjT = big.enter_context(nc.sbuf_tensor("adjT", [P, T, NP // 4], U32))
                keep.col32 = lambda t: adjT[:, :, bass.ds(t * (P // 4), P // 4)]
                keep.adj32 = lambda half, j: adjT[:, j, bass.ds(half * (HN // 4), HN // 4)]
                adjacency(nc, adj, identity, scratch_xd, keep)
                attention(nc, scratch_u.rearrange("a h n -> (a h) n"), scratch_x, keep)
            residual(nc, x, identity, keep, scratch_x1, yT)
        sb = lambda n, s, d=FP32: ctx.enter_context(nc.sbuf_tensor(n, s, d))
        k = Keep()
        k.ident = sb("ident", [P, P])
        k.ident16 = sb("ident16", [P, P], FP16)
        k.wq = [sb(f"wqT{n}", [P, KC, H * QD], FP16) for n in range(2)]
        k.bq = sb("bqc", [P, H])
        k.kg = sb("kg", [P, 2, 2 * KEYS], FP16)
        k.kb = sb("kb", [3 * H, H, 2 * KEYS], FP16)
        k.rq = sb("rq", [P, 2, 2], FP16)
        k.rsq = sb("rsq", [P, 3])
        k.bsq = sb("bsq", [P, 2])
        k.eps = sb("eps", [P, 1])
        k.own = sb("own", [P, QUAD])
        k.down = [sb(f"downT{n}", [P, KC, EB, EA, QUAD], FP16) for n in range(2)]
        k.up = sb("upb", [P, EB, D])
        k.acts = sb("acts", [P, EB, G * P // QUAD, QUAD])
        router_weights(nc, wq, bq, ln_g, ln_b, (keys0, keys1), down, up, identity, centre, own, k)
        experts(nc, yT, scratch_x1, merge, k, out)


def kernel(**inputs):
    import numpy as _np
    import concourse.bacc as _bacc
    from concourse import mybir as _mybir
    from concourse.bass_utils import run_bass_kernel_spmd as _run

    nc = _bacc.Bacc("TRN2", target_bir_lowering=False, num_devices=1)
    arrays, args = {}, []

    def give(name, array):
        array = _np.ascontiguousarray(array)
        arrays[name] = array
        args.append(nc.dram_tensor(name, array.shape, _mybir.dt.from_np(array.dtype), kind="ExternalInput").ap())
    for name in ("x", "adj", "L0_gnn_W_w", "L0_gnn_W_b", "L0_gnn_a", "L0_ffn_Wq", "L0_ffn_bq", "L0_ffn_ln_g", "L0_ffn_ln_b",
                 "L0_ffn_keys0", "L0_ffn_keys1", "L0_ffn_expert_down", "L0_ffn_expert_up"):
        give(f"in_{name}", inputs[name])
    give("in_identity", _np.eye(P, dtype=_np.float32))
    give("in_centre", _np.eye(P, dtype=_np.float32) - _np.float32(1.0 / P))
    give("in_own", _np.tile(_np.eye(QUAD, dtype=_np.float32) / _np.float32(RSCALE), (EA, 1)))
    merge = _np.zeros((2 * PAIRS, 2, KR), _np.float32)
    for c, s in enumerate(slots()):
        for head in range(2):
            for n in range(2):
                merge[head * PAIRS + c, n, (2 * n + head) * SLOTS + s] = 1.0
    give("in_merge", merge)
    args.append(nc.dram_tensor("out_0", (N, D), _mybir.dt.float32, kind="ExternalOutput").ap())
    program(nc, *args)
    r = _run(nc, [arrays], core_ids=[0])
    return r.results[0]["out_0"]
```

```python
import concourse.bass as bass
from concourse import mybir
from contextlib import ExitStack

FP32 = mybir.dt.float32
FP16 = mybir.dt.float16
BF16 = mybir.dt.bfloat16
FP8 = mybir.dt.float8e4
U8 = mybir.dt.uint8
U16 = mybir.dt.uint16
U32 = mybir.dt.uint32
ALU = mybir.AluOpType
ACT = mybir.ActivationFunctionType
AX = mybir.AxisListType

P = 128
N = 3327
T = (N + P - 1) // P
NP = T * P
LAST = N - (T - 1) * P
D = 256
KC = D // P
H = 8
HD = D // H
HA = HD + 1
XC = 4 * HA
HT = T // 2
HN = HT * P
PASSES = 2 * H
RSCALE = 64.0
SCALE = 1024.0
EPS = 1e-5
BY_DVE = 12
AMASKS, DMASKS = 4, 3
AHEAD = 4
CREDIT = 16


def chain(eng, sem, per=0, turn=0):
    n = [0]

    def link(ins, wait=True):
        n[0] += 1
        ins.then_inc(sem, 1)
        if wait:
            if per:
                hold(eng, sem, turn * per + n[0])
            else:
                eng.wait_ge(sem, n[0])
        return ins
    link.n = n
    return link


def hold(eng, sem, value):
    eng.wait_ge(sem, value)
    eng.nop(nofuse=True)


def split_product(nc, o, lhs, rhs, start, stop):
    for n, (a, b) in enumerate(((0, 0), (0, 1), (1, 0))):
        last = nc.tensor.matmul(o, lhs[a], rhs[b], start=start and n == 0, stop=stop and n == 2)
    return last


def bc(ap, n):
    return ap.unsqueeze(len(ap.shape)).to_broadcast(list(ap.shape) + [n])


def project(nc, x, adj, w, wb, a, identity, scratch_u, scratch_x, keep):
    with ExitStack() as ctx:
        sb = lambda n, s, d=FP32: ctx.enter_context(nc.sbuf_tensor(n, s, d))
        pb = lambda n, s, d=FP32: ctx.enter_context(nc.psum_tensor(n, s, d))
        sem = lambda n: ctx.enter_context(nc.semaphore(n))
        PARTS = 4
        cut = [HT * n // PARTS * 2 for n in range(PARTS)] + [T]
        W = D + 2 * H
        xs = sb("p_xs", [P, T, D])
        ident = sb("p_ident", [P, P])
        wn = sb("p_wn", [P, KC, D])
        ablk = sb("p_ablk", [P, KC, 2 * H])
        brow = sb("p_brow", [1, W])
        bcol = sb("p_bcol", [P, KC])
        ones = sb("p_ones", [P, P])
        ones16 = sb("p_ones16", [1, P], FP16)
        waug = [sb(f"p_waug{n}", [P, KC, W], FP16) for n in range(2)]
        bias = [sb(f"p_bias{n}", [1, W], FP16) for n in range(2)]
        mv = sb("p_mv", [P, T, 2])
        st = sb("p_st", [P, T, 6])
        rstd = sb("p_rstd", [P, T])
        xh = [sb(f"p_xh{n}", [P, D]) for n in range(2)]
        xhT = [[sb(f"p_xhT{s}{n}", [P, KC, P], FP16) for n in range(2)] for s in range(2)]
        haug = sb("p_haug", [P, T, H, HA])
        uv = sb("p_uv", [P, T, 2 * H])
        uvT = sb("p_uvT", [2 * H, NP])
        mx = sb("p_mx", [2 * H, 1])
        dmx = sb("p_dmx", [2 * H, 2 * H])
        mall = sb("p_mall", [P, 2 * H])
        tv = sb("p_tv", [P, T, H])
        t1 = sb("p_t1", [P, T, H])
        bexp = sb("p_bexp", [P, T, H])
        dexp = sb("p_dexp", [P, T, H])
        flat = xs[:].rearrange("p t d -> p (t d)")
        prod = [[flat[:, (2 * s + n) * T * HA:(2 * s + n + 1) * T * HA].rearrange("p (t d) -> p t d", d=HA) for n in range(2)]
                for s in range(2)]
        xb = [sb(f"p_xb{s}", [P, T, 2 * HA], FP16) for s in range(2)]

        def part(h, n):
            return keep.xd[:, h] if n else xb[h % 2][:]
        ps_w = [pb(f"p_psw{k}", [P, 512]) for k in range(KC)]
        ps_t = [pb(f"p_pst{k}", [P, 512]) for k in range(2)]
        ps_h = [pb(f"p_psh{k}", [P, 512]) for k in range(2)]
        ps_b = pb("p_psb", [P, 512])
        ps_s = pb("p_pss", [P, 512])
        z_done, in_w, in_x = sem("p_zeroed"), sem("p_in_w"), [sem(f"p_inx{n}") for n in range(PARTS)]
        wt_done, waug_done, st_done = sem("p_wt"), sem("p_waug"), sem("p_stats")
        dv, std_done = sem("p_dv"), sem("p_std")
        xh_done, xt_done, high, low = sem("p_xh"), sem("p_xt"), sem("p_high"), sem("p_low")
        mm_done, out_done = sem("p_mm"), sem("p_out")
        dm_done, m_bc = sem("p_dm"), sem("p_mbc")
        arg_done, exp_done, scaled, u_st, x_st = sem("p_arg"), sem("p_exp"), sem("p_scaled"), sem("p_ust"), [sem("p_xst0"), sem("p_xst1")]
        pad_done, hs_done, nv_done = sem("p_pad"), sem("p_hs"), sem("p_nv")
        prod_b, prod_d, xb_high, xb_low = sem("p_prodb"), sem("p_prodd"), sem("p_xbh"), sem("p_xbl")

        with nc.Block() as block:
            @block.sync
            def _(sp):
                for n in range(PARTS):
                    if n == PARTS - 1:
                        sp.wait_ge(z_done, 1)
                        sp.dma_start(xs[:, cut[n]:T - 1, :], x[cut[n] * P:(T - 1) * P, :].rearrange("(t p) d -> p t d", p=P)).then_inc(in_x[n], 16)
                        sp.dma_start(xs[0:LAST, T - 1, :], x[(T - 1) * P:N, :]).then_inc(in_x[n], 16)
                    else:
                        sp.dma_start(xs[:, cut[n]:cut[n + 1], :], x[cut[n] * P:cut[n + 1] * P, :].rearrange("(t p) d -> p t d", p=P)).then_inc(in_x[n], 16)
                sp.wait_ge(out_done, T + 2)
                for half in range(2):
                    sp.dma_start(scratch_u[half], uvT[0:H, half * HN:(half + 1) * HN]).then_inc(u_st, 16)
                for h in range(H):
                    for n in range(2):
                        sp.wait_ge(xb_low, 2 * h + n + 1)
                        sp.dma_start(scratch_x[h, :, n], part(h, n)).then_inc(x_st[h % 2], 16)
                sp.wait_ge(u_st, 32)
                for s in range(2):
                    sp.wait_ge(x_st[s], 32 * (H // 2))

            @block.vector
            def _(dve):
                v = nc.vector
                v.memset(xs[:, T - 1, :], 0.0).then_inc(z_done, 1)
                v.memset(ablk[:], 0.0).then_inc(z_done, 1)
                v.memset(ones[:], 1.0).then_inc(z_done, 1)
                v.memset(ones16[:], 1.0).then_inc(z_done, 1)
                v.memset(haug[:, :, :, HD], 1.0).then_inc(z_done, 1)
                for n in range(PARTS):
                    dve.wait_ge(in_x[n], 32 if n == PARTS - 1 else 16)
                    with dve.Fori(cut[n], cut[n + 1]) as t:
                        v.bn_stats(st[:, bass.ds(t, 1), :].rearrange("p a c -> p (a c)"),
                                   xs[:, bass.ds(t, 1), :].rearrange("p a d -> p (a d)")).then_inc(st_done, 1)
                dve.wait_ge(st_done, T)
                for t in range(T):
                    last = v.bn_aggr(mv[:, t, :], st[:, t, :])
                link = chain(dve, dv)
                link(last)
                link(v.tensor_scalar(rstd[:], mv[:, :, 1], EPS, None, ALU.add), wait=False)
                for k in range(KC):
                    dve.wait_ge(wt_done, k + 1)
                    link(v.tensor_scalar(waug[0][:, k, :], ps_w[k][:, 0:W], RSCALE, None, ALU.mult))
                    v.scalar_tensor_tensor(waug[1][:, k, :], ps_w[k][:, 0:W], RSCALE, waug[0][:, k, :],
                                           ALU.mult, ALU.subtract).then_inc(waug_done, 1)
                dve.wait_ge(wt_done, 3)
                link(v.tensor_copy(brow[0:1, D:], ps_b[0:1, 0:2 * H]))
                link(v.tensor_scalar(bias[0][:], brow[:], RSCALE, None, ALU.mult))
                v.scalar_tensor_tensor(bias[1][:], brow[:], RSCALE, bias[0][:], ALU.mult, ALU.subtract).then_inc(waug_done, 1)
                dve.wait_ge(std_done, 1)
                link(v.reciprocal(rstd[:], rstd[:]))

                def normal(t, s):
                    dve.wait_ge(xt_done, t + 1)
                    v.tensor_scalar(xh[s][:], xs[:, bass.ds(t, 1), :].rearrange("p a d -> p (a d)"),
                                    mv[:, bass.ds(t, 1), 0], rstd[:, bass.ds(t, 1)],
                                    ALU.subtract, ALU.mult).then_inc(xh_done, 1)

                def lows(t, s):
                    dve.wait_ge(high, t + 1)
                    v.tensor_tensor(xhT[s][1][:], ps_t[s][:, 0:D].rearrange("p (c n) -> p c n", c=KC), xhT[s][0][:],
                                    ALU.subtract).then_inc(low, 1)
                for t in range(2):
                    normal(t, t)
                with dve.Fori(0, HT - 1) as i:
                    for s in range(2):
                        lows(2 * i + s, s)
                        normal(2 * i + s + 2, s)
                for s in range(2):
                    lows(T - 2 + s, s)
                dve.wait_ge(out_done, T + 2)
                link(v.reduce_max(mx[:], uvT[:, 0:N], AX.X))
                v.tensor_scalar(dmx[:], ident[0:2 * H, 0:2 * H], mx[:, 0:1], None, ALU.mult).then_inc(dm_done, 1)
                dve.wait_ge(m_bc, 1)
                link(v.tensor_copy(mall[:], ps_s[:, 0:2 * H]))
                mb = mall[:, H:2 * H].unsqueeze(1).to_broadcast([P, T, H])
                link(v.tensor_tensor(bexp[:], uv[:, :, H:2 * H], mb, ALU.subtract), wait=False)
                link(v.tensor_tensor(tv[:], uv[:, :, 0:H], mb, ALU.add))
                v.tensor_scalar(bexp[:], bexp[:], 0.0, None, ALU.min).then_inc(arg_done, 1)
                v.tensor_scalar(t1[:], tv[:], 0.8, 0.0, ALU.mult, ALU.min).then_inc(arg_done, 1)
                v.tensor_scalar(tv[:], tv[:], -0.8, 0.0, ALU.mult, ALU.min).then_inc(arg_done, 1)
                dve.wait_ge(exp_done, 2)
                v.tensor_scalar(bexp[:], bexp[:], SCALE, None, ALU.mult).then_inc(scaled, 1)
                v.tensor_scalar(dexp[:], dexp[:], SCALE, None, ALU.mult).then_inc(scaled, 1)
                dve.wait_ge(scaled, 2)

                def product(h):
                    if h >= 2:
                        dve.wait_ge(xb_low, 2 * (h - 1))
                    v.tensor_tensor(prod[h % 2][0], haug[:, :, h, :], bc(bexp[:, :, h], HA), ALU.mult).then_inc(prod_b, 1)
                product(0)
                for h in range(H):
                    if h + 1 < H:
                        product(h + 1)
                    for n in range(2):
                        dve.wait_ge(xb_high, 2 * h + n + 1)
                        o = part(h, n)
                        v.tensor_tensor(o[:, :, HA:2 * HA], prod[h % 2][n], o[:, :, 0:HA], ALU.subtract).then_inc(xb_low, 1)
                v.tensor_scalar(keep.negv[:], uv[:, :, H:2 * H].rearrange("p t h -> p h t"), -1.0, None, ALU.mult).then_inc(nv_done, 1)
                dve.wait_ge(hs_done, 1)
                v.tensor_copy(keep.hsum[:], ps_s[:, 0:H * HA]).then_inc(nv_done, 1)

            @block.gpsimd
            def _(pool):
                g = nc.gpsimd
                for s in range(2):
                    g.memset(keep.stage[s][:, N:NP], 0.0).then_inc(pad_done, 1)
                pool.wait_ge(pad_done, 2)
                for n in range(PARTS):
                    pool.wait_ge(in_x[n], 32 if n == PARTS - 1 else 16)
                for s in range(2):
                    g.dma_start(keep.stage[s][:, 0:N], adj[s * P:(s + 1) * P, :]).then_inc(keep.in_adj[s], 16)
                pool.wait_ge(scaled, 2)
                for h in range(H):
                    if h >= 2:
                        pool.wait_ge(xb_low, 2 * (h - 1))
                    g.tensor_tensor(prod[h % 2][1], haug[:, :, h, :], bc(dexp[:, :, h], HA), ALU.mult).then_inc(prod_d, 1)

            @block.scalar
            def _(act):
                s_ = nc.scalar
                s_.dma_start(wn[:], w.rearrange("(c p) d -> p c d", p=P)).then_inc(in_w, 16)
                s_.dma_start(ident[:], identity).then_inc(in_w, 16)
                s_.dma_start(brow[0:1, 0:D], wb.unsqueeze(0)).then_inc(in_w, 16)
                s_.dma_start(bcol[:], wb.rearrange("(c p) -> p c", p=P), allow_slow_non_contiguous=True).then_inc(in_w, 16)
                act.wait_ge(z_done, 5)
                for h in range(H):
                    for s in range(2):
                        q = HD * (h % 4)
                        s_.dma_start(ablk[q:q + HD, h // 4, s * H + h:s * H + h + 1],
                                     a[s * HD:(s + 1) * HD, :]).then_inc(in_w, 16)
                act.wait_ge(dv, 2)
                s_.activation(rstd[:], rstd[:], ACT.Sqrt).then_inc(std_done, 1)

                def highs(t, s):
                    act.wait_ge(xt_done, t + 3)
                    act.wait_ge(mm_done, t + 1)
                    s_.activation(xhT[s][0][:], ps_t[s][:, 0:D].rearrange("p (c n) -> p c n", c=KC), ACT.Copy).then_inc(high, 1)

                def outs(t, s):
                    act.wait_ge(mm_done, t + 3)
                    s_.activation(haug[:, bass.ds(t, 1), :, 0:HD].rearrange("p a h d -> p (a h) d"),
                                  ps_h[s][:, 0:D].rearrange("p (h d) -> p h d", h=H), ACT.Copy, scale=1.0 / RSCALE)
                    s_.activation(uv[:, bass.ds(t, 1), :].rearrange("p a c -> p (a c)"), ps_h[s][:, D:W], ACT.Copy, scale=1.0 / RSCALE)
                    s_.activation(uvT[:, bass.ds(t * P, P)], ps_w[s][0:2 * H, 0:P], ACT.Copy, scale=1.0 / RSCALE).then_inc(out_done, 1)
                highs(0, 0)
                with act.Fori(0, HT - 1) as i:
                    for s in range(2):
                        highs(2 * i + s + 1, 1 - s)
                        outs(2 * i + s, s)
                highs(T - 1, 1)
                outs(T - 2, 0)
                outs(T - 1, 1)
                act.wait_ge(arg_done, 1)
                s_.activation(dexp[:], bexp[:], ACT.Exp, scale=0.2).then_inc(exp_done, 1)
                act.wait_ge(exp_done, 1)
                s_.activation(bexp[:], bexp[:], ACT.Exp).then_inc(exp_done, 1)
                act.wait_ge(arg_done, 3)
                s_.activation(keep.a[:].rearrange("p h t -> p t h"), t1[:], ACT.Exp)
                s_.activation(keep.c[:].rearrange("p h t -> p t h"), tv[:], ACT.Exp)
                for h in range(H):
                    if h >= 2:
                        act.wait_ge(x_st[h % 2], 32 * (h // 2))
                    for n, ready in enumerate((prod_b, prod_d)):
                        act.wait_ge(ready, h + 1)
                        s_.activation(part(h, n)[:, :, 0:HA], prod[h % 2][n], ACT.Copy).then_inc(xb_high, 1)

            @block.tensor
            def _(pe):
                t_ = nc.tensor
                pe.wait_ge(in_w, 16 * (4 + 2 * H))
                pe.wait_ge(z_done, 5)
                for k in range(KC):
                    for c in range(KC):
                        t_.transpose(ps_w[k][:, c * P:(c + 1) * P], wn[:, c, k * P:(k + 1) * P], ident[:])
                    for c in range(KC):
                        last = t_.matmul(ps_w[k][:, D:W], wn[:, c, k * P:(k + 1) * P], ablk[:, c, :],
                                         start=c == 0, stop=c == KC - 1)
                    last.then_inc(wt_done, 1)
                for c in range(KC):
                    last = t_.matmul(ps_b[0:1, 0:2 * H], bcol[:, c:c + 1], ablk[:, c, :], start=c == 0, stop=c == KC - 1)
                last.then_inc(wt_done, 1)
                pe.wait_ge(waug_done, KC + 1)
                for free in (xt_done, low, mm_done, out_done):
                    pe.nop().then_inc(free, 2)

                def transposes(t, s):
                    pe.wait_ge(xh_done, t + 1)
                    pe.wait_ge(low, t + 1)
                    for k in range(KC):
                        last = t_.transpose(ps_t[s][:, k * P:(k + 1) * P], xh[s][:, k * P:(k + 1) * P], ident[:])
                    last.then_inc(xt_done, 1)

                def products(t, s):
                    pe.wait_ge(low, t + 3)
                    pe.wait_ge(out_done, t + 1)
                    uvo = ps_w[s][0:2 * H, 0:P]
                    for k in range(KC):
                        y, wk = [p[:, k, :] for p in xhT[s]], [p[:, k, :] for p in waug]
                        split_product(nc, ps_h[s][:, 0:W], y, wk, k == 0, False)
                        split_product(nc, uvo, [p[:, D:W] for p in wk], y, k == 0, False)
                    for n in range(2):
                        t_.matmul(ps_h[s][:, 0:W], ones16[:], bias[n][:], start=False, stop=n == 1)
                        last = t_.matmul(uvo, bias[n][:, D:W], ones16[:], start=False, stop=n == 1)
                    last.then_inc(mm_done, 1)
                transposes(0, 0)
                with pe.Fori(0, HT - 1) as i:
                    for s in range(2):
                        transposes(2 * i + s + 1, 1 - s)
                        products(2 * i + s, s)
                transposes(T - 1, 1)
                products(T - 2, 0)
                products(T - 1, 1)
                pe.wait_ge(dm_done, 1)
                t_.matmul(ps_s[:, 0:2 * H], ones[0:2 * H, :], dmx[:], start=True, stop=True).then_inc(m_bc, 1)
                pe.wait_ge(out_done, T + 2)
                pe.wait_ge(arg_done, 1)
                for t in range(T):
                    rows = LAST if t == T - 1 else P
                    last = t_.matmul(ps_s[:, 0:H * HA], ones[0:rows, :], haug[0:rows, t].rearrange("p h d -> p (h d)"),
                                     start=t == 0, stop=t == T - 1)
                last.then_inc(hs_done, 1)


def adjacency(nc, adj, identity, keep):
    with ExitStack() as ctx:
        sb = lambda n, s, d=FP32: ctx.enter_context(nc.sbuf_tensor(n, s, d))
        pb = lambda n, s, d=FP32: ctx.enter_context(nc.psum_tensor(n, s, d))
        sem = lambda n: ctx.enter_context(nc.semaphore(n))
        ident32 = sb("a_id32", [P, P])
        ident = sb("a_ident", [P, P], BF16)
        xd, stage = keep.xd, keep.stage
        col = [sb(f"a_col{s}", [P, T, P], U8) for s in range(2)]
        raw = [sb(f"a_raw{s}", [P, H, 2, HA]) for s in range(2)]
        GRP = 8
        groups = [(g, min(GRP, T - g)) for g in range(0, T, GRP)]
        NG = len(groups)
        ps_t = [pb(f"a_pst{k}", [P, GRP * P], BF16) for k in range(NG)]
        ps_d = [[pb(f"a_psd{s}{k}", [P, 512]) for k in range(2)] for s in range(2)]
        in_id, id_done, in_adj = sem("a_inid"), sem("a_id"), keep.in_adj
        tr, tr_out, copied, mm, raw_done, add_done = (sem("a_tr"), sem("a_trout"), sem("a_copied"), sem("a_mm"),
                                                      sem("a_raw"), sem("a_add"))

        with nc.Block() as block:
            @block.sync
            def _(sp):
                sp.dma_start(ident32[:], identity).then_inc(in_id, 16)

            @block.gpsimd
            def _(pool):
                g = nc.gpsimd

                def load(t, s, rows=P):
                    g.dma_start(stage[s][0:rows, 0:N], adj[bass.ds(t * P, rows), :]).then_inc(in_adj[s], 16)

                def turn(t, s, rows=P):
                    pool.wait_ge(tr, NG * (t + 1))
                    load(t + 2, s, rows)
                    collect(t, s)

                def collect(t, s):
                    pool.wait_ge(tr_out, NG * (t + 1))
                    g.tensor_copy(keep.col32(t), col[s][:].bitcast(U32)).then_inc(copied, 1)
                    pool.wait_ge(raw_done, t + 1)
                    g.tensor_tensor(keep.adjd[:, bass.ds(t, 1)].rearrange("p a h d -> p (a h) d"), raw[s][:, :, 0, :],
                                    raw[s][:, :, 1, :], ALU.add).then_inc(add_done, 1)
                with pool.Fori(0, HT - 2) as i:
                    for s in range(2):
                        turn(2 * i + s, s)
                turn(T - 4, 0)
                turn(T - 3, 1, LAST)
                collect(T - 2, 0)
                collect(T - 1, 1)

            @block.vector
            def _(dve):
                v = nc.vector
                dve.wait_ge(in_id, 16)
                v.tensor_copy(ident[:], ident32[:]).then_inc(id_done, 1)
                v.nop().then_inc(copied, 2)
                with dve.Fori(0, HT) as i:
                    for s in range(2):
                        t = 2 * i + s
                        dve.wait_ge(copied, t + 1)
                        dve.wait_ge(mm, t + 1)
                        for n, (g0, w) in enumerate(groups):
                            dve.wait_ge(tr, NG * t + n + 1)
                            v.tensor_scalar(col[s][:, g0:g0 + w, :].rearrange("p a b -> p (a b)"), ps_t[n][:, 0:w * P],
                                            0.0, 64.0, ALU.not_equal, ALU.mult).then_inc(tr_out, 1)

            @block.scalar
            def _(act):
                s_ = nc.scalar
                act.nop().then_inc(add_done, 2)
                with act.Fori(0, HT) as i:
                    for s in range(2):
                        t = 2 * i + s
                        act.wait_ge(mm, t + 3)
                        act.wait_ge(add_done, t + 1)
                        for k in range(2):
                            ins = s_.activation(raw[s][:, 4 * k:4 * k + 4].rearrange("p h a d -> p (h a d)"),
                                                ps_d[s][k][:, 0:8 * HA], ACT.Copy)
                        ins.then_inc(raw_done, 1)

            @block.tensor
            def _(pe):
                t_ = nc.tensor
                pe.nop().then_inc(mm, 2)
                pe.wait_ge(id_done, 1)

                def transposes(t, s, loads):
                    pe.wait_ge(in_adj[s], 16 * loads)
                    for n, (g0, w) in enumerate(groups):
                        if not (isinstance(t, int) and t == 0):
                            pe.wait_ge(tr_out, NG * (t - 1) + n + 1)
                        for k in range(w):
                            last = t_.transpose(ps_t[n][:, k * P:(k + 1) * P], stage[s][:, (g0 + k) * P:(g0 + k + 1) * P], ident[:])
                        last.then_inc(tr, 1)

                def products(t, s):
                    hold(pe, tr_out, NG * (t + 1))
                    for j in range(T):
                        for k in range(2):
                            last = t_.matmul(ps_d[s][k][:, 0:8 * HA], col[s][:, j, :].bitcast(FP8),
                                             xd[:, 4 * k:4 * k + 4, j, :],
                                             start=j == 0, stop=j == T - 1)
                    last.then_inc(mm, 1)
                transposes(0, 0, 1)
                with pe.Fori(0, HT - 1) as i:
                    transposes(2 * i + 1, 1, i + 1)
                    pe.wait_ge(add_done, 2 * i + 1)
                    products(2 * i, 0)
                    transposes(2 * i + 2, 0, i + 2)
                    pe.wait_ge(add_done, 2 * i + 2)
                    products(2 * i + 1, 1)
                transposes(T - 1, 1, HT)
                pe.wait_ge(add_done, T - 1)
                products(T - 2, 0)
                pe.wait_ge(add_done, T)
                products(T - 1, 1)


def attention(nc, scratch_u, scratch_x, keep):
    with ExitStack() as ctx:
        sb = lambda n, s, d=FP32: ctx.enter_context(nc.sbuf_tensor(n, s, d))
        pb = lambda n, s, d=FP32: ctx.enter_context(nc.psum_tensor(n, s, d))
        sem = lambda n: ctx.enter_context(nc.semaphore(n))
        PER = 3
        NB = (HT + PER - 1) // PER
        ub = keep.ub
        nv = [sb(f"g_nv{s}", [P, T]) for s in range(2)]
        room = keep.xd[:].rearrange("p h t c -> p (h t c)")
        xo = [room[:, s * T * XC:(s + 1) * T * XC].rearrange("p (n t c) -> p n t c", n=2, t=T) for s in range(2)]
        mask = {True: [sb(f"g_amask{k}", [P, HN], FP8) for k in range(AMASKS)],
                False: [sb(f"g_dmask{k}", [P, HN], FP8) for k in range(DMASKS)]}
        rest = room[:, 2 * T * XC:].bitcast(FP32)
        raw = rest[:, 0:HT * XC].rearrange("p (t c) -> p t c", c=XC)
        comb = rest[:, HT * XC:HT * XC + 2 * HT * HA].rearrange("p (t k a) -> p t k a", k=2, a=HA)
        acc = pb("g_acc", [P, NB, 512])
        loaded = [sem("g_in0"), sem("g_in1")]
        signs, made, ready, free, evac, summed, pl = (sem("g_signs"), sem("g_made"), sem("g_ready"), sem("g_free"), sem("g_evac"),
                                                      sem("g_summed"), sem("g_pl"))

        by_act = [not (j + 1) * BY_DVE // T > j * BY_DVE // T for j in range(T)] * 2
        assert 2 * (T - BY_DVE) % AMASKS == 0 and 2 * BY_DVE % DMASKS == 0
        order = [sum(1 for m in range(n) if by_act[m] == by_act[n]) for n in range(2 * T)]
        buf = [mask[by_act[n]][order[n] % (AMASKS if by_act[n] else DMASKS)] for n in range(2 * T)]
        before = [max(m for m in range(-2 * T, n) if buf[m % (2 * T)] is buf[n]) for n in range(2 * T)]
        assert min(before) >= -CREDIT

        with nc.Block() as block:
            @block.sync
            def _(sp):
                def load(p, h, s):
                    sp.dma_start(ub[s], scratch_u[bass.ds(p, 1), :].partition_broadcast(P)).then_inc(loaded[s], 16)
                    sp.dma_start(xo[s].rearrange("p n t c -> p (n t c)"), scratch_x[bass.ds(h, 1)].rearrange("a p n t c -> p (a n t c)")).then_inc(loaded[s], 16)
                    sp.dma_start(nv[s][:], keep.negv[:, bass.ds(h, 1), :].rearrange("p a t -> p (a t)")).then_inc(loaded[s], 16)

                def turn(p, h, s):
                    sp.wait_ge(free, CREDIT + T * (p - 1))
                    load(p, h, s)
                for s in range(2):
                    load(s, s, s)
                with sp.Fori(1, H // 2) as q:
                    for s in range(2):
                        turn(2 * q + s, 2 * q + s, s)
                with sp.Fori(0, H // 2) as q:
                    for s in range(2):
                        turn(H + 2 * q + s, 2 * q + s, s)

            @block.scalar
            def _(act):
                s_ = nc.scalar
                full = (NB - 1) * PER

                def masks(r, s, columns):
                    for j in columns:
                        n = s * T + j
                        if j == 0:
                            act.wait_ge(loaded[s], 48 * (r + 1))
                        if by_act[n]:
                            hold(act, free, 2 * T * r + before[n] + 1 + CREDIT)
                            s_.activation(buf[n][:], ub[s], ACT.Sign, bias=nv[s][:, j:j + 1], scale=-1.0, saturate=False).then_inc(signs, 1)

                def copy_out(p):
                    act.wait_ge(free, CREDIT + T * (p + 1))
                    act.wait_ge(summed, p + 1)
                    s_.activation(raw[:, 0:full, :].rearrange("p (b t) c -> p b (t c)", t=PER),
                                  acc[:, 0:NB - 1, 0:PER * XC], ACT.Copy).then_inc(evac, 1)
                    s_.activation(raw[:, full:HT, :].rearrange("p t c -> p (t c)"),
                                  acc[:, NB - 1, 0:(HT - full) * XC], ACT.Copy).then_inc(evac, 1)

                masks(0, 0, range(AHEAD))

                def turn(r, more=True):
                    masks(r, 0, range(AHEAD, T))
                    masks(r, 1, range(AHEAD))
                    copy_out(2 * r)
                    masks(r, 1, range(AHEAD, T))
                    if more:
                        masks(r + 1, 0, range(AHEAD))
                    copy_out(2 * r + 1)
                with act.Fori(0, PASSES // 2 - 1) as r:
                    turn(r)
                turn(PASSES // 2 - 1, False)

            @block.vector
            def _(dve):
                v = nc.vector
                A2, D2 = 2 * (T - BY_DVE), 2 * BY_DVE
                with dve.Fori(0, 2) as half:
                    with dve.Fori(0, H // 2) as q:
                        def make(n):
                            s, j = n // T, n % T
                            hold(dve, free, (H * T) * half + (2 * T) * q + before[n] + 1 + CREDIT)
                            v.tensor_scalar(buf[n][:], ub[s], nv[s][:, j:j + 1], 2.0, ALU.is_gt, ALU.mult, saturate=False).then_inc(made, 1)

                        for n in range(2 * T):
                            s, j = n // T, n % T
                            if j == 0:
                                dve.wait_ge(loaded[s], 16 * 3 * (H // 2) * half + 48 * q + 48)
                            if j + 1 < T and not by_act[n + 1]:
                                make(n + 1)
                            bits, edges = buf[n][:].bitcast(U32), keep.adj32(half, j)
                            if by_act[n]:
                                dve.wait_ge(signs, (A2 * (H // 2)) * half + A2 * q + order[n] + 1)
                                v.scalar_tensor_tensor(bits, bits, 1, edges, ALU.logical_shift_right, ALU.bitwise_and).then_inc(ready, 1)
                            else:
                                dve.wait_ge(made, (D2 * (H // 2)) * half + D2 * q + order[n] + 1)
                                v.tensor_tensor(bits, bits, edges, ALU.bitwise_and).then_inc(ready, 1)

            @block.tensor
            def _(pe):
                t_ = nc.tensor
                pe.nop().then_inc(free, CREDIT)
                pe.nop().then_inc(evac, 2)
                with pe.Fori(0, PASSES // 2) as r:
                    for n in range(2 * T):
                        s, j = n // T, n % T
                        if j == 0:
                            pe.wait_ge(loaded[s], 48 * (r + 1))
                            pe.wait_ge(evac, 2 * (2 * r + s) + 2)
                        hold(pe, ready, 2 * T * r + n + 1)
                        for it in range(HT):
                            b, c = it // PER, it % PER
                            last = t_.matmul(acc[:, b, c * XC:(c + 1) * XC], buf[n][:, it * P:(it + 1) * P],
                                             xo[s][:, :, j, :], start=(j == 0 and c == 0), stop=j == T - 1, skip_group_check=True)
                        last.then_inc(free, 1)

            @block.gpsimd
            def _(pool):
                g = nc.gpsimd
                g.nop().then_inc(summed, 1)
                with pool.Fori(0, 2) as half:
                    with pool.Fori(0, H) as h:
                        p = H * half + h
                        rr = raw.rearrange("p t (k a d) -> p t k a d", k=2, a=2)
                        at = keep.adjd[:, bass.ds(half * HT, HT), bass.ds(h, 1), :].rearrange("p t a d -> p t (a d)")
                        link = chain(pool, pl, 6, p)
                        pool.wait_ge(evac, 2 * p + 4)
                        link(g.tensor_tensor(comb[:, :, 0], rr[:, :, 0, 0], rr[:, :, 0, 1], ALU.add), wait=False)
                        link(g.tensor_tensor(comb[:, :, 1], rr[:, :, 1, 0], rr[:, :, 1, 1], ALU.add))
                        g.nop().then_inc(summed, 1)
                        link(g.tensor_tensor(comb[:, :, 1], at, comb[:, :, 1], ALU.subtract))
                        ah = keep.a[:, bass.ds(h, 1), bass.ds(half * HT, HT)].rearrange("p a t -> p (a t)")
                        ch = keep.c[:, bass.ds(h, 1), bass.ds(half * HT, HT)].rearrange("p a t -> p (a t)")
                        link(g.tensor_tensor(comb[:, :, 0], comb[:, :, 0], bc(ah, HA), ALU.mult), wait=False)
                        link(g.tensor_tensor(comb[:, :, 1], comb[:, :, 1], bc(ch, HA), ALU.mult))
                        link(g.tensor_tensor(at, comb[:, :, 0], comb[:, :, 1], ALU.add))


def residual(nc, ctx, x, identity, keep, scratch_x1, yT, weights):
    sb = lambda n, s, d=FP32: ctx.enter_context(nc.sbuf_tensor(n, s, d))
    sem = lambda n: ctx.enter_context(nc.semaphore(n))
    B = 2
    NB = T // B
    PARTS = 4
    cut = [NB * n // PARTS * B for n in range(PARTS)] + [T]
    ident = sb("r_ident", [P, P])
    xs = sb("r_xs", [P, T, D])
    flag = sb("r_flag", [P, T, H])
    fall = sb("r_fall", [P, B, H, HA])
    rec = sb("r_rec", [P, T, H])
    hv = sb("r_hv", [P, T, D])
    ng = keep.xd[:].rearrange("p h t c -> p (h t c)").bitcast(FP32)[:, 0:T * D].rearrange("p (t d) -> p t d", d=D)
    st = sb("r_st", [P, T, 6])
    mv = sb("r_mv", [P, T, 2])
    rstd = sb("r_rstd", [P, T])
    SL = 4
    y = [sb(f"r_y{s}", [P, D]) for s in range(SL)]
    ps = weights.banks[0:SL]
    relu = sem("r_relu")
    in_id, zeroed, stored = sem("r_inid"), sem("r_z"), sem("r_stored")
    in_x = [sem(f"r_inx{n}") for n in range(PARTS)]
    fl, num, div, added, neg, ex, x1_done, stats, scales, std, y_done, tr, high, low = (
        sem("r_fl"), sem("r_num"), sem("r_div"), sem("r_added"), sem("r_neg"), sem("r_ex"), sem("r_x1"), sem("r_stats"), sem("r_scales"),
        sem("r_std"), sem("r_y"), sem("r_tr"), sem("r_high"), sem("r_low"))
    with nc.Block() as block:
        @block.sync
        def _(sp):
            for n in range(PARTS):
                if n == PARTS - 1:
                    sp.wait_ge(zeroed, 1)
                    sp.dma_start(xs[:, cut[n]:T - 1, :], x[cut[n] * P:(T - 1) * P, :].rearrange("(t p) d -> p t d", p=P)).then_inc(in_x[n], 16)
                    sp.dma_start(xs[0:LAST, T - 1, :], x[(T - 1) * P:N, :]).then_inc(in_x[n], 16)
                else:
                    sp.dma_start(xs[:, cut[n]:cut[n + 1], :], x[cut[n] * P:cut[n + 1] * P, :].rearrange("(t p) d -> p t d", p=P)).then_inc(in_x[n], 16)
            sp.dma_start(ident[:], identity).then_inc(in_id, 16)
            for n in range(PARTS):
                sp.wait_ge(x1_done, cut[n + 1] // B)
                sp.dma_start(scratch_x1[cut[n] * P:cut[n + 1] * P, :].rearrange("(t p) d -> p t d", p=P), xs[:, cut[n]:cut[n + 1], :]).then_inc(stored, 16)
            sp.wait_ge(stored, 16 * PARTS)
            sp.wait_ge(weights.loaded, weights.loads_count)

        @block.gpsimd
        def _(pool):
            g = nc.gpsimd
            g.tensor_scalar(flag[:], keep.adjd[:, :, :, HD], 0.0, None, ALU.is_equal).then_inc(fl, 1)
            pool.wait_ge(fl, 1)
            hsum = keep.hsum[:].rearrange("p (h d) -> p h d", h=H).unsqueeze(1).to_broadcast([P, B, H, HA])
            with pool.Fori(0, NB) as b:
                row = keep.adjd[:, bass.ds(B * b, B)]
                g.tensor_tensor(fall[:], hsum, bc(flag[:, bass.ds(B * b, B), :], HA), ALU.mult).then_inc(fl, 1)
                hold(pool, fl, b + 2)
                g.tensor_tensor(row, row, fall[:], ALU.add).then_inc(num, 1)
                hold(pool, num, b + 1)

        @block.vector
        def _(dve):
            v = nc.vector
            v.memset(xs[:, T - 1, :], 0.0).then_inc(zeroed, 1)

            def quotient(b):
                row = keep.adjd[:, bass.ds(B * b, B)].rearrange("p b h d -> p (b h) d")
                at = bass.ds(B * b, B)
                dve.wait_ge(num, b + 1)
                r = rec[:, at, :].rearrange("p b h -> p (b h)")
                v.reciprocal(r, row[:, :, HD]).then_inc(div, 1)
                dve.wait_ge(div, b + 1)
                h = hv[:, at, :].rearrange("p b d -> p (b d)")
                v.tensor_tensor(h.rearrange("p (u d) -> p u d", d=HD), row[:, :, 0:HD], bc(r, HD), ALU.mult).then_inc(neg, 1)

            def add(b):
                at = bass.ds(B * b, B)
                xt, h, e = (t[:, at, :].rearrange("p b d -> p (b d)") for t in (xs, hv, ng))
                dve.wait_ge(neg, b + 1)
                v.scalar_tensor_tensor(xt, h, 0.0, xt, ALU.max, ALU.add).then_inc(added, 1)
                dve.wait_ge(ex, b + 1)
                dve.wait_ge(added, b + 1)
                v.scalar_tensor_tensor(xt, e, -1.0, xt, ALU.add, ALU.add).then_inc(x1_done, 1)

            def moments(b):
                hold(dve, x1_done, b + 1)
                for n in range(B):
                    v.bn_stats(st[:, bass.ds(B * b + n, 1), :].rearrange("p a c -> p (a c)"),
                               xs[:, bass.ds(B * b + n, 1), :].rearrange("p a d -> p (a d)")).then_inc(stats, 1)

            quotient(0)
            for n in range(PARTS):
                dve.wait_ge(in_x[n], 32 if n == PARTS - 1 else 16)
                lo, hi = cut[n] // B, min(cut[n + 1] // B, NB - 1)
                with dve.Fori(lo, hi) as b:
                    quotient(b + 1)
                    add(b)
                    moments(b)
                if n < PARTS - 1:
                    weights.vector[n](dve)
            add(NB - 1)
            moments(NB - 1)
            weights.vector[PARTS - 1](dve)
            dve.wait_ge(stats, T)
            for t in range(T):
                last = v.bn_aggr(mv[:, t, :], st[:, t, :])
            last.then_inc(stats, 1)
            dve.wait_ge(stats, T + 1)
            v.tensor_scalar(rstd[:], mv[:, :, 1], EPS, None, ALU.add).then_inc(scales, 1)
            dve.wait_ge(std, 1)
            v.reciprocal(rstd[:], rstd[:]).then_inc(scales, 1)
            dve.wait_ge(scales, 2)

            def normal(t, s):
                dve.wait_ge(tr, t + 1)
                v.tensor_scalar(y[s][:], xs[:, bass.ds(t, 1), :].rearrange("p a d -> p (a d)"), mv[:, bass.ds(t, 1), 0],
                                rstd[:, bass.ds(t, 1)], ALU.subtract, ALU.mult).then_inc(y_done, 1)

            def lows(t, s):
                hold(dve, high, t + 1)
                v.tensor_tensor(yT[1][:, :, bass.ds(t * P, P)], ps[s][:, 0:D].rearrange("p (c n) -> p c n", c=KC),
                                yT[0][:, :, bass.ds(t * P, P)], ALU.subtract).then_inc(low, 1)
            for t in range(2):
                normal(t, t)
            with dve.Fori(0, (T - 2) // SL) as i:
                for s in range(SL):
                    normal(SL * i + s + 2, (s + 2) % SL)
                    lows(SL * i + s, s)
            for t in range(T - 2, T):
                lows(t, t % SL)

        @block.scalar
        def _(act):
            s_ = nc.scalar
            weights.loads(s_)

            def exponential(b):
                act.wait_ge(neg, b + 1)
                h, e = (t[:, bass.ds(B * b, B), :].rearrange("p b d -> p (b d)") for t in (hv, ng))
                s_.activation(e, h, ACT.Relu, scale=-1.0).then_inc(relu, 1)
                hold(act, relu, b + 1)
                s_.activation(e, e, ACT.Exp, scale=-1.0).then_inc(ex, 1)
            for n in range(PARTS):
                exponential(cut[n] // B)
                with act.Fori(cut[n] // B + 1, cut[n + 1] // B) as b:
                    exponential(b)
                if n == 0:
                    weights.scalar(act)
                if n == 1:
                    weights.scalar_queries(act)
            act.wait_ge(scales, 1)
            s_.activation(rstd[:], rstd[:], ACT.Sqrt).then_inc(std, 1)

            def highs(t, s):
                act.wait_ge(tr, t + SL + 1)
                s_.activation(yT[0][:, :, bass.ds(t * P, P)], ps[s][:, 0:D].rearrange("p (c n) -> p c n", c=KC), ACT.Copy).then_inc(high, 1)
            with act.Fori(0, T // SL) as i:
                for s in range(SL):
                    highs(SL * i + s, s)
            for t in range(T // SL * SL, T):
                highs(t, t % SL)

        @block.tensor
        def _(pe):
            t_ = nc.tensor
            weights.tensor(pe)
            pe.wait_ge(in_id, 16)
            pe.nop().then_inc(tr, SL)
            pe.nop().then_inc(low, SL)

            def transposes(t, s):
                pe.wait_ge(y_done, t + 1)
                pe.wait_ge(low, t + 1)
                for k in range(KC):
                    last = t_.transpose(ps[s][:, k * P:(k + 1) * P], y[s][:, k * P:(k + 1) * P], ident[:])
                last.then_inc(tr, 1)
            with pe.Fori(0, T // SL) as i:
                for s in range(SL):
                    transposes(SL * i + s, s)
            for t in range(T // SL * SL, T):
                transposes(t, t % SL)


class Keep:
    pass


PAIRS = 50
TOP = 16
KEYS = 128
QD = 128
HALF = QD // 2
G = 2
GT = G * P
NGRP = T // G
U = G * H
ROWS = [TOP // (i + 1) for i in range(TOP)]
AT = [sum(ROWS[:i]) for i in range(TOP)]
SLOTS = 23
BLK = 4
KT = 2
KR = 4 * SLOTS
EA, EB = 32, 8
QUAD = 4
WSCALE = 4096.0
LOW = -3.0e38


def slots():
    cells = [(i + 1, j + 1) for i in range(TOP) for j in range(ROWS[i])]

    def together(a, b):
        return a[0] * a[1] + b[0] * b[1] - min(a[0], b[0]) * min(a[1], b[1]) <= TOP
    near = [[k for k in range(PAIRS) if k != m and together(cells[m], cells[k])] for m in range(PAIRS)]
    slot = [-1] * PAIRS
    for _ in range(PAIRS):
        open_ = [m for m in range(PAIRS) if slot[m] < 0]
        used = {m: {slot[k] for k in near[m] if slot[k] >= 0} for m in open_}
        m = max(open_, key=lambda m: (len(used[m]), len(near[m]), -m))
        slot[m] = min(c for c in range(PAIRS) if c not in used[m])
    assert max(slot) < SLOTS
    return slot


def router_weights(nc, ctx, wq, bq, ln_g, ln_b, keys, down, identity, centre, own, k):
    sb = lambda n, s, d=FP32: ctx.enter_context(nc.sbuf_tensor(n, s, d))
    pb = lambda n, s, d=FP32: ctx.enter_context(nc.psum_tensor(n, s, d))
    sem = lambda n: ctx.enter_context(nc.semaphore(n))
    wn = sb("w_wn", [P, H, D])
    bt = sb("w_bt", [P, H])
    cm = sb("w_cm", [P, P])
    gb = sb("w_gb", [P, 2])
    kn = sb("w_kn", [P, 2, HALF])
    ksq = sb("w_ksq", [P, 2, HALF])
    kz = sb("w_kz", [P, 2, QD])
    nrm = sb("w_nrm", [P, 2])
    ones = sb("w_ones", [P, P])
    half = sb("w_half", [P, 2])
    tmp = sb("w_tmp", [P, 2])
    kt = sb("w_kt", [P, 2 * KEYS])
    bsel = sb("w_bsel", [P, H * (3 * H + 1)])
    kgf = sb("w_kgf", [P, 2 * KEYS])
    rqf = sb("w_rqf", [P, 2])
    kbh = sb("w_kbh", [3 * H, H, 2 * KEYS], FP16)
    kbl = sb("w_kbl", [3 * H, H, 2 * KEYS], FP16)
    low_row = sb("w_low", [3 * H, 2])
    dn = sb("w_dn", [P, KC, D])
    ps = [pb(f"w_ps{n}", [P, 512]) for n in range(8)]
    got_keys, mq, wide_high, wide_low = sem("w_gotkeys"), sem("w_mq"), sem("w_wideh"), sem("w_widel")
    got, zero, st, mm, sq, ev = (sem("w_got"), sem("w_zero"), sem("w_st"), sem("w_mm"), sem("w_sq"), sem("w_ev"))
    def loads(dma):
        dma.dma_start(k.ident[:], identity).then_inc(got_keys, 16)
        for n in range(2):
            dma.dma_start(kn[:, n, :], keys[n]).then_inc(got_keys, 16)
        dma.dma_start(gb[:, 0:1], ln_g.unsqueeze(1), allow_slow_non_contiguous=True).then_inc(got_keys, 16)
        dma.dma_start(gb[:, 1:2], ln_b.unsqueeze(1), allow_slow_non_contiguous=True).then_inc(got_keys, 16)
        dma.dma_start(wn[:], wq.rearrange("(h q) d -> q h d", q=QD)).then_inc(got, 16)
        dma.dma_start(bt[:], bq.rearrange("(h q) -> q h", q=QD), allow_slow_non_contiguous=True).then_inc(got, 16)
        dma.dma_start(cm[:], centre).then_inc(got, 16)
        dma.dma_start(dn[:], down[0:EA * EB, :].rearrange("(c p) d -> p c d", p=P)).then_inc(got, 16)
        dma.dma_start(k.own[:], own).then_inc(got, 16)

    link = chain(nc.vector, st)

    def keys_first(dve):
        v = nc.vector
        v.memset(ones[:], 1.0).then_inc(zero, 1)
        v.memset(kz[:], 0.0).then_inc(zero, 1)
        v.memset(half[:], 0.0).then_inc(zero, 1)
        v.memset(bsel[:], 0.0).then_inc(zero, 1)
        v.memset(low_row[:], 0.0).then_inc(zero, 1)
        v.memset(k.eps[:], EPS).then_inc(zero, 1)
        dve.wait_ge(zero, 6)
        v.memset(half[0:HALF, 0:1], 1.0).then_inc(zero, 1)
        v.memset(half[HALF:QD, 1:2], 1.0).then_inc(zero, 1)
        v.memset(k.rsq[:, 0:1], 1.0 / QD).then_inc(zero, 1)
        dve.wait_ge(zero, 9)
        dve.wait_ge(got_keys, 16 * 5)
        link(v.tensor_copy(k.ident16[:], k.ident[:]), wait=False)
        link(v.tensor_tensor(ksq[:], kn[:], kn[:], ALU.mult))
        link(v.tensor_reduce(nrm[:], ksq[:], AX.X, ALU.add))
        dve.wait_ge(sq, 1)
        link(v.tensor_scalar(nrm[:], nrm[:], 1e-12, None, ALU.max))
        link(v.reciprocal(nrm[:], nrm[:]))
        link(v.tensor_scalar(nrm[:], nrm[:], RSCALE, None, ALU.mult))
        for n in range(2):
            link(v.tensor_scalar(kz[:, n, n * HALF:(n + 1) * HALF], kn[:, n, :], nrm[:, n:n + 1], None, ALU.mult), wait=n == 1)
        for n in range(3):
            link(v.tensor_copy(bsel[:].rearrange("p (h x) -> p h x", h=H)[:, :, n * H], gb[:, 1:2].to_broadcast([P, H])), wait=False)
        link(v.tensor_reduce(low_row[:, 0:1], k.ident[0:3 * H, H:2 * H], AX.X, ALU.add))
        link(v.tensor_scalar(low_row[:, 1:2], low_row[:, 0:1], -1.0, 1.0, ALU.mult, ALU.add), wait=False)
        link(v.tensor_scalar(tmp[:], half[:], gb[:, 1:2], None, ALU.mult))
        link(v.tensor_scalar(rqf[:], tmp[:], gb[:, 0:1], 2.0, ALU.mult, ALU.mult))
        link(v.tensor_copy(k.rq[:, 0, :], rqf[:]))
        link(v.tensor_tensor(k.rq[:, 1, :], rqf[:], k.rq[:, 0, :], ALU.subtract), wait=False)
        link(v.tensor_scalar(k.rsq[:, 1:3], half[:], gb[:, 0:1], gb[:, 0:1], ALU.mult, ALU.mult), wait=False)
        link(v.tensor_scalar(tmp[:], tmp[:], gb[:, 1:2], None, ALU.mult))

    def keys_second(dve):
        v = nc.vector
        dve.wait_ge(mm, 2)
        link(v.tensor_copy(kt[:], ps[4][:, 0:2 * KEYS]))
        link(v.tensor_scalar(kgf[:], kt[:], gb[:, 0:1], None, ALU.mult))
        link(v.tensor_copy(k.kg[:, 0, :], kgf[:]))
        link(v.tensor_tensor(k.kg[:, 1, :], kgf[:], k.kg[:, 0, :], ALU.subtract))
        dve.wait_ge(mm, 3)
        v.tensor_copy(k.bsq[:], ps[5][:, 0:2]).then_inc(ev, 1)

    def shifts(dve):
        v = nc.vector
        dve.wait_ge(mm, 4)
        for n in range(4):
            two = lambda t: t[:, 2 * n:2 * n + 2, :].rearrange("p h k -> p (h k)")
            link(v.tensor_copy(two(kbh), ps[n][0:3 * H, :]))
            v.tensor_tensor(two(kbl), ps[n][0:3 * H, :], two(kbh), ALU.subtract).then_inc(ev, 1)
        dve.wait_ge(ev, 5)
        link(v.tensor_scalar(kbl[:], kbl[:], low_row[:, 0:1], None, ALU.mult))
        link(v.scalar_tensor_tensor(k.kb[:], kbh[:], low_row[:, 1:2], kbl[:], ALU.mult, ALU.add), wait=False)

    wide = lambda part, n: k.wq[part][:, n // 2, (n % 2) * 512:(n % 2 + 1) * 512]
    rows = lambda c: ps[6 + c][:, 0:D].rearrange("p (a b) -> p b a", b=EB)

    def queries(dve):
        v = nc.vector
        for n in range(4):
            dve.wait_ge(wide_high, n + 1)
            v.scalar_tensor_tensor(wide(1, n), ps[n][:], RSCALE, wide(0, n), ALU.mult, ALU.subtract).then_inc(wide_low, 1)
        for n in range(KC * QUAD):
            c, q = n // QUAD, n % QUAD
            dve.wait_ge(wide_high, 5 + QUAD * (c + 1))
            v.scalar_tensor_tensor(k.down[1][:, c, :, :, q], rows(c), RSCALE, k.down[0][:, c, :, :, q],
                                   ALU.mult, ALU.subtract).then_inc(wide_low, 1)

    def scalar_queries(act):
        s_ = nc.scalar
        act.wait_ge(mq, 2)
        for n in range(4):
            s_.activation(wide(0, n), ps[n][:], ACT.Copy, scale=RSCALE).then_inc(wide_high, 1)
        s_.activation(k.bq[:], ps[5][:, 0:H], ACT.Copy).then_inc(wide_high, 1)
        for n in range(KC * QUAD):
            c, q = n // QUAD, n % QUAD
            s_.activation(k.down[0][:, c, :, :, q], rows(c), ACT.Copy, scale=RSCALE).then_inc(wide_high, 1)

    def scalar(act):
        act.wait_ge(st, 3)
        nc.scalar.activation(nrm[:], nrm[:], ACT.Sqrt).then_inc(sq, 1)

    def tensor(pe):
        t_ = nc.tensor
        pe.wait_ge(got, 16 * 5)
        pe.wait_ge(got_keys, 16 * 5)
        for h in range(H):
            for c in range(KC):
                last = t_.matmul(ps[2 * c + h // 4][:, (h % 4) * P:(h % 4 + 1) * P], wn[:, h, c * P:(c + 1) * P], cm[:],
                                 start=True, stop=True)
        last.then_inc(mq, 1)
        t_.matmul(ps[5][:, 0:H], cm[:], bt[:], start=True, stop=True)
        for c in range(KC):
            for e in range(KC):
                last = t_.transpose(ps[6 + c][:, e * P:(e + 1) * P], dn[:, e, c * P:(c + 1) * P], k.ident[:])
        last.then_inc(mq, 1)
        pe.wait_ge(zero, 9)
        pe.wait_ge(st, 19)
        for n in range(2):
            t_.transpose(ps[4][:, n * KEYS:(n + 1) * KEYS], kz[:, n, :], k.ident[:]).then_inc(mm, 1)
        pe.wait_ge(wide_high, 5)
        t_.matmul(ps[5][:, 0:2], ones[:], tmp[:], start=True, stop=True).then_inc(mm, 1)
        pe.wait_ge(st, 20)
        pe.wait_ge(wide_low, 4)
        for h in range(H):
            last = t_.matmul(ps[h // 2][0:3 * H, (h % 2) * 256:(h % 2 + 1) * 256], bsel[:, 3 * H * h:3 * H * (h + 1)], kt[:],
                             start=True, stop=True)
        last.then_inc(mm, 1)

    steps = Keep()
    steps.loads, steps.scalar, steps.tensor = loads, scalar, tensor
    steps.scalar_queries = scalar_queries
    steps.vector = (keys_first, queries, keys_second, shifts)
    steps.loaded, steps.loads_count, steps.banks = got, 16 * 5, ps
    return steps


def experts(nc, yT, scratch_x1, merge, up, k, out):
    with ExitStack() as ctx:
        sb = lambda n, s, d=FP32: ctx.enter_context(nc.sbuf_tensor(n, s, d))
        pb = lambda n, s, d=FP32: ctx.enter_context(nc.psum_tensor(n, s, d))
        sem = lambda n: ctx.enter_context(nc.semaphore(n))
        qT = sb("f_qT", [P, H, GT])
        qq = sb("f_qq", [P, H, GT])
        qh = sb("f_qh", [P, H, GT], FP16)
        ql = sb("f_ql", [P, H, GT], FP16)
        stdx = sb("f_stdx", [P, G, 3 * H], FP16)
        stdT = sb("f_stdT", [3 * H, GT], FP16)
        stt = sb("f_stt", [P, U, 5])
        facn = sb("f_facn", [P, U, 2])
        std = sb("f_std", [P, U])
        fac = sb("f_fac", [P, U, 2])
        fa2 = sb("f_fa2", [P, U, 2])
        z = sb("f_z", [P, U, 2 * KEYS])
        zr = sb("f_zr", [P, 2, 2 * KEYS])
        top = sb("f_top", [P, U, 2, TOP])
        idx = sb("f_idx", [P, U, 2, TOP], U16)
        sc = sb("f_sc", [P, U, 2, TOP])
        ixf = sb("f_ixf", [P, U, 2, TOP])
        cand = sb("f_cand", [P, U, PAIRS])
        ecand = sb("f_ecand", [P, U, PAIRS])
        cr1 = sb("f_cr1", [P, U, PAIRS])
        cr2 = sb("f_cr2", [P, U, PAIRS])
        best = sb("f_best", [P, U, TOP])
        be = sb("f_be", [P, U, TOP])
        zsum = sb("f_zsum", [P, U])
        wgt = cr1
        wm = sb("f_wm", [P, U, PAIRS])
        kept = wm
        em = sb("f_em", [P, U, PAIRS], FP16)
        wT = sb("f_wT", [2 * PAIRS, BLK, GT])
        eT = sb("f_eT", [2 * PAIRS, BLK, GT], FP16)
        mg = sb("f_mg", [2 * PAIRS, 2, KR])
        mg16 = sb("f_mg16", [2 * PAIRS, 2, KR], FP16)
        wh = sb("f_wh", [KR, KT * GT], FP16)
        wl = sb("f_wl", [KR, KT * GT], FP16)
        eu = sb("f_eu", [KR, KT * GT], U16)
        ea = sb("f_ea", [KR, KT * GT], U16)
        eb = sb("f_eb", [KR, KT * GT], U16)
        oa = sb("f_oa", [KR, KT * GT // QUAD, EA, QUAD], FP16)
        ob = sb("f_ob", [KR, EB, KT * GT], FP16)
        wob = [sb("f_wob0", [KR, EB, KT * GT], FP16), ob]
        hh = sb("f_hh", [P, G, EB, P])
        x1 = sb("f_x1", [P, G, D])
        res = sb("f_res", [P, G, D])
        ps_q = [pb(f"f_psq{n}", [P, 512]) for n in range(2)]
        ps_z = [pb(f"f_psz{n}", [P, 512]) for n in range(2)]
        ps_s = pb("f_pss", [P, 512])
        ps_b = [pb(f"f_psb{n}", [P, 512]) for n in range(3)]
        S_ = {n: sem("f_" + n) for n in (
            "q_mm", "q_out", "stdx", "stdxT", "stdT", "stats", "std", "statsd", "fac", "facd", "qls", "ones0", "eud", "wlow", "inverted", "z_mm", "z_out", "z_free", "fstep", "tstep",
            "top", "pool", "sums", "sel", "arg", "expd", "wgtd", "masked", "mstep", "tr", "trout", "mrg", "whd",
            "oh", "ostep", "sct", "prod", "fin", "inner", "gelu", "res", "resd", "mgd")}
        in_up = sem("f_inup")
        in_x1, in_mg = [sem("f_inx0"), sem("f_inx1")], sem("f_inmg")
        put = [sem("f_put0"), sem("f_put1")]

        with nc.Block() as block:
            @block.sync
            def _(sp):
                sp.dma_start(mg[:], merge).then_inc(in_mg, 16)
                for q in range(QUAD):
                    sp.dma_start(k.up[q:P:QUAD], up[0:EA * EB, :].rearrange("(a b) o -> a b o", b=EB)).then_inc(in_up, 16)
                for t in range(G):
                    sp.nop().then_inc(put[t], 16)

                def turn(g, rows):
                    for t in range(G):
                        sp.wait_ge(put[t], 16 * g + 16)
                        sp.dma_start(x1[:, t, :], scratch_x1[bass.ds((g * G + t) * P, P), :]).then_inc(in_x1[t], 16)
                    for t in range(G):
                        sp.wait_ge(S_["resd"], G * g + G + t + 1)
                        n = rows if t == G - 1 else P
                        sp.dma_start(out[bass.ds((g * G + t) * P, n), :], x1[0:n, t, :]).then_inc(put[t], 16)
                with sp.Fori(0, NGRP - 1) as g:
                    turn(g, P)
                turn(NGRP - 1, LAST)
                for t in range(G):
                    sp.wait_ge(put[t], 16 * NGRP + 16)

            @block.tensor
            def _(pe):
                t_ = nc.tensor

                def queries(g):
                    for h in range(H):
                        n = h % 2
                        pe.wait_ge(S_["q_out"], 3 * (H * g + h) + 3)
                        for c in range(KC):
                            last = split_product(nc, ps_q[n][:, 0:GT], [w[:, c, h * QD:(h + 1) * QD] for w in k.wq],
                                         [y[:, c, bass.ds(g * GT, GT)] for y in yT], c == 0, c == KC - 1)
                        last.then_inc(S_["q_mm"], 1)

                def statistics(g):
                    pe.wait_ge(S_["q_out"], 3 * H * (g + 1) + 6)
                    pe.wait_ge(S_["statsd"], g + 1)
                    for t in range(G):
                        for h in range(H):
                            at = 5 * (t * H + h)
                            t_.matmul(ps_s[:, at + 2:at + 5], qq[:, h, t * P:(t + 1) * P], k.rsq[:], start=True, stop=True)
                    pe.wait_ge(S_["qls"], 2 * (g + 1))
                    for t in range(G):
                        for h in range(H):
                            at = 5 * (t * H + h)
                            last = split_product(nc, ps_s[:, at:at + 2], [q[:, h, t * P:(t + 1) * P] for q in (qh, ql)],
                                         [k.rq[:, 0, :], k.rq[:, 1, :]], True, True)
                    last.then_inc(S_["stats"], 1)

                def deviations(g):
                    pe.wait_ge(S_["stdx"], g + 1)
                    for t in range(G):
                        last = t_.transpose(ps_s[0:3 * H, KEYS:].bitcast(FP16)[:, t * P:(t + 1) * P], stdx[:, t, :], k.ident16[:])
                    last.then_inc(S_["stdxT"], 1)

                def scores(g):
                    pe.wait_ge(S_["stdT"], g + 1)
                    for t in range(G):
                        for h2 in range(H // 2):
                            n = h2 % 2
                            pe.wait_ge(S_["z_out"], H * g + 4 * t + h2 + 1)
                            for h in (2 * h2, 2 * h2 + 1):
                                o = ps_z[n][:, (h % 2) * 256:(h % 2 + 1) * 256]
                                split_product(nc, o, [q[:, h, t * P:(t + 1) * P] for q in (qh, ql)], [k.kg[:, 0, :], k.kg[:, 1, :]], True, False)
                                last = t_.matmul(o, stdT[:, t * P:(t + 1) * P], k.kb[:, h, :], start=False, stop=True)
                            last.then_inc(S_["z_mm"], 1)

                def transposes(g):
                    pe.wait_ge(S_["masked"], 2 * (g + 1))
                    pe.wait_ge(S_["res"], G * g + G)
                    for t in range(G):
                        for b in range(BLK):
                            n = t * BLK + b
                            src = wm[:, t * H + 2 * b:t * H + 2 * b + 2, :].rearrange("p h c -> p (h c)")
                            t_.transpose(ps_b[n // 4][0:2 * PAIRS, (n % 4) * P:(n % 4 + 1) * P], src, k.ident[:])
                    for t in range(G):
                        for b in range(BLK):
                            n = t * BLK + b
                            src = em[:, t * H + 2 * b:t * H + 2 * b + 2, :].rearrange("p h c -> p (h c)")
                            last = t_.transpose(ps_b[2][0:2 * PAIRS, :].bitcast(FP16)[:, n * P:(n + 1) * P], src, k.ident16[:])
                    last.then_inc(S_["tr"], 1)

                def merges(g):
                    pe.wait_ge(S_["trout"], 3 * (g + 1))
                    for kt in range(KT):
                        for n in range(2):
                            t_.matmul(ps_b[0][0:KR, kt * GT:(kt + 1) * GT], mg[:, n, :], wT[:, 2 * kt + n, :], start=n == 0, stop=n == 1)
                    for kt in range(KT):
                        for n in range(2):
                            last = t_.matmul(ps_b[1][0:KR, kt * GT:(kt + 1) * GT], mg16[:, n, :], eT[:, 2 * kt + n, :],
                                             start=n == 0, stop=n == 1)
                    last.then_inc(S_["mrg"], 1)

                def inner(g):
                    for r in range(EB // 2):
                        n = r % 2
                        pe.wait_ge(S_["gelu"], QUAD * (4 * g + r) + QUAD)
                        for b in (2 * r, 2 * r + 1):
                            for c in range(KC):
                                last = split_product(nc, ps_q[n][:, (b % 2) * GT:(b % 2 + 1) * GT],
                                             [w[:, c, b].rearrange("p a g -> p (a g)") for w in k.down],
                                             [y[:, c, bass.ds(g * GT, GT)] for y in yT], c == 0, c == KC - 1)
                        last.then_inc(S_["inner"], 1)

                HALF_G = P // QUAD // 2

                def scatter(g):
                    pe.wait_ge(S_["oh"], g + 1)
                    pe.wait_ge(S_["wlow"], g + 1)
                    for q in range(2 * G):
                        bank = ps_b[q % 3]
                        if q == 3:
                            pe.wait_ge(S_["prod"], 2 * G * g + 2 * G + 1)
                        for m in range(HALF_G):
                            tok = (q // 2) * P + (q % 2) * (P // 2) + m * QUAD
                            for kt in range(KT):
                                for part in range(2):
                                    at = kt * GT + tok
                                    last = t_.matmul(bank[:].rearrange("p (b m g) -> p b m g", b=EB, g=QUAD)[:, :, m, :],
                                                     oa[:, at // QUAD].rearrange("p a g -> p (a g)"),
                                                     wob[part][:, :, at:at + QUAD],
                                                     start=kt == 0 and part == 0, stop=kt == KT - 1 and part == 1)
                        last.then_inc(S_["sct"], 1)

                def final(g):
                    for t in range(G):
                        pe.wait_ge(S_["prod"], 2 * G * g + 2 * G + (2, 4)[t])
                        for b in range(EB):
                            last = t_.matmul(ps_b[1 + t][:, 0:D],
                                             hh[:, t, b, :], k.up[:, b, :], start=b == 0, stop=b == EB - 1)
                        last.then_inc(S_["fin"], 1)

                def turn(g, more=True):
                    pe.wait_ge(S_["gelu"], QUAD * 4 * g + 2 * QUAD)
                    if more:
                        queries(g + 2)
                    transposes(g)
                    if more:
                        statistics(g + 2)
                    merges(g)
                    if more:
                        deviations(g + 2)
                    inner(g)
                    if more:
                        scores(g + 2)
                    scatter(g)
                    final(g)
                pe.nop().then_inc(S_["q_out"], 6)
                pe.nop().then_inc(S_["z_out"], 2)
                pe.nop().then_inc(S_["gelu"], 2 * QUAD)
                pe.wait_ge(S_["mgd"], 1)
                for g in range(2):
                    queries(g)
                    statistics(g)
                    deviations(g)
                    scores(g)
                pe.wait_ge(in_up, 16 * QUAD)
                with pe.Fori(0, NGRP - 2) as g:
                    turn(g)
                turn(NGRP - 2, False)
                turn(NGRP - 1, False)

            @block.scalar
            def _(act):
                s_ = nc.scalar

                def queries(g):
                    for h in range(H):
                        n = h % 2
                        act.wait_ge(S_["q_mm"], H * g + h + 1)
                        if h == 0:
                            act.wait_ge(S_["z_mm"], H * g + H)
                        for dst, f in ((qh, ACT.Identity), (qT, ACT.Identity), (qq, ACT.Square)):
                            s_.activation(dst[:, h, :], ps_q[n][:, 0:GT], f, bias=k.bq[:, h:h + 1], scale=1.0 / RSCALE).then_inc(S_["q_out"], 1)

                def statistics(g):
                    act.wait_ge(S_["stats"], g + 1)
                    s_.activation(stt[:].rearrange("p u c -> p (u c)"), ps_s[:, 0:5 * U], ACT.Copy)
                    s_.activation(std[:], ps_s[:, 0:5 * U].rearrange("p (u c) -> p u c", c=5)[:, :, 2], ACT.Sqrt,
                                  bias=k.eps[:, :]).then_inc(S_["std"], 1)
                    act.nop().then_inc(S_["statsd"], 1)

                def deviations(g):
                    act.wait_ge(S_["stdxT"], g + 1)
                    s_.activation(stdT[:], ps_s[0:3 * H, KEYS:].bitcast(FP16)[:, 0:GT], ACT.Copy).then_inc(S_["stdT"], 1)
                    act.wait_ge(S_["fac"], g + 1)
                    s_.activation(facn[:], facn[:], ACT.Sqrt, scale=RSCALE * RSCALE).then_inc(S_["facd"], 1)

                def scores(g):
                    for t in range(G):
                        for h2 in range(H // 2):
                            n = h2 % 2
                            at = 4 * t + h2
                            act.wait_ge(S_["z_mm"], H * g + H + at + 1)
                            act.wait_ge(S_["z_free"], H * g + at + 1)
                            s_.activation(z[:, 2 * at:2 * at + 2, :].rearrange("p u c -> p (u c)"), ps_z[n][:], ACT.Copy).then_inc(S_["z_out"], 1)

                def results(g):
                    for t in range(G):
                        act.wait_ge(S_["fin"], G * g + t + 1)
                        act.wait_ge(S_["resd"], G * g + t + 1)
                        s_.activation(res[:, t, :], ps_b[1 + t][:, 0:D], ACT.Copy).then_inc(S_["res"], 1)

                def weights(g):
                    act.wait_ge(S_["arg"], 2 * g + 1)
                    s_.activation(be[:], be[:], ACT.Exp).then_inc(S_["expd"], 1)
                    act.wait_ge(S_["arg"], 2 * g + 2)
                    s_.activation(wgt[:], wgt[:], ACT.Exp).then_inc(S_["expd"], 1)

                def transposed(g):
                    act.wait_ge(S_["tr"], g + 1)
                    for t in range(G):
                        s_.activation(wT[:, :, t * P:(t + 1) * P], ps_b[t][0:2 * PAIRS, :].rearrange("p (b n) -> p b n", b=BLK),
                                      ACT.Copy).then_inc(S_["trout"], 1)
                    s_.activation(eT[:].rearrange("p b (t n) -> p t b n", t=G),
                                  ps_b[2][0:2 * PAIRS, :].bitcast(FP16).rearrange("p (t b n) -> p t b n", t=G, b=BLK),
                                  ACT.Copy).then_inc(S_["trout"], 1)

                def merged(g):
                    act.wait_ge(S_["mrg"], g + 1)
                    s_.activation(wh[:], ps_b[0][0:KR, :], ACT.Copy).then_inc(S_["whd"], 1)
                    s_.activation(eu[:], ps_b[1][0:KR, :], ACT.Copy).then_inc(S_["eud"], 1)

                def inner(g):
                    act.wait_ge(S_["prod"], 2 * G * g + 4)
                    for r in range(EB // 2):
                        n = r % 2
                        act.wait_ge(S_["inner"], 4 * g + r + 1)
                        for q in range(QUAD):
                            src = ps_q[n][:].rearrange("p (b m g) -> p b m g", b=2, g=QUAD)[:, :, :, q]
                            dst = k.acts[:, 2 * r:2 * r + 2, :, q]
                            s_.activation(dst, src, ACT.Gelu, scale=k.own[:, q:q + 1]).then_inc(S_["gelu"], 1)
                act.nop().then_inc(S_["z_mm"], H)
                act.nop().then_inc(S_["statsd"], 1)
                act.nop().then_inc(S_["prod"], 4)
                act.nop().then_inc(S_["res"], G)
                for g in range(2):
                    queries(g)
                    statistics(g)
                    deviations(g)
                    scores(g)
                weights(0)
                with act.Fori(0, NGRP - 2) as g:
                    queries(g + 2)
                    transposed(g)
                    statistics(g + 2)
                    merged(g)
                    deviations(g + 2)
                    inner(g)
                    scores(g + 2)
                    weights(g + 1)
                    results(g)
                for g in (NGRP - 2, NGRP - 1):
                    transposed(g)
                    merged(g)
                    inner(g)
                    if g == NGRP - 2:
                        weights(g + 1)
                    results(g)

            @block.vector
            def _(dve):
                v = nc.vector

                def topk(g, pairs):
                    for m in pairs:
                        hold(dve, S_["z_out"], H * g + m + 3)
                        halves = [(2 * m + s, s, n) for s in range(2) for n in range(2)]
                        base = 6 * U * g + 12 * m
                        zz = lambda u, s, n: z[:, u, n * KEYS:(n + 1) * KEYS]
                        zq = lambda u, s, n: zr[:, s, n * KEYS:(n + 1) * KEYS]
                        hi = lambda u, n: top[:, u, n, 0:8]
                        lo = lambda u, n: top[:, u, n, 8:16]
                        for u, s, n in halves:
                            v.max(hi(u, n), zz(u, s, n)).then_inc(S_["tstep"], 1)
                        for u, s, n in halves:
                            if n == 0:
                                hold(dve, S_["tstep"], base + 2 * s + 2)
                            v.match_replace(zq(u, s, n), hi(u, n), zz(u, s, n), LOW).then_inc(S_["tstep"], 1)
                        for u, s, n in halves:
                            if n == 0:
                                hold(dve, S_["tstep"], base + 2 * s + 6)
                            v.max(lo(u, n), zq(u, s, n)).then_inc(S_["tstep"], 1)
                        for u, s, n in halves:
                            last = v.max_index(idx[:, u, n, 0:8], hi(u, n), zz(u, s, n))
                        last.then_inc(S_["z_free"], 1)
                        hold(dve, S_["tstep"], base + 12)
                        for u, s, n in halves:
                            last = v.max_index(idx[:, u, n, 8:16], lo(u, n), zq(u, s, n))
                    if m == U // 2 - 1:
                        last.then_inc(S_["top"], 1)

                def invert(g):
                    dve.wait_ge(S_["facd"], g + 1)
                    v.reciprocal(fac[:], facn[:]).then_inc(S_["inverted"], 1)

                def select(g, more=True):
                    hold(dve, S_["sums"], 2 * (g + 1))
                    if more:
                        invert(g + 1)
                    for q in range(4):
                        for u in range(U):
                            if q and u % (U // 2) == 0:
                                hold(dve, S_["sel"], 4 * U * g + (q - 1) * U + u + U // 2)
                            if q == 0:
                                ins = v.max(best[:, u, 0:8], cand[:, u, :])
                            elif q == 1:
                                ins = v.match_replace(cr1[:, u, :], best[:, u, 0:8], cand[:, u, :], LOW)
                            elif q == 2:
                                ins = v.max(best[:, u, 8:16], cr1[:, u, :])
                            else:
                                ins = v.match_replace(cr2[:, u, :], best[:, u, 8:16], cr1[:, u, :], LOW)
                            ins.then_inc(S_["sel"], 1)

                def totals(g, step):
                    if step == 0:
                        dve.wait_ge(S_["expd"], 2 * g + 1)
                        v.tensor_reduce(zsum[:], be[:], AX.X, ALU.add).then_inc(S_["mstep"], 1)
                    elif step == 1:
                        dve.wait_ge(S_["mstep"], 3 * g + 1)
                        v.reciprocal(zsum[:], zsum[:]).then_inc(S_["mstep"], 1)
                    else:
                        dve.wait_ge(S_["mstep"], 3 * g + 2)
                        v.tensor_scalar(zsum[:], zsum[:], WSCALE, None, ALU.mult).then_inc(S_["mstep"], 1)

                def onehots(g):
                    lk = chain(dve, S_["ostep"], 3 + EB, g)
                    dve.wait_ge(S_["whd"], g + 1)
                    dve.wait_ge(S_["eud"], g + 1)
                    lk(v.tensor_scalar(eb[:], eu[:], EB - 1, None, ALU.bitwise_and), wait=False)
                    lk(v.tensor_scalar(ea[:], eu[:], 3, None, ALU.logical_shift_right), wait=False)
                    lk(v.tensor_tensor(wl[:], ps_b[0][0:KR, :], wh[:], ALU.subtract))
                    for b in range(EB):
                        lk(v.tensor_scalar(ob[:, b, :], eb[:], float(b), None, ALU.is_equal), wait=b == EB - 1)
                    v.tensor_tensor(wob[0][:], ob[:], wh[:].unsqueeze(1).to_broadcast([KR, EB, KT * GT]), ALU.mult).then_inc(S_["ones0"], 1)
                    for a in range(EA):
                        last = v.tensor_scalar(oa[:, :, a, :], ea[:].rearrange("p (m g) -> p m g", g=QUAD), float(a), None, ALU.is_equal)
                    last.then_inc(S_["oh"], 1)

                HALF_G = P // QUAD // 2

                def products(g):
                    dve.wait_ge(S_["gelu"], QUAD * (4 * g + 4) + 2 * QUAD)
                    for q in range(2 * G):
                        t, n = q // 2, q % 2
                        dve.wait_ge(S_["sct"], 2 * G * g + q + 1)
                        at = t * (P // QUAD) + n * HALF_G
                        v.scalar_tensor_tensor(hh[:, t, :, n * (P // 2):(n + 1) * (P // 2)],
                                               ps_b[q % 3][:].rearrange("p (b n) -> p b n", b=EB), 1.0 / WSCALE,
                                               k.acts[:, :, at:at + HALF_G].rearrange("p b m g -> p b (m g)"),
                                               ALU.mult, ALU.mult).then_inc(S_["prod"], 1)

                v.nop().then_inc(S_["z_free"], H)
                dve.wait_ge(in_mg, 16)
                v.tensor_copy(mg16[:], mg[:]).then_inc(S_["mgd"], 1)
                invert(0)
                topk(0, range(U // 2))
                select(0)

                def turn(g, first=False, more=True):
                    topk(g + 1, range(0, 1))
                    totals(g, 0)
                    if not first:
                        products(g - 1)
                    totals(g, 1)
                    topk(g + 1, range(1, 2))
                    totals(g, 2)
                    topk(g + 1, range(2, U // 2))
                    onehots(g)
                    select(g + 1, more)
                turn(0, first=True)
                with dve.Fori(1, NGRP - 2) as g:
                    turn(g)
                turn(NGRP - 2, more=False)
                totals(NGRP - 1, 0)
                products(NGRP - 2)
                totals(NGRP - 1, 1)
                totals(NGRP - 1, 2)
                onehots(NGRP - 1)
                products(NGRP - 1)

            @block.gpsimd
            def _(pool):
                g_ = nc.gpsimd

                def prepare(g):
                    for n in range(2):
                        hs = slice(n * H // 2, (n + 1) * H // 2)
                        hold(pool, S_["q_out"], 3 * (H * g + (n + 1) * H // 2) + 6)
                        g_.tensor_tensor(ql[:, hs, :], qT[:, hs, :], qh[:, hs, :], ALU.subtract).then_inc(S_["qls"], 1)
                    lk = chain(pool, S_["fstep"], 9, g)
                    hold(pool, S_["std"], g + 1)
                    byh = std[:].rearrange("p (t h) -> p t h", t=G)
                    lk(g_.tensor_copy(stdx[:, :, 0:2 * H].rearrange("p t (n h) -> p t n h", n=2),
                                      byh.unsqueeze(2).to_broadcast([P, G, 2, H])))
                    g_.tensor_tensor(stdx[:, :, 2 * H:], byh, stdx[:, :, 0:H], ALU.subtract).then_inc(S_["stdx"], 1)
                    sdb = bc(std[:], 2)
                    lk(g_.tensor_tensor(fa2[:], sdb, k.bsq[:].unsqueeze(1).to_broadcast([P, U, 2]), ALU.mult))
                    lk(g_.tensor_tensor(fa2[:], fa2[:], stt[:, :, 0:2], ALU.add))
                    lk(g_.tensor_tensor(fa2[:], fa2[:], sdb, ALU.mult))
                    lk(g_.tensor_tensor(facn[:], fa2[:], stt[:, :, 3:5], ALU.add))
                    lk(g_.tensor_scalar(fa2[:], sdb, 1e-12, None, ALU.mult))
                    lk(g_.tensor_tensor(fa2[:], fa2[:], fa2[:], ALU.mult))
                    lk(g_.tensor_tensor(facn[:], facn[:], fa2[:], ALU.subtract))
                    lk(g_.tensor_scalar(facn[:], facn[:], 0.0, None, ALU.max))
                    g_.tensor_tensor(facn[:], facn[:], fa2[:], ALU.add).then_inc(S_["fac"], 1)

                def sums(g):
                    lk = chain(pool, S_["pool"], 2, g)
                    hold(pool, S_["top"], g + 1)
                    hold(pool, S_["inverted"], g + 1)
                    lk(g_.tensor_copy(ixf[:], idx[:]), wait=False)
                    lk(g_.tensor_tensor(sc[:], top[:], bc(fac[:], TOP), ALU.mult))
                    for dst, src in ((cand, sc), (ecand, ixf)):
                        last = None
                        i = 0
                        while i < TOP:
                            m = ROWS[i]
                            n = sum(1 for r in ROWS if r == m)
                            o = dst[:, :, AT[i]:AT[i] + n * m].rearrange("p u (n m) -> p u n m", m=m)
                            last = g_.tensor_tensor(o, src[:, :, 0, i:i + n].unsqueeze(3).to_broadcast([P, U, n, m]),
                                                    src[:, :, 1, 0:m].unsqueeze(2).to_broadcast([P, U, n, m]), ALU.add)
                            i += n
                        last.then_inc(S_["sums"], 1)

                def low_weights(g):
                    hold(pool, S_["ones0"], g + 1)
                    g_.tensor_tensor(ob[:], ob[:], wl[:].unsqueeze(1).to_broadcast([KR, EB, KT * GT]), ALU.mult).then_inc(S_["wlow"], 1)

                def arguments(g):
                    pool.wait_ge(S_["sel"], 4 * U * (g + 1))
                    mx = best[:, :, 0]
                    g_.tensor_tensor(be[:], best[:], bc(mx, TOP), ALU.subtract).then_inc(S_["arg"], 1)
                    g_.tensor_tensor(wgt[:], cand[:], bc(mx, PAIRS), ALU.subtract).then_inc(S_["arg"], 1)

                def normalise(g):
                    pool.wait_ge(S_["expd"], 2 * (g + 1))
                    hold(pool, S_["mstep"], 3 * (g + 1))
                    g_.tensor_scalar(kept[:], cr2[:], LOW / 2, None, ALU.is_lt).then_inc(S_["wgtd"], 1)
                    g_.tensor_tensor(wgt[:], wgt[:], bc(zsum[:], PAIRS), ALU.mult).then_inc(S_["wgtd"], 1)
                    hold(pool, S_["wgtd"], 2 * g + 1)
                    g_.tensor_tensor(em[:], kept[:], ecand[:], ALU.mult).then_inc(S_["masked"], 1)
                    hold(pool, S_["wgtd"], 2 * g + 2)
                    hold(pool, S_["masked"], 2 * g + 1)
                    g_.tensor_tensor(wm[:], kept[:], wgt[:], ALU.mult).then_inc(S_["masked"], 1)

                def results(g):
                    for t in range(G):
                        pool.wait_ge(S_["res"], G * g + G + t + 1)
                        hold(pool, in_x1[t], 16 * (g + 1))
                        g_.tensor_tensor(x1[:, t, :], res[:, t, :], x1[:, t, :], ALU.add).then_inc(S_["resd"], 1)

                def turn(g, first=False, more=True):
                    normalise(g)
                    if not first:
                        results(g - 1)
                    if more:
                        prepare(g + 2)
                    sums(g + 1)
                    low_weights(g)
                    arguments(g + 1)
                g_.nop().then_inc(S_["resd"], G)
                prepare(0)
                pool.wait_ge(S_["inverted"], 1)
                prepare(1)
                sums(0)
                arguments(0)
                turn(0, first=True)
                with pool.Fori(1, NGRP - 2) as g:
                    turn(g)
                turn(NGRP - 2, more=False)
                normalise(NGRP - 1)
                results(NGRP - 2)
                low_weights(NGRP - 1)
                results(NGRP - 1)


def program(nc, x, adj, w, wb, a, wq, bq, ln_g, ln_b, keys0, keys1, down, up, identity, centre, own, merge, out):
    with ExitStack() as ctx:
        scratch_u = nc.dram_tensor("scratch_u", [2, H, HN], FP32, kind="Internal").ap()
        scratch_x = nc.dram_tensor("scratch_x", [H, P, 2, T, 2 * HA], FP16, kind="Internal").ap()
        scratch_x1 = nc.dram_tensor("scratch_x1", [NP, D], FP32, kind="Internal").ap()
        yT = [ctx.enter_context(nc.sbuf_tensor(f"yT{n}", [P, KC, NP], FP16)) for n in range(2)]
        sb = lambda n, s, d=FP32: ctx.enter_context(nc.sbuf_tensor(n, s, d))
        k = Keep()
        k.ident = sb("ident", [P, P])
        k.ident16 = sb("ident16", [P, P], FP16)
        k.wq = [sb(f"wqT{n}", [P, KC, H * QD], FP16) for n in range(2)]
        k.bq = sb("bqc", [P, H])
        k.kg = sb("kg", [P, 2, 2 * KEYS], FP16)
        k.kb = sb("kb", [3 * H, H, 2 * KEYS], FP16)
        k.rq = sb("rq", [P, 2, 2], FP16)
        k.rsq = sb("rsq", [P, 3])
        k.bsq = sb("bsq", [P, 2])
        k.eps = sb("eps", [P, 1])
        k.own = sb("own", [P, QUAD])
        k.down = [sb(f"downT{n}", [P, KC, EB, EA, QUAD], FP16) for n in range(2)]
        with ExitStack() as gnn:
            sb = lambda n, s, d=FP32: gnn.enter_context(nc.sbuf_tensor(n, s, d))
            keep = Keep()
            keep.adjd = sb("adjd", [P, T, H, HA])
            keep.a = sb("a_all", [P, H, T])
            keep.c = sb("c_all", [P, H, T])
            keep.negv = sb("negv", [P, H, T])
            keep.hsum = sb("hsum", [P, H * HA])
            keep.xd = sb("xd", [P, H, T, 2 * HA], FP16)
            keep.stage = [yT[0][:, n, :].bitcast(BF16) for n in range(2)]
            keep.in_adj = [gnn.enter_context(nc.semaphore(f"in_adj{n}")) for n in range(2)]
            keep.ub = [yT[0][:, n, :].bitcast(FP32) for n in range(2)]
            project(nc, x, adj, w, wb, a, identity, scratch_u, scratch_x, keep)
            with ExitStack() as big:
                adjT = big.enter_context(nc.sbuf_tensor("adjT", [P, T, NP // 4], U32))
                keep.col32 = lambda t: adjT[:, :, bass.ds(t * (P // 4), P // 4)]
                keep.adj32 = lambda half, j: adjT[:, j, bass.ds(half * (HN // 4), HN // 4)]
                adjacency(nc, adj, identity, keep)
                attention(nc, scratch_u.rearrange("a h n -> (a h) n"), scratch_x, keep)
            with ExitStack() as both:
                weights = router_weights(nc, both, wq, bq, ln_g, ln_b, (keys0, keys1), down, identity, centre, own, k)
                residual(nc, both, x, identity, keep, scratch_x1, yT, weights)
        k.up = ctx.enter_context(nc.sbuf_tensor("upb", [P, EB, D], FP32))
        k.acts = ctx.enter_context(nc.sbuf_tensor("acts", [P, EB, G * P // QUAD, QUAD], FP32))
        experts(nc, yT, scratch_x1, merge, up, k, out)


def kernel(**inputs):
    import numpy as _np
    import concourse.bacc as _bacc
    from concourse import mybir as _mybir
    from concourse.bass_utils import run_bass_kernel_spmd as _run

    nc = _bacc.Bacc("TRN2", target_bir_lowering=False, num_devices=1)
    arrays, args = {}, []

    def give(name, array):
        array = _np.ascontiguousarray(array)
        arrays[name] = array
        args.append(nc.dram_tensor(name, array.shape, _mybir.dt.from_np(array.dtype), kind="ExternalInput").ap())
    for name in ("x", "adj", "L0_gnn_W_w", "L0_gnn_W_b", "L0_gnn_a", "L0_ffn_Wq", "L0_ffn_bq", "L0_ffn_ln_g", "L0_ffn_ln_b",
                 "L0_ffn_keys0", "L0_ffn_keys1", "L0_ffn_expert_down", "L0_ffn_expert_up"):
        give(f"in_{name}", inputs[name])
    give("in_identity", _np.eye(P, dtype=_np.float32))
    give("in_centre", _np.eye(P, dtype=_np.float32) - _np.float32(1.0 / P))
    give("in_own", _np.tile(_np.eye(QUAD, dtype=_np.float32) / _np.float32(RSCALE), (EA, 1)))
    merge = _np.zeros((2 * PAIRS, 2, KR), _np.float32)
    for c, s in enumerate(slots()):
        for head in range(2):
            for n in range(2):
                merge[head * PAIRS + c, n, (2 * n + head) * SLOTS + s] = 1.0
    give("in_merge", merge)
    args.append(nc.dram_tensor("out_0", (N, D), _mybir.dt.float32, kind="ExternalOutput").ap())
    program(nc, *args)
    r = _run(nc, [arrays], core_ids=[0])
    return r.results[0]["out_0"]
```
